# Optimizing a Trainium2 kernel written in Bass

```python
import numpy as np
import jax
import jax.numpy as jnp

def _softmax(x, axis=-1):
    return jax.nn.softmax(x, axis=axis)

def _gelu(x):
    return jax.nn.gelu(x, approximate=True)

def _silu(x):
    return jax.nn.silu(x)

def _sigmoid(x):
    return jax.nn.sigmoid(x)

def _layernorm(x, axis=-1, eps=1e-05):
    m = jnp.mean(x, axis=axis, keepdims=True)
    v = jnp.var(x, axis=axis, keepdims=True)
    return (x - m) / jnp.sqrt(v + eps)

def _scatter_add(tgt, idx, src, axis=0):
    return tgt.at[idx].add(src)

def _segment_sum(src, seg, n):
    return jax.ops.segment_sum(src, seg, n)
kernel_name = 'mk_decoder_preln_d2_seqx_r8_e7a213'

def setup_inputs(seed: int=0):
    np.random.seed(seed)
    _w = jnp.asarray

    def _rec_inputs():
        import jax
        import jax.numpy as jnp
        _rk = jax.random.key(seed)
        x = 0.0002417 + 0.9998 * jax.random.normal(jax.random.fold_in(_rk, 1), (2, 512, 128), jnp.float32)
        _lenS = 512 - jax.random.randint(jax.random.fold_in(_rk, 7), (2,), 0, max(1, 512 // 4) + 1, jnp.int32)
        _lenS2 = 77 - jax.random.randint(jax.random.fold_in(_rk, 8), (2,), 0, max(1, 77 // 4) + 1, jnp.int32)
        _ctx_1024P = jax.random.normal(jax.random.fold_in(_rk, 11), (2, 16, 128), jnp.float32)
        _ctx_1024c = jax.random.dirichlet(jax.random.fold_in(_rk, 511), 0.3 * jnp.ones((16,), jnp.float32), (2, 77))
        _ctx_1024t = jnp.einsum('bsk,bkd->bsd', _ctx_1024c, _ctx_1024P)
        _ctx_1024t = _ctx_1024t * jax.lax.rsqrt(jnp.mean(jnp.square(_ctx_1024t)) + 1e-12) * 0.953939
        ctx_1024 = 7.22013e-05 + 1.00017 * (_ctx_1024t + 0.3 * jax.random.normal(jax.random.fold_in(_rk, 611), (2, 77, 128), jnp.float32))
        _validS = jnp.arange(512)[None, :] < _lenS[:, None]
        _validS2 = jnp.arange(77)[None, :] < _lenS2[:, None]
        _causal = jnp.tril(jnp.ones((512, 512), dtype=bool))
        mask_BxSxS2_bk1 = jnp.broadcast_to(_validS2[:, None, :], (2, 512, 77))
        mask_Bx1x1xS2_if1 = jnp.where(jnp.ones((2, 1, 1, 77), dtype=bool), 1, 0).astype(jnp.int32)
        return (x, ctx_1024, mask_BxSxS2_bk1, mask_Bx1x1xS2_if1)
    x, ctx_1024, mask_BxSxS2_bk1, mask_Bx1x1xS2_if1 = _rec_inputs()

    def _L0_attn_setup():
        import jax, jax.numpy as jnp
        import numpy as np
        B, N, E, D = (2, 512, 128, 128)
        H = E // D
        LN_EPS = 1e-05

        def _gla_scan(q, k, v, g):

            def step(S, inp):
                qt, kt, vt, gt = inp
                S = jnp.exp(gt)[..., None] * S + kt[..., None] * vt[..., None, :]
                ot = jnp.einsum('bhd,bhde->bhe', qt, S)
                return (S, ot)
            xs = tuple((jnp.moveaxis(a, 2, 0) for a in (q, k, v, g)))
            S0 = jnp.zeros(q.shape[:2] + (q.shape[-1], v.shape[-1]), q.dtype)
            _, o = jax.lax.scan(step, S0, xs)
            return jnp.moveaxis(o, 0, 2)
        key = jax.random.key(seed)
        ks = jax.random.split(key, 6)
        s = 0.02
        return {'x': jax.random.normal(ks[0], (B, N, E), jnp.float32), 'W_in': jax.random.normal(ks[1], (3 * E, E), jnp.float32) * s, 'W_out': jax.random.normal(ks[2], (E, E), jnp.float32) * s, 'W_g1': jax.random.normal(ks[3], (D, E), jnp.float32) * s, 'W_g2': jax.random.normal(ks[4], (E, D), jnp.float32) * s, 'ln_w': jnp.ones((E,), jnp.float32)}
    _L0_attn_all = _L0_attn_setup()
    _L0_attn_in = {k: v for k, v in _L0_attn_all.items() if k in ('W_in', 'W_out', 'W_g1', 'W_g2', 'ln_w')}
    del _L0_attn_all

    def _L0_xattn_setup():
        import jax, jax.numpy as jnp
        import numpy as np
        HEAD_NUM = 16
        HIDDEN = 128
        HEAD_SIZE = HIDDEN // HEAD_NUM
        B, S = (4, 256)

        def _shape(x, b):
            return x.reshape(b, -1, HEAD_NUM, HEAD_SIZE).transpose(0, 2, 1, 3)
        key = jax.random.key(seed)
        ks = jax.random.split(key, 12)
        sc = 1.0 / np.sqrt(HIDDEN)
        inp = {'key': jax.random.normal(ks[0], (B, S, HIDDEN), jnp.float32), 'value': jax.random.normal(ks[1], (B, S, HIDDEN), jnp.float32), 'query': jax.random.normal(ks[2], (B, S, HIDDEN), jnp.float32), 'mask': jax.random.randint(ks[3], (B, S, S), 0, 2) > 0, 'Wq': jax.random.normal(ks[4], (HIDDEN, HIDDEN), jnp.float32) * sc, 'bq': jnp.zeros((HIDDEN,), jnp.float32), 'Wk': jax.random.normal(ks[5], (HIDDEN, HIDDEN), jnp.float32) * sc, 'bk': jnp.zeros((HIDDEN,), jnp.float32), 'Wv': jax.random.normal(ks[6], (HIDDEN, HIDDEN), jnp.float32) * sc, 'bv': jnp.zeros((HIDDEN,), jnp.float32), 'Wo': jax.random.normal(ks[7], (HIDDEN, HIDDEN), jnp.float32) * sc, 'bo': jnp.zeros((HIDDEN,), jnp.float32)}
        return inp
    _L0_xattn_all = _L0_xattn_setup()
    _L0_xattn_in = {k: v for k, v in _L0_xattn_all.items() if k in ('Wq', 'bq', 'Wk', 'bk', 'Wv', 'bv', 'Wo', 'bo')}
    del _L0_xattn_all

    def _L0_ffn_setup():
        import jax, jax.numpy as jnp
        import numpy as np
        B, S, H, I, E, TOP_K = (1, 256, 128, 256, 8, 2)
        key = jax.random.key(seed)
        ks = jax.random.split(key, 6)
        x = jax.random.normal(ks[0], (B, S, H), dtype=jnp.float32)
        Wr = jax.random.normal(ks[1], (H, E), dtype=jnp.float32) * (1.0 / np.sqrt(H))
        br = jnp.zeros((E,), dtype=jnp.float32)
        W1 = jax.random.normal(ks[2], (E, H, I), dtype=jnp.float32) * (1.0 / np.sqrt(H))
        W3 = jax.random.normal(ks[3], (E, H, I), dtype=jnp.float32) * (1.0 / np.sqrt(H))
        W2 = jax.random.normal(ks[4], (E, I, H), dtype=jnp.float32) * (1.0 / np.sqrt(I))
        return {'x': x, 'Wr': Wr, 'br': br, 'W1': W1, 'W3': W3, 'W2': W2}
    _L0_ffn_all = _L0_ffn_setup()
    _L0_ffn_in = {k: v for k, v in _L0_ffn_all.items() if k in ('Wr', 'br', 'W1', 'W3', 'W2')}
    del _L0_ffn_all

    def _L1_attn_setup():
        import jax, jax.numpy as jnp
        import numpy as np
        B, T, IN_DIM, EMB = (8, 256, 128, 128)
        NEG_INF = -1e+30
        key = jax.random.key(seed)
        ks = jax.random.split(key, 7)
        s = 1.0 / np.sqrt(IN_DIM)
        return {'x': jax.random.normal(ks[0], (B, T, IN_DIM), dtype=jnp.float32), 'Wq': jax.random.normal(ks[1], (IN_DIM, EMB), dtype=jnp.float32) * s, 'bq': jax.random.normal(ks[2], (EMB,), dtype=jnp.float32) * 0.01, 'Wk': jax.random.normal(ks[3], (IN_DIM, EMB), dtype=jnp.float32) * s, 'bk': jax.random.normal(ks[4], (EMB,), dtype=jnp.float32) * 0.01, 'Wv': jax.random.normal(ks[5], (IN_DIM, EMB), dtype=jnp.float32) * s, 'bv': jax.random.normal(ks[6], (EMB,), dtype=jnp.float32) * 0.01}
    _L1_attn_all = _L1_attn_setup()
    _L1_attn_in = {k: v for k, v in _L1_attn_all.items() if k in ('Wq', 'bq', 'Wk', 'bk', 'Wv', 'bv')}
    del _L1_attn_all

    def _L1_xattn_setup():
        import jax, jax.numpy as jnp
        import numpy as np
        N_HEADS = 16
        D_MODEL = 128
        D_K = D_MODEL // N_HEADS
        B, S = (2, 256)
        key = jax.random.key(seed)
        ks = jax.random.split(key, 12)
        sc = 1.0 / np.sqrt(D_MODEL)
        inp = {'query': jax.random.normal(ks[0], (B, S, D_MODEL), jnp.float32), 'key': jax.random.normal(ks[1], (B, S, D_MODEL), jnp.float32), 'value': jax.random.normal(ks[2], (B, S, D_MODEL), jnp.float32), 'mask': jnp.ones((B, 1, 1, S), jnp.int32), 'Wq': jax.random.normal(ks[3], (D_MODEL, D_MODEL), jnp.float32) * sc, 'bq': jnp.zeros((D_MODEL,), jnp.float32), 'Wk': jax.random.normal(ks[4], (D_MODEL, D_MODEL), jnp.float32) * sc, 'bk': jnp.zeros((D_MODEL,), jnp.float32), 'Wv': jax.random.normal(ks[5], (D_MODEL, D_MODEL), jnp.float32) * sc, 'bv': jnp.zeros((D_MODEL,), jnp.float32), 'Wo': jax.random.normal(ks[6], (D_MODEL, D_MODEL), jnp.float32) * sc, 'bo': jnp.zeros((D_MODEL,), jnp.float32)}
        return inp
    _L1_xattn_all = _L1_xattn_setup()
    _L1_xattn_in = {k: v for k, v in _L1_xattn_all.items() if k in ('Wq', 'bq', 'Wk', 'bk', 'Wv', 'bv', 'Wo', 'bo')}
    del _L1_xattn_all

    def _L1_ffn_setup():
        import jax, jax.numpy as jnp
        import numpy as np
        K = 2
        CAP_FACTOR = 1.25
        key = jax.random.key(seed)
        ks = jax.random.split(key, 6)
        B, T, C, H, E = (8, 256, 128, 512, 8)
        return {'x': jax.random.normal(ks[0], (B, T, C), dtype=jnp.float32), 'Wr': jax.random.normal(ks[1], (C, E), dtype=jnp.float32) * 0.02, 'W1': jax.random.normal(ks[2], (E, C, H), dtype=jnp.float32) * 0.02, 'b1': jax.random.normal(ks[3], (E, H), dtype=jnp.float32) * 0.02, 'W2': jax.random.normal(ks[4], (E, H, C), dtype=jnp.float32) * 0.02, 'b2': jax.random.normal(ks[5], (E, C), dtype=jnp.float32) * 0.02}
    _L1_ffn_all = _L1_ffn_setup()
    _L1_ffn_in = {k: v for k, v in _L1_ffn_all.items() if k in ('Wr', 'W1', 'b1', 'W2', 'b2')}
    del _L1_ffn_all
    return {'x': x, 'ctx_1024': ctx_1024, 'mask_BxSxS2_bk1': mask_BxSxS2_bk1, 'mask_Bx1x1xS2_if1': mask_Bx1x1xS2_if1, 'L0_attn_W_in': _L0_attn_in['W_in'], 'L0_attn_W_out': _L0_attn_in['W_out'], 'L0_attn_W_g1': _L0_attn_in['W_g1'], 'L0_attn_W_g2': _L0_attn_in['W_g2'], 'L0_attn_ln_w': _L0_attn_in['ln_w'], 'L0_xattn_Wq': _L0_xattn_in['Wq'], 'L0_xattn_bq': _L0_xattn_in['bq'], 'L0_xattn_Wk': _L0_xattn_in['Wk'], 'L0_xattn_bk': _L0_xattn_in['bk'], 'L0_xattn_Wv': _L0_xattn_in['Wv'], 'L0_xattn_bv': _L0_xattn_in['bv'], 'L0_xattn_Wo': _L0_xattn_in['Wo'], 'L0_xattn_bo': _L0_xattn_in['bo'], 'L0_ffn_Wr': _L0_ffn_in['Wr'], 'L0_ffn_br': _L0_ffn_in['br'], 'L0_ffn_W1': _L0_ffn_in['W1'], 'L0_ffn_W3': _L0_ffn_in['W3'], 'L0_ffn_W2': _L0_ffn_in['W2'], 'L1_attn_Wq': _L1_attn_in['Wq'], 'L1_attn_bq': _L1_attn_in['bq'], 'L1_attn_Wk': _L1_attn_in['Wk'], 'L1_attn_bk': _L1_attn_in['bk'], 'L1_attn_Wv': _L1_attn_in['Wv'], 'L1_attn_bv': _L1_attn_in['bv'], 'L1_xattn_Wq': _L1_xattn_in['Wq'], 'L1_xattn_bq': _L1_xattn_in['bq'], 'L1_xattn_Wk': _L1_xattn_in['Wk'], 'L1_xattn_bk': _L1_xattn_in['bk'], 'L1_xattn_Wv': _L1_xattn_in['Wv'], 'L1_xattn_bv': _L1_xattn_in['bv'], 'L1_xattn_Wo': _L1_xattn_in['Wo'], 'L1_xattn_bo': _L1_xattn_in['bo'], 'L1_ffn_Wr': _L1_ffn_in['Wr'], 'L1_ffn_W1': _L1_ffn_in['W1'], 'L1_ffn_b1': _L1_ffn_in['b1'], 'L1_ffn_W2': _L1_ffn_in['W2'], 'L1_ffn_b2': _L1_ffn_in['b2']}

def reference(x, ctx_1024, mask_BxSxS2_bk1, mask_Bx1x1xS2_if1, L0_attn_W_in, L0_attn_W_out, L0_attn_W_g1, L0_attn_W_g2, L0_attn_ln_w, L0_xattn_Wq, L0_xattn_bq, L0_xattn_Wk, L0_xattn_bk, L0_xattn_Wv, L0_xattn_bv, L0_xattn_Wo, L0_xattn_bo, L0_ffn_Wr, L0_ffn_br, L0_ffn_W1, L0_ffn_W3, L0_ffn_W2, L1_attn_Wq, L1_attn_bq, L1_attn_Wk, L1_attn_bk, L1_attn_Wv, L1_attn_bv, L1_xattn_Wq, L1_xattn_bq, L1_xattn_Wk, L1_xattn_bk, L1_xattn_Wv, L1_xattn_bv, L1_xattn_Wo, L1_xattn_bo, L1_ffn_Wr, L1_ffn_W1, L1_ffn_b1, L1_ffn_W2, L1_ffn_b2):
    import jax
    import jax.numpy as jnp

    def _L0_attn_ref(x, W_in, W_out, W_g1, W_g2, ln_w):
        import jax, jax.numpy as jnp
        import numpy as np
        B, N, E, D = (2, 512, 128, 128)
        H = E // D
        LN_EPS = 1e-05

        def _gla_scan(q, k, v, g):

            def step(S, inp):
                qt, kt, vt, gt = inp
                S = jnp.exp(gt)[..., None] * S + kt[..., None] * vt[..., None, :]
                ot = jnp.einsum('bhd,bhde->bhe', qt, S)
                return (S, ot)
            xs = tuple((jnp.moveaxis(a, 2, 0) for a in (q, k, v, g)))
            S0 = jnp.zeros(q.shape[:2] + (q.shape[-1], v.shape[-1]), q.dtype)
            _, o = jax.lax.scan(step, S0, xs)
            return jnp.moveaxis(o, 0, 2)
        b, n, e = x.shape
        u = x @ W_in.T
        v, q, lg = jnp.split(u, 3, axis=-1)
        q = jax.nn.silu(q)
        f = jax.nn.sigmoid(lg)
        k = 1.0 - f
        g = jax.nn.log_sigmoid(lg)

        def tohead(a):
            return a.reshape(b, n, H, D).transpose(0, 2, 1, 3)
        o = _gla_scan(tohead(q), tohead(k), tohead(v), tohead(g))
        o = o.transpose(0, 2, 1, 3).reshape(b, n, e)
        gate = jax.nn.sigmoid(x @ W_g1.T @ W_g2.T)
        o = o * gate
        mu = jnp.mean(o, axis=-1, keepdims=True)
        var = jnp.var(o, axis=-1, keepdims=True)
        o = (o - mu) * jax.lax.rsqrt(var + LN_EPS) * ln_w
        return o @ W_out.T

    def _L0_xattn_ref(key, value, query, mask, Wq, bq, Wk, bk, Wv, bv, Wo, bo):
        import jax, jax.numpy as jnp
        import numpy as np
        HEAD_NUM = 16
        HIDDEN = 128
        HEAD_SIZE = HIDDEN // HEAD_NUM
        B, S = (4, 256)

        def _shape(x, b):
            return x.reshape(b, -1, HEAD_NUM, HEAD_SIZE).transpose(0, 2, 1, 3)
        b = key.shape[0]
        q = _shape(query @ Wq + bq, b) / jnp.asarray(HEAD_SIZE, query.dtype) ** 0.5
        k = _shape(key @ Wk + bk, b)
        v = _shape(value @ Wv + bv, b)
        scores = jnp.einsum('bhqd,bhkd->bhqk', q, k).astype(jnp.float32)
        scores = jnp.where(mask[:, None, :, :], jnp.float32(-1e+18), scores)
        attn = jax.nn.softmax(scores, axis=-1).astype(q.dtype)
        ctx = jnp.einsum('bhqk,bhkd->bhqd', attn, v)
        ctx = ctx.transpose(0, 2, 1, 3).reshape(b, -1, HEAD_NUM * HEAD_SIZE)
        return ctx @ Wo + bo

    def _L0_ffn_ref(x, Wr, br, W1, W3, W2):
        import jax, jax.numpy as jnp
        import numpy as np
        B, S, H, I, E, TOP_K = (1, 256, 128, 256, 8, 2)
        logits = jnp.einsum('bsh,he->bse', x, Wr) + br
        routing_weights, expert_indices = jax.lax.top_k(logits, TOP_K)
        routing_weights = jax.nn.softmax(routing_weights, axis=-1)
        c = jnp.sum(jax.nn.one_hot(expert_indices, E, dtype=x.dtype) * routing_weights[..., None], axis=-2)
        gate = jnp.einsum('bsh,ehi->besi', x, W1)
        up = jnp.einsum('bsh,ehi->besi', x, W3)
        h = jax.nn.silu(gate) * up
        y = jnp.einsum('besi,eih->besh', h, W2)
        out = jnp.einsum('bse,besh->bsh', c, y)
        return out

    def _L1_attn_ref(x, Wq, bq, Wk, bk, Wv, bv):
        import jax, jax.numpy as jnp
        import numpy as np
        B, T, IN_DIM, EMB = (8, 256, 128, 128)
        NEG_INF = -1e+30
        q = x @ Wq + bq
        k = x @ Wk + bk
        v = x @ Wv + bv
        scale = jnp.asarray(EMB, x.dtype) ** 0.5
        scores = jnp.einsum('btd,bsd->bts', q, k) / scale
        Tq = scores.shape[-2]
        causal = jnp.tril(jnp.ones((Tq, Tq), dtype=bool))
        scores = jnp.where(causal, scores, jnp.asarray(NEG_INF, scores.dtype))
        m = jnp.max(scores, axis=(-2, -1), keepdims=True)
        e = jnp.exp(scores - m)
        w = e / jnp.sum(e, axis=(-2, -1), keepdims=True)
        return jnp.einsum('bts,bsd->btd', w, v)

    def _L1_xattn_ref(query, key, value, mask, Wq, bq, Wk, bk, Wv, bv, Wo, bo):
        import jax, jax.numpy as jnp
        import numpy as np
        N_HEADS = 16
        D_MODEL = 128
        D_K = D_MODEL // N_HEADS
        B, S = (2, 256)
        q = query @ Wq.T + bq
        k = key @ Wk.T + bk
        v = value @ Wv.T + bv

        def split_heads(x):
            b, s, _ = x.shape
            return x.reshape(b, s, N_HEADS, D_K).transpose(0, 2, 1, 3)
        q, k, v = (split_heads(q), split_heads(k), split_heads(v))
        att = jnp.einsum('bhqd,bhkd->bhqk', q, k) / jnp.sqrt(jnp.float32(D_K))
        att = jnp.where(mask == 0, -jnp.inf, att)
        scores = jax.nn.softmax(att, axis=-1)
        out = jnp.einsum('bhqk,bhkd->bhqd', scores, v)
        b = out.shape[0]
        out = out.transpose(0, 2, 1, 3).reshape(b, -1, N_HEADS * D_K)
        return out @ Wo.T + bo

    def _L1_ffn_ref(x, Wr, W1, b1, W2, b2):
        import jax, jax.numpy as jnp
        import numpy as np
        K = 2
        CAP_FACTOR = 1.25
        B, T, C = x.shape
        E = Wr.shape[1]
        capacity = int(T / E * CAP_FACTOR)
        probs = jax.nn.softmax(x @ Wr, axis=-1)
        topk_probs, topk_experts = jax.lax.top_k(probs, K)
        S = T * K
        e_flat = topk_experts.reshape(B, S)
        p_flat = topk_probs.reshape(B, S)
        x_rep = jnp.repeat(x, K, axis=1)
        onehot = jax.nn.one_hot(e_flat, E, dtype=jnp.int32)
        pos_all = jnp.cumsum(onehot, axis=1) - onehot
        pos = jnp.take_along_axis(pos_all, e_flat[..., None], axis=-1)[..., 0]
        keep = pos < capacity
        pos_c = jnp.minimum(pos, capacity - 1)
        b_idx = jnp.broadcast_to(jnp.arange(B)[:, None], (B, S))
        buf = jnp.zeros((E, B, capacity, C), dtype=x.dtype)
        buf = buf.at[e_flat, b_idx, pos_c].add(x_rep * keep[..., None].astype(x.dtype))
        h = jax.nn.relu(jnp.einsum('ebnc,ech->ebnh', buf, W1) + b1[:, None, None, :])
        y = jnp.einsum('ebnh,ehc->ebnc', h, W2) + b2[:, None, None, :]
        y_tok = y[e_flat, b_idx, pos_c]
        y_tok = y_tok * keep[..., None].astype(x.dtype) * p_flat[..., None]
        out = y_tok.reshape(B, T, K, C).sum(axis=2)
        return out
    x = x + _L0_attn_ref(_layernorm(x, axis=-1), L0_attn_W_in, L0_attn_W_out, L0_attn_W_g1, L0_attn_W_g2, L0_attn_ln_w)
    x = x + _L0_xattn_ref(ctx_1024, ctx_1024, _layernorm(x, axis=-1), mask_BxSxS2_bk1, L0_xattn_Wq, L0_xattn_bq, L0_xattn_Wk, L0_xattn_bk, L0_xattn_Wv, L0_xattn_bv, L0_xattn_Wo, L0_xattn_bo)
    x = x + _L0_ffn_ref(_layernorm(x, axis=-1), L0_ffn_Wr, L0_ffn_br, L0_ffn_W1, L0_ffn_W3, L0_ffn_W2)
    x = x + _L1_attn_ref(_layernorm(x, axis=-1), L1_attn_Wq, L1_attn_bq, L1_attn_Wk, L1_attn_bk, L1_attn_Wv, L1_attn_bv)
    x = x + _L1_xattn_ref(_layernorm(x, axis=-1), ctx_1024, ctx_1024, mask_Bx1x1xS2_if1, L1_xattn_Wq, L1_xattn_bq, L1_xattn_Wk, L1_xattn_bk, L1_xattn_Wv, L1_xattn_bv, L1_xattn_Wo, L1_xattn_bo)
    x = x + _L1_ffn_ref(_layernorm(x, axis=-1), L1_ffn_Wr, L1_ffn_W1, L1_ffn_b1, L1_ffn_W2, L1_ffn_b2)
    return x

_drawn_inputs = setup_inputs


def setup_inputs(seed=0):
    import zlib

    import numpy as np

    out = dict(_drawn_inputs(seed))
    spreads = {'L0_attn_ln_w': (1.0, 0.2),
     'L0_xattn_bq': (0.0, 0.1),
     'L0_xattn_bk': (0.0, 2.0),
     'L0_xattn_bv': (0.0, 0.1),
     'L0_xattn_bo': (0.0, 0.1),
     'L0_ffn_br': (0.0, 0.1),
     'L1_xattn_bq': (0.0, 0.464),
     'L1_xattn_bk': (0.0, 2.0),
     'L1_xattn_bv': (0.0, 0.1),
     'L1_xattn_bo': (0.0, 0.1)}
    factors = {'L1_attn_Wq': 8.0,
     'L1_attn_bq': 200.0,
     'L1_attn_Wk': 8.0,
     'L1_attn_bk': 64.0,
     'L1_attn_Wv': 8.0,
     'L1_attn_bv': 64.0,
     'L1_ffn_Wr': 7.489,
     'L1_ffn_W1': 8.0,
     'L1_ffn_b1': 8.0,
     'L1_ffn_W2': 7.13,
     'L1_ffn_b2': 8.0}
    for name, (base, spread) in spreads.items():
        noise = np.random.default_rng([zlib.crc32(name.encode()), seed]).standard_normal(out[name].shape)
        drawn = base * np.exp(spread * noise) if base else spread * noise
        out[name] = jnp.asarray(drawn.astype(out[name].dtype))
    for name, factor in factors.items():
        out[name] = (out[name] * factor).astype(out[name].dtype)
    return out
```

```python
from collections import namedtuple
from contextlib import ExitStack

import numpy as np

import concourse.bass as bass
from concourse import mybir

ALU = mybir.AluOpType
ACT = mybir.ActivationFunctionType
AX = mybir.AxisListType
F32 = mybir.dt.float32
BF16 = mybir.dt.bfloat16
U32 = mybir.dt.uint32
I32 = mybir.dt.int32
U8 = mybir.dt.uint8

B, S, D = 2, 512, 128
P = 128
TPB = S // P
NT = B * TPB
KEYS, H, HD = 77, 16, 8
HK = H * KEYS
NCH = -(-HK // P)
LASTR = HK - (NCH - 1) * P
NHC = 3
E0, I0 = 8, 256
C0 = I0 // P
E1, I1 = 8, 512
C1 = I1 // P
CAP = int(S / E1 * 1.25)
LEVELS = 8
EPS = 1e-5
BIG = 1024.0
HEADS_OF_BANK = (6, 6, 4)
HEAD_BASE = (0, 6, 12)
HLO = [min(P * c // KEYS, H - NHC) for c in range(NCH)]
XSCALE = float(HD) ** -0.5
ASCALE = float(D) ** -0.5


def columns(*parts):
    at, out = 0, {}
    for name, n in parts:
        out[name] = (at, n)
        at += n
    return out, at


EARLY, EARLY_N = columns(("win", 3 * D), ("wg1", D), ("wg2", D), ("wout", D), ("lnw", 1), ("ident", P))
GLA_MASK_N = LEVELS * P
WORK, WORK_N = columns(
    ("wv0", D), ("wv1", D), ("wk0", D), ("wk1", D), ("ctx0", 3 * KEYS), ("ctx1", 3 * KEYS),
    ("wq0", D), ("wo0", D), ("wq1", D), ("wo1", D), ("aq", D), ("ak", D), ("av", D),
    ("wr0", E0), ("wr1", E1),
    ("bq0", 1), ("bk0", 1), ("bv0", 1), ("bq1", 1), ("bk1", 1), ("bv1", 1), ("abq", 1), ("abk", 1),
    ("b1", E1 * C1),
    ("bo0", D), ("bo1", D), ("abv", D), ("br0", E0), ("b2", E1 * D),
    ("headmask", H), ("rowmask", NCH * NHC), ("slots", CAP), ("experts", E0),
)
HALF, HALF_N = columns(("ident", P), ("below", P), ("ones", P), ("future", P), ("maskout", HK))


def program(nc, x, early, glamask, work, half, padmask, keymask, keyrows, ffn0, ffn1, out):
    ctx = ExitStack()
    with ctx:
        def sb(name, shape, dt=F32):
            return ctx.enter_context(nc.sbuf_tensor(name, shape, dt))

        X = sb("X", [P, NT, D])
        N = sb("N", [P, NT, D])
        nT = sb("nT", [P, NT * P])
        early_sb = sb("early_sb", [P, EARLY_N])
        work_sb = sb("work_sb", [P, WORK_N])
        half_sb = sb("half_sb", [P, HALF_N], mybir.dt.uint16)
        ffn1_sb = sb("ffn1_sb", [P, E1, 2, I1])
        stats = sb("stats", [P, TPB, 6])
        moments = sb("moments", [P, TPB, 2])
        logvar = sb("logvar", [P, TPB])
        rstd = sb("rstd", [P, TPB])
        tiny = sb("tiny", [P, 1])

        def wk(name, lo=0, n=None):
            at, size = WORK[name]
            return work_sb[:, at + lo:at + (size if n is None else lo + n)]

        def ea(name, lo=0, n=None):
            at, size = EARLY[name]
            return early_sb[:, at + lo:at + (size if n is None else lo + n)]

        def hf(name, rows=P):
            at, size = HALF[name]
            return half_sb[0:rows, at:at + size].bitcast(BF16)

        region_a = sb("region_a", [P, 11 * NT * P + 3 * B * D])
        gla = [region_a[:, i * NT * P:(i + 1) * NT * P] for i in range(11)]
        decay, qp, ks, sig, A, v, gate, khat, g1T, og, glam = gla
        state = region_a[:, 11 * NT * P:].rearrange("p (b c e) -> p b c e", b=B, c=3)
        dpT = region_a[0:CAP, 0:B * E1 * S].rearrange("p (b e t) -> p b e t", b=B, e=E1)
        region_b = sb("region_b", [P, E0 * 3 * I0])
        ffn0_sb = region_b[:, :].rearrange("p (e m i) -> p e m i", e=E0, m=3)
        disp = region_b[:, 0:NT * E1 * CAP].rearrange("p (j e c) -> p j e c", j=NT, e=E1)
        region_c = sb("region_c", [P, 6 * HK])
        kblk = region_c[:, 0:4 * HK].rearrange("p (l b n) -> p l b n", l=2, b=B)
        probs = region_c[:, 4 * HK:].rearrange("p (i n) -> p i n", i=2)
        wdisp = region_c[:, 0:NT * E1 * CAP].rearrange("p (j e c) -> p j e c", j=NT, e=E1)

        totals = sb("totals", [P, 2 * NT * P])
        vblk = sb("vblk", [P, 2, B, NCH * NHC, HD + 1])
        rowm1 = sb("rowm1", [P, B, NCH * NHC])
        keep1 = sb("keep1", [P, B, NCH])
        keyrows_sb = sb("keyrows_sb", [P, B, NCH], I32)
        keymask_sb = sb("keymask_sb", [KEYS, B], I32)
        padmask_sb = sb("padmask_sb", [KEYS, NT * P // 4], U32)
        maskT0 = sb("maskT0", [KEYS, NT * P], BF16)
        maskT1 = sb("maskT1", [KEYS, B, P], BF16)
        keyoff = sb("keyoff", [KEYS, B])
        kT = sb("kT", [P, 2, B, KEYS])
        qT = sb("qT", [P, NT * P])
        ptT = sb("ptT", [P, NCH, P])
        rowmax = sb("rowmax", [P, H])
        rsum = sb("rsum", [P, H])
        heads = sb("heads", [P, H, HD])
        headsT = sb("headsT", [P, P])
        logits = sb("logits", [P, NT, E0])
        top = sb("top", [P, NT, 8])
        topi = sb("topi", [P, NT, 8], U32)
        topf = sb("topf", [P, NT, 2])
        two = sb("two", [P, 3, NT])
        sel = sb("sel", [P, 2, NT, E0])
        coef = sb("coef", [P, NT, E0])
        selh = sb("selh", [P, NT, E1], BF16)
        slot = sb("slot", [P, NT, E1])
        late = 8 * NT * P
        gact = region_a[:, late:late + 2 * S].rearrange("p (i t) -> p i t", i=2)
        hid = region_a[:, late + 2 * S:late + 2 * S + 2 * C0 * S].rearrange("p (i c t) -> p i c t", i=2, c=C0)
        akT = region_a[:, 0:NT * P]
        av_sb = region_a[:, NT * P:2 * NT * P].rearrange("p (j d) -> p j d", j=NT)
        expo = region_a[:, late:late + B * 3 * S].rearrange("p (b k t) -> p b k t", b=B, k=3)
        amax = sb("amax", [P, B, 4])
        gmax = sb("gmax", [P, B])
        nmax = sb("nmax", [P, B])
        asum = sb("asum", [P, B, 4])
        gsum = sb("gsum", [P, B])
        rtot = sb("rtot", [P, B])
        xd = sb("xd", [P, E1, B, CAP])
        h1 = sb("h1", [P, 2, C1, B * CAP])
        y1 = sb("y1", [CAP, 2, B, D])

        bank = [ctx.enter_context(nc.psum_tensor(f"bank{i}", [P, 512], F32)) for i in range(8)]

        names = """x_in early_in glam_in work_in half_in masks_in ffn0_in ffn1_in out_done
        stats moments logvar rstd normed turned nT
        p_lg p_q p_g1 p_v p_gate f_ready k_ready sigq q_ready g1_ready v_ready gate_ready
        A_zero level_mm level_kept qp_step ks_step tot_step khat_T khat_ready upd state_ready
        o_ready og_ready x_gla p_out
        kT_mm kT_ready vrep vb_ready kblk_ready setup keyoff rowm maskT
        q_mm qT_ready score score_free rmax probs_ready exp_ready pT pT_ready pv heads_r rsum_r hT hT_ready
        wo x_bias x_res
        r_mm logit top topi topf diff ediff one w1 w2 eq1 coef_p coef
        gu act hid down x_ffn act_free
        a_q a_k a_qk a_v av_ready a_score a_pmax a_max a_gmax a_nmax a_exp a_sum a_gsum a_rtot a_pv x_att
        b_shift b_exp b_sum b_rec b_prob selp selh pos slot disp wdisp xd xd_ready dpT dpT_ready
        h_mm h_ready y_mm y_ready comb final""".split()
        s = namedtuple("Signals", names)(*[ctx.enter_context(nc.semaphore(n)) for n in names])
        block = ctx.enter_context(nc.Block())

        tile = lambda t, j: t[:, j * P:(j + 1) * P]
        seq = lambda t, b: t[:, b * S:(b + 1) * S]
        ident = ea("ident")
        LN_X, LN_GLA, LN_X0, LN_F0, LN_ATT, LN_X1, LN_F1 = range(7)

        def total(level, b):
            if level == 0:
                return seq(decay, b)
            at = sum(NT * P >> i for i in range(1, level))
            n = S >> level
            return totals[:, at + b * n:at + (b + 1) * n]

        @block.sync
        def _(sp):
            for b in range(B):
                sp.dma_start(X[:, b * TPB:(b + 1) * TPB, :],
                             x[b].rearrange("(j p) d -> p j d", p=P)).then_inc(s.x_in, 16)
            sp.dma_start(early_sb[:, :], early).then_inc(s.early_in, 16)
            sp.dma_start(glam[:, 0:GLA_MASK_N], glamask).then_inc(s.glam_in, 16)
            sp.dma_start(work_sb[:, :], work).then_inc(s.work_in, 16)
            sp.dma_start(ffn0_sb[:, :, :, :], ffn0.rearrange("p (e m i) -> p e m i", e=E0, m=3)).then_inc(s.ffn0_in, 16)
            sp.dma_start(ffn1_sb[:, :, :, :], ffn1.rearrange("p (e m i) -> p e m i", e=E1, m=2)).then_inc(s.ffn1_in, 16)
            for b in range(B):
                sp.wait_ge(s.final, b + 1)
                sp.dma_start(out[b].rearrange("(j p) d -> p j d", p=P),
                             X[:, b * TPB:(b + 1) * TPB, :]).then_inc(s.out_done, 16)
            sp.wait_ge(s.out_done, 16 * B)

        @block.gpsimd
        def _(pool):
            pool.dma_start(half_sb[:, :], half).then_inc(s.half_in, 16)
            pool.dma_start(padmask_sb[:, :], padmask).then_inc(s.masks_in, 16)
            pool.dma_start(keymask_sb[:, :], keymask).then_inc(s.masks_in, 16)
            pool.dma_start(keyrows_sb[:, :, :], keyrows).then_inc(s.masks_in, 16)
            pool.memset(A, 0.0).then_inc(s.A_zero, 1)
            for lv in range(1, LEVELS):
                for b in range(B):
                    if lv == 1:
                        pool.wait_ge(s.f_ready, b + 1)
                        pool.wait_ge(s.k_ready, b + 1)
                    else:
                        pool.wait_ge(s.tot_step, B * (lv - 2) + b + 1)
                    t = total(lv - 1, b).rearrange("p (n two) -> p n two", two=2)
                    pool.tensor_tensor(total(lv, b), t[:, :, 0], t[:, :, 1], ALU.mult).then_inc(s.tot_step, 1)
                    pool.wait_ge(s.level_mm, B * lv + b + 1)
                    seg = 1 << (lv - 1)
                    kv = seq(ks, b).rearrange("p (n two g) -> p n two g", two=2, g=seg)[:, :, 0, :]
                    right = t[:, :, 1].rearrange("p (n one) -> p n one", one=1).broadcast_to([P, S // (2 * seg), seg])
                    pool.tensor_tensor(kv, kv, right, ALU.mult).then_inc(s.ks_step, 1)
            for l in range(2):
                for b in range(B):
                    pool.wait_ge(s.kT_ready, l + 1)
                    pool.wait_ge(s.work_in, 16)
                    pool.tensor_tensor(
                        kblk[:, l, b, :].rearrange("p (h k) -> p h k", h=H),
                        kT[:, l, b, :].rearrange("p (one k) -> p one k", one=1).broadcast_to([P, H, KEYS]),
                        wk("headmask").rearrange("p (h one) -> p h one", one=1).broadcast_to([P, H, KEYS]),
                        ALU.mult).then_inc(s.kblk_ready, 1)

            def add_bias(l):
                for b in range(B):
                    pool.wait_ge(s.normed, 2 * (LN_X0 if l == 0 else LN_X1) + b + 1)
                    xs = X[:, b * TPB:(b + 1) * TPB, :]
                    bo = wk("bo0" if l == 0 else "bo1").rearrange("p (one d) -> p one d", one=1).broadcast_to([P, TPB, D])
                    pool.tensor_tensor(xs, xs, bo, ALU.add).then_inc(s.x_bias, 1)

            add_bias(0)
            for b in range(B):
                pool.wait_ge(s.a_max, b + 1)
                pool.partition_all_reduce(gmax[:, b:b + 1], amax[:, b, 3:4], P, bass.bass_isa.ReduceOp.max).then_inc(s.a_gmax, 1)
                pool.wait_ge(s.a_sum, b + 1)
                pool.partition_all_reduce(gsum[:, b:b + 1], asum[:, b, 3:4], P, bass.bass_isa.ReduceOp.add).then_inc(s.a_gsum, 1)
            add_bias(1)
            for j in range(NT):
                pool.wait_ge(s.disp, j + 1)
                pool.tensor_tensor(
                    wdisp[:, j, :, :], disp[:, j, :, :],
                    coef[:, j, :].rearrange("p (e one) -> p e one", one=1).broadcast_to([P, E1, CAP]),
                    ALU.mult).then_inc(s.wdisp, 1)

        @block.scalar
        def _(act):
            def ln(k, b):
                i = 2 * k + b
                act.wait_ge(s.moments, i + 1)
                if i:
                    act.wait_ge(s.normed, i)
                act.activation(logvar[:, :], moments[:, :, 1], ACT.Ln, bias=tiny[:, 0:1]).then_inc(s.logvar, 1)
                act.wait_ge(s.logvar, i + 1)
                act.activation(rstd[:, :], logvar[:, :], ACT.Exp, scale=-0.5).then_inc(s.rstd, 1)

            def ln_out(k, b, scale=1.0):
                act.wait_ge(s.turned, 2 * k + b + 1)
                act.activation(seq(nT, b), bank[7][:, :], ACT.Copy, scale=scale).then_inc(s.nT, 1)

            act.wait_ge(s.setup, 1)
            act.preload_act_table_set("natural_log_exp_and_others")
            for b in range(B):
                ln(LN_X, b)
                ln_out(LN_X, b)
            for b in range(B):
                act.wait_ge(s.p_lg, b + 1)
                act.activation(seq(decay, b), bank[1][:, :], ACT.Sigmoid).then_inc(s.f_ready, 1)
                act.activation(seq(ks, b), bank[1][:, :], ACT.Sigmoid, scale=-1.0).then_inc(s.k_ready, 1)
                act.wait_ge(s.p_q, b + 1)
                act.activation(seq(sig, b), bank[0][:, :], ACT.Sigmoid).then_inc(s.sigq, 1)
                act.wait_ge(s.p_g1, b + 1)
                act.copy(seq(g1T, b), bank[2][:, :]).then_inc(s.g1_ready, 1)
                act.wait_ge(s.p_v, b + 1)
                act.copy(seq(v, b), bank[3][:, :]).then_inc(s.v_ready, 1)
                act.wait_ge(s.p_gate, b + 1)
                act.activation(seq(gate, b), bank[4][:, :], ACT.Sigmoid).then_inc(s.gate_ready, 1)
            for l in range(2):
                act.wait_ge(s.kT_mm, l + 1)
                act.activation(kT[:, l, :, :], bank[2 + l][:, 0:B * KEYS].rearrange("p (b k) -> p b k", b=B),
                               ACT.Identity, bias=wk(f"bk{l}")).then_inc(s.kT_ready, 1)
            for b in range(B):
                act.wait_ge(s.khat_T, b + 1)
                act.copy(seq(khat, b)[:, 0:3 * P], bank[b][:, 0:3 * P]).then_inc(s.khat_ready, 1)
            act.preload_act_table_set("natural_log_exp_and_others")
            for b in range(B):
                ln(LN_GLA, b)
                ln_out(LN_GLA, b, scale=ea("lnw"))

            def cross(l):
                for b in range(B):
                    ln(LN_X0 if l == 0 else LN_X1, b)
                    ln_out(LN_X0 if l == 0 else LN_X1, b)
                    act.wait_ge(s.q_mm, 2 * l + b + 1)
                    act.activation(seq(qT, b), bank[6][:, :], ACT.Identity, bias=wk(f"bq{l}")).then_inc(s.qT_ready, 1)
                for i in range(NT + 2):
                    if 1 <= i <= NT:
                        g = l * NT + i - 1
                        if g:
                            act.wait_ge(s.pv, g)
                        for k in range(3):
                            act.wait_ge(s.pT, 3 * g + k + 1)
                            if k < 2:
                                act.copy(ptT[:, 4 * k:4 * k + 4, :].rearrange("p c q -> p (c q)"), bank[3 + k][:, :]).then_inc(s.pT_ready, 1)
                            else:
                                act.copy(ptT[:, 8, :], bank[5][:, 0:P])
                                act.copy(ptT[0:LASTR, 9, :], bank[5][0:LASTR, P:2 * P]).then_inc(s.pT_ready, 1)
                    if i >= 2:
                        g = l * NT + i - 2
                        act.wait_ge(s.hT, g + 1)
                        act.activation(headsT[:, :], bank[7][:, 0:P], ACT.Identity, bias=wk(f"bv{l}")).then_inc(s.hT_ready, 1)
                    if i < NT:
                        g = l * NT + i
                        act.wait_ge(s.probs_ready, g + 1)
                        act.activation(probs[:, g % 2, :], probs[:, g % 2, :], ACT.Exp, scale=XSCALE).then_inc(s.exp_ready, 1)

            cross(0)
            for b in range(B):
                ln(LN_F0, b)
                ln_out(LN_F0, b)
            act.wait_ge(s.diff, 1)
            act.activation(two[:, 1, :], two[:, 0, :], ACT.Exp).then_inc(s.ediff, 1)
            for u in range(E0 * B * C0):
                act.wait_ge(s.gu, u + 1)
                if u >= 2:
                    act.wait_ge(s.hid, u - 1)
                act.activation(gact[:, u % 2, :], bank[2 * (u % 2)][:, :], ACT.Silu).then_inc(s.act, 1)
            act.preload_act_table_set("natural_log_exp_and_others")
            for b in range(B):
                ln(LN_ATT, b)
                ln_out(LN_ATT, b)
                act.wait_ge(s.a_qk, 2 * b + 1)
                act.activation(seq(qT, b), bank[0][:, :], ACT.Identity, bias=wk("abq")).then_inc(s.a_q, 1)
                act.wait_ge(s.a_qk, 2 * b + 2)
                act.activation(seq(akT, b), bank[1][:, :], ACT.Identity, bias=wk("abk")).then_inc(s.a_k, 1)
            for b in range(B):
                act.wait_ge(s.a_gmax, b + 1)
                act.mul(nmax[:, b:b + 1], gmax[:, b:b + 1], -ASCALE).then_inc(s.a_nmax, 1)
                act.wait_ge(s.a_nmax, b + 1)
                for k, n in enumerate((S, S, 2 * P)):
                    act.activation(expo[:, b, k, 0:n], bank[3 + k][:, 0:n], ACT.Exp, bias=nmax[:, b:b + 1],
                                   scale=ASCALE, accum_out=asum[:, b, k:k + 1]).then_inc(s.a_exp, 1)
            cross(1)
            for b in range(B):
                ln(LN_F1, b)
                ln_out(LN_F1, b)
            act.wait_ge(s.b_shift, 1)
            act.activation(coef[:, :, :], coef[:, :, :], ACT.Exp).then_inc(s.b_exp, 1)
            for b in range(B):
                for hf_ in range(2):
                    act.wait_ge(s.xd, 2 * b + hf_ + 1)
                    act.copy(xd[:, 4 * hf_:4 * hf_ + 4, b, :],
                             bank[hf_][:, 0:4 * CAP].rearrange("p (e c) -> p e c", e=4)).then_inc(s.xd_ready, 1)
                for e in range(E1):
                    act.wait_ge(s.dpT, b * E1 + e + 1)
                    act.copy(dpT[:, b, e, :], bank[2 + e % 2][0:CAP, :]).then_inc(s.dpT_ready, 1)

        @block.vector
        def _(dve):
            def ln(k, b, src):
                i = 2 * k + b
                if i:
                    dve.wait_ge(s.normed, i)
                for j in range(TPB):
                    last = dve.bn_stats(stats[:, j, :], src[:, b * TPB + j, :])
                last.then_inc(s.stats, 1)
                dve.wait_ge(s.stats, i + 1)
                for j in range(TPB):
                    last = dve.bn_aggr(moments[:, j, :], stats[:, j, :])
                last.then_inc(s.moments, 1)
                dve.wait_ge(s.rstd, i + 1)
                if i >= 2:
                    dve.wait_ge(s.turned, i - 1)
                for j in range(TPB):
                    last = dve.tensor_scalar(N[:, b * TPB + j, :], src[:, b * TPB + j, :], moments[:, j, 0:1],
                                             rstd[:, j:j + 1], ALU.subtract, ALU.mult)
                last.then_inc(s.normed, 1)

            dve.memset(tiny[:, :], EPS).then_inc(s.setup, 1)
            for b in range(B):
                dve.wait_ge(s.x_in, 16 * B)
                ln(LN_X, b, X)
            for b in range(B):
                dve.wait_ge(s.sigq, b + 1)
                dve.tensor_tensor(seq(qp, b), bank[0][:, :], seq(sig, b), ALU.mult).then_inc(s.q_ready, 1)
            dve.wait_ge(s.glam_in, 16)
            dve.wait_ge(s.A_zero, 1)
            for lv in range(LEVELS):
                for b in range(B):
                    i = B * lv + b
                    if lv == 0:
                        pass
                    dve.wait_ge(s.level_mm, i + 1)
                    dve.copy_predicated(
                        seq(A, b).rearrange("p (j t) -> p j t", j=TPB),
                        tile(glam, lv).rearrange("p (one t) -> p one t", one=1).broadcast_to([P, TPB, P]).bitcast(U32),
                        bank[5 + b][:, :].rearrange("p (j t) -> p j t", j=TPB)).then_inc(s.level_kept, 1)
                    if lv == 0:
                        dve.wait_ge(s.f_ready, b + 1)
                        dve.tensor_tensor(seq(qp, b), seq(qp, b), seq(decay, b), ALU.mult).then_inc(s.qp_step, 1)
                    else:
                        seg = 1 << (lv - 1)
                        if lv >= 2:
                            dve.wait_ge(s.tot_step, B * (lv - 2) + b + 1)
                        dve.wait_ge(s.qp_step, i)
                        qv = seq(qp, b).rearrange("p (n two g) -> p n two g", two=2, g=seg)[:, :, 1, :]
                        left = total(lv - 1, b).rearrange("p (n two) -> p n two", two=2)[:, :, 0]
                        left = left.rearrange("p (n one) -> p n one", one=1).broadcast_to([P, S // (2 * seg), seg])
                        dve.tensor_tensor(qv, qv, left, ALU.mult).then_inc(s.qp_step, 1)
            dve.wait_ge(s.work_in, 16)
            dve.wait_ge(s.masks_in, 48)
            dve.tensor_scalar(keep1[:, :, :], keyrows_sb[:, :, :], 0.0, None, ALU.not_equal).then_inc(s.rowm, 1)
            dve.tensor_scalar(keyoff[:, :], keymask_sb[:, :], 0.0, None, ALU.is_equal).then_inc(s.keyoff, 1)
            dve.tensor_copy(maskT0[:, :], padmask_sb[:, :].bitcast(U8)).then_inc(s.maskT, 1)
            dve.wait_ge(s.rowm, 1)
            for b in range(B):
                dve.tensor_tensor(
                    rowm1[:, b, :].rearrange("p (c h) -> p c h", c=NCH),
                    wk("rowmask").rearrange("p (c h) -> p c h", c=NCH),
                    keep1[:, b, :].rearrange("p (c one) -> p c one", one=1).broadcast_to([P, NCH, NHC]),
                    ALU.mult).then_inc(s.rowm, 1)
            dve.wait_ge(s.keyoff, 1)
            for b in range(B):
                dve.tensor_copy(maskT1[:, b, :], keyoff[:, b:b + 1].broadcast_to([KEYS, P])).then_inc(s.maskT, 1)
            dve.wait_ge(s.rowm, 1 + B)
            for b in range(B):
                dve.wait_ge(s.vrep, b + 1)
                for l in range(2):
                    m = wk("rowmask") if l == 0 else rowm1[:, b, :]
                    m = m.rearrange("p (n one) -> p n one", one=1)
                    pv = bank[3 + b][:, 0:NCH * 2 * NHC * HD].rearrange("p (c l n) -> p c l n", c=NCH, l=2)[:, :, l, :]
                    dve.tensor_tensor(
                        vblk[:, l, b, :, 0:HD].rearrange("p (c h) f -> p c h f", c=NCH),
                        pv.rearrange("p c (h f) -> p c h f", h=NHC),
                        m.broadcast_to([P, NCH * NHC, HD]).rearrange("p (c h) f -> p c h f", c=NCH), ALU.mult)
                    dve.tensor_copy(vblk[:, l, b, :, HD:HD + 1], m).then_inc(s.vb_ready, 1)
            for c in range(3):
                for b in range(B):
                    dve.wait_ge(s.upd, 3 * (b + 1))
                    u = bank[2 if b == 0 else 0][:, c * P:(c + 1) * P]
                    if c == 0:
                        dve.tensor_copy(state[:, b, 0, :], u).then_inc(s.state_ready, 1)
                    else:
                        if b == 0:
                            dve.wait_ge(s.tot_step, B * (LEVELS - 1))
                        dve.wait_ge(s.state_ready, B * (c - 1) + b + 1)
                        dve.scalar_tensor_tensor(out=state[:, b, c, :], in0=state[:, b, c - 1, :],
                                                 scalar=total(LEVELS - 1, b)[:, c:c + 1], in1=u,
                                                 op0=ALU.mult, op1=ALU.add).then_inc(s.state_ready, 1)
            for b in range(B):
                dve.wait_ge(s.o_ready, b + 1)
                dve.wait_ge(s.gate_ready, b + 1)
                dve.tensor_tensor(seq(og, b), bank[5 + b][:, :], seq(gate, b), ALU.mult).then_inc(s.og_ready, 1)
                dve.wait_ge(s.og_ready, b + 1)
                ln(LN_GLA, b, og.rearrange("p (j d) -> p j d", j=NT))
            for b in range(B):
                dve.wait_ge(s.p_out, b + 1)
                xs = X[:, b * TPB:(b + 1) * TPB, :].rearrange("p j d -> p (j d)")
                dve.tensor_tensor(xs, xs, bank[b][:, :], ALU.add).then_inc(s.x_gla, 1)

            def cross(l):
                for b in range(B):
                    if l == 0:
                        dve.wait_ge(s.x_gla, b + 1)
                    else:
                        dve.wait_ge(s.x_att, b + 1)
                    ln(LN_X0 if l == 0 else LN_X1, b, X)
                for i in range(NT + 2):
                    if i < NT:
                        g = l * NT + i
                        if g >= 2:
                            dve.wait_ge(s.pT, 3 * (g - 1))
                        for k, (n, h0) in enumerate(zip(HEADS_OF_BANK, HEAD_BASE)):
                            dve.wait_ge(s.score, 3 * g + k + 1)
                            sc = bank[k][:, 0:n * KEYS].rearrange("p (h k) -> p h k", h=n)
                            dve.tensor_reduce(rowmax[:, h0:h0 + n], sc, AX.X, ALU.max).then_inc(s.rmax, 1)
                            dve.wait_ge(s.rmax, 3 * g + k + 1)
                            last = dve.tensor_tensor(
                                probs[:, g % 2, h0 * KEYS:(h0 + n) * KEYS].rearrange("p (h k) -> p h k", h=n), sc,
                                rowmax[:, h0:h0 + n].rearrange("p (h one) -> p h one", one=1).broadcast_to([P, n, KEYS]),
                                ALU.subtract)
                            last.then_inc(s.score_free, 1)
                        dve.wait_ge(s.score_free, 3 * g + 3)
                        dve.engine_nop().then_inc(s.probs_ready, 1) if False else dve.sem_inc(s.probs_ready, 1)
                    if 1 <= i <= NT:
                        g = l * NT + i - 1
                        dve.wait_ge(s.pv, g + 1)
                        pvv = bank[6][:, 0:H * (HD + 1)].rearrange("p (h f) -> p h f", h=H)
                        if g:
                            dve.wait_ge(s.heads_r, g)
                        dve.reciprocal(rsum[:, :], pvv[:, :, HD]).then_inc(s.rsum_r, 1)
                        dve.wait_ge(s.rsum_r, g + 1)
                        if g:
                            dve.wait_ge(s.hT, g)
                        dve.tensor_tensor(heads[:, :, :], pvv[:, :, 0:HD],
                                          rsum[:, :].rearrange("p (h one) -> p h one", one=1).broadcast_to([P, H, HD]),
                                          ALU.mult).then_inc(s.heads_r, 1)
                    if i >= 2:
                        g = l * NT + i - 2
                        dve.wait_ge(s.wo, g + 1)
                        dve.wait_ge(s.x_bias, B * l + (i - 2) // TPB + 1)
                        dve.tensor_tensor(X[:, i - 2, :], X[:, i - 2, :], bank[7][:, P:2 * P], ALU.add).then_inc(s.x_res, 1)

            cross(0)

            def top_two():
                pass

            for b in range(B):
                dve.wait_ge(s.x_res, (b + 1) * TPB)
                ln(LN_F0, b, X)
            dve.wait_ge(s.r_mm, 1)
            dve.tensor_tensor(logits[:, :, :], bank[6][:, 0:NT * E0].rearrange("p (j e) -> p j e", j=NT),
                              wk("br0").rearrange("p (one e) -> p one e", one=1).broadcast_to([P, NT, E0]),
                              ALU.add).then_inc(s.logit, 1)

            def ranks(n):
                dve.wait_ge(s.logit, n)
                for j in range(NT):
                    last = dve.max(top[:, j, :], logits[:, j, :])
                last.then_inc(s.top, 1)
                dve.wait_ge(s.top, n)
                for j in range(NT):
                    last = dve.max_index(topi[:, j, :], top[:, j, :], logits[:, j, :])
                last.then_inc(s.topi, 1)
                dve.wait_ge(s.topi, n)
                dve.tensor_copy(topf[:, :, :], topi[:, :, 0:2]).then_inc(s.topf, 1)
                dve.wait_ge(s.topf, n)
                ex = wk("experts").rearrange("p (one e) -> p one e", one=1).broadcast_to([P, NT, E0])
                for r in range(2):
                    last = dve.tensor_tensor(sel[:, r, :, :], ex, topf[:, :, r:r + 1].broadcast_to([P, NT, E0]), ALU.is_equal)
                last.then_inc(s.eq1, 1)

            ranks(1)
            dve.tensor_tensor(two[:, 0, :], top[:, :, 1], top[:, :, 0], ALU.subtract).then_inc(s.diff, 1)
            dve.wait_ge(s.ediff, 1)
            dve.tensor_scalar(two[:, 2, :], two[:, 1, :], 1.0, None, ALU.add).then_inc(s.one, 1)
            dve.wait_ge(s.one, 1)
            dve.reciprocal(two[:, 0, :], two[:, 2, :]).then_inc(s.w1, 1)
            dve.wait_ge(s.w1, 1)
            dve.tensor_tensor(two[:, 2, :], two[:, 0, :], two[:, 1, :], ALU.mult).then_inc(s.w2, 1)
            dve.wait_ge(s.w2, 1)
            dve.wait_ge(s.eq1, 1)
            for r, w in ((0, 0), (1, 2)):
                last = dve.tensor_tensor(sel[:, r, :, :], sel[:, r, :, :],
                                         two[:, w, :].rearrange("p (j one) -> p j one", one=1).broadcast_to([P, NT, E0]), ALU.mult)
            last.then_inc(s.coef_p, 1)
            dve.wait_ge(s.coef_p, 1)
            dve.tensor_tensor(coef[:, :, :], sel[:, 0, :, :], sel[:, 1, :, :], ALU.add).then_inc(s.coef, 1)
            dve.wait_ge(s.coef, 1)
            units = [(e, b) for e in range(E0) for b in range(B)]
            for i in range(len(units) + 1):
                if i < len(units):
                    for c in range(C0):
                        u = C0 * i + c
                        dve.wait_ge(s.act, u + 1)
                        if i >= 2:
                            dve.wait_ge(s.down, i - 1)
                        dve.tensor_tensor(hid[:, i % 2, c, :], bank[2 * (u % 2) + 1][:, :], gact[:, u % 2, :], ALU.mult).then_inc(s.hid, 1)
                if i >= 1:
                    e, b = units[i - 1]
                    dve.wait_ge(s.down, i)
                    if i - 1 >= B:
                        dve.wait_ge(s.x_ffn, i - B)
                    for j in range(TPB):
                        t = b * TPB + j
                        last = dve.scalar_tensor_tensor(out=X[:, t, :], in0=bank[4 + (i - 1) % 2][:, j * P:(j + 1) * P],
                                                        scalar=coef[:, t, e:e + 1], in1=X[:, t, :], op0=ALU.mult, op1=ALU.add)
                    last.then_inc(s.x_ffn, 1)
            for b in range(B):
                dve.wait_ge(s.x_ffn, len(units) - B + b + 1)
                ln(LN_ATT, b, X)
                dve.wait_ge(s.a_v, b + 1)
                dve.tensor_tensor(av_sb[:, b * TPB:(b + 1) * TPB, :], bank[2][:, :].rearrange("p (j d) -> p j d", j=TPB),
                                  wk("abv").rearrange("p (one d) -> p one d", one=1).broadcast_to([P, TPB, D]),
                                  ALU.add).then_inc(s.av_ready, 1)
            for b in range(B):
                for k, n in enumerate((S, S, 2 * P)):
                    dve.wait_ge(s.a_score, 3 * b + k + 1)
                    dve.tensor_reduce(amax[:, b, k:k + 1], bank[3 + k][:, 0:n], AX.X, ALU.max).then_inc(s.a_pmax, 1)
                dve.wait_ge(s.a_pmax, 3 * b + 3)
                dve.tensor_reduce(amax[:, b, 3:4], amax[:, b, 0:3], AX.X, ALU.max).then_inc(s.a_max, 1)
                dve.wait_ge(s.a_exp, 3 * b + 3)
                dve.tensor_reduce(asum[:, b, 3:4], asum[:, b, 0:3], AX.X, ALU.add).then_inc(s.a_sum, 1)
                dve.wait_ge(s.a_gsum, b + 1)
                dve.reciprocal(rtot[:, b:b + 1], gsum[:, b:b + 1]).then_inc(s.a_rtot, 1)
                dve.wait_ge(s.a_rtot, b + 1)
                dve.wait_ge(s.a_pv, b + 1)
                xs = X[:, b * TPB:(b + 1) * TPB, :].rearrange("p j d -> p (j d)")
                dve.scalar_tensor_tensor(out=xs, in0=bank[6][:, :], scalar=rtot[:, b:b + 1], in1=xs,
                                         op0=ALU.mult, op1=ALU.add).then_inc(s.x_att, 1)
            cross(1)
            for b in range(B):
                dve.wait_ge(s.x_res, NT + (b + 1) * TPB)
                ln(LN_F1, b, X)
            dve.wait_ge(s.r_mm, 2)
            dve.tensor_copy(logits[:, :, :], bank[6][:, 0:NT * E1].rearrange("p (j e) -> p j e", j=NT)).then_inc(s.logit, 1)
            ranks(2)
            dve.tensor_tensor(coef[:, :, :], logits[:, :, :], top[:, :, 0:1].broadcast_to([P, NT, E1]), ALU.subtract).then_inc(s.b_shift, 1)
            dve.wait_ge(s.eq1, 2)
            dve.tensor_tensor(selh[:, :, :], sel[:, 0, :, :], sel[:, 1, :, :], ALU.add).then_inc(s.selh, 1)
            dve.wait_ge(s.b_exp, 1)
            dve.tensor_reduce(two[:, 0, :], coef[:, :, :], AX.X, ALU.add).then_inc(s.b_sum, 1)
            dve.wait_ge(s.b_sum, 1)
            dve.reciprocal(two[:, 1, :], two[:, 0, :]).then_inc(s.b_rec, 1)
            dve.wait_ge(s.b_rec, 1)
            dve.tensor_tensor(coef[:, :, :], coef[:, :, :], two[:, 1, :].rearrange("p (j one) -> p j one", one=1).broadcast_to([P, NT, E1]),
                              ALU.mult).then_inc(s.b_prob, 1)
            dve.wait_ge(s.b_prob, 1)
            dve.wait_ge(s.pos, 1)
            dve.wait_ge(s.selh, 1)
            dve.scalar_tensor_tensor(out=slot[:, :, :], in0=selh[:, :, :], scalar=-BIG,
                                     in1=bank[5][:, 0:NT * E1].rearrange("p (j e) -> p j e", j=NT),
                                     op0=ALU.mult, op1=ALU.add).then_inc(s.slot, 1)
            dve.wait_ge(s.slot, 1)
            for j in range(NT):
                dve.tensor_tensor(disp[:, j, :, :],
                                  wk("slots").rearrange("p (one c) -> p one c", one=1).broadcast_to([P, E1, CAP]),
                                  slot[:, j, :].rearrange("p (e one) -> p e one", one=1).broadcast_to([P, E1, CAP]),
                                  ALU.is_equal).then_inc(s.disp, 1)
            for e in range(E1 + 1):
                if e < E1:
                    for c in range(C1):
                        q = e * C1 + c
                        dve.wait_ge(s.h_mm, q // 2 + 1)
                        if e >= 2 and c == 0:
                            dve.wait_ge(s.y_mm, B * (e - 1))
                        last = dve.tensor_scalar(h1[:, e % 2, c, :], bank[2 + c // 2][:, (c % 2) * B * CAP:(c % 2 + 1) * B * CAP],
                                                 wk("b1", q, 1), 0.0, ALU.add, ALU.max)
                        if c % 2:
                            last.then_inc(s.h_ready, 1)
                if e >= 1:
                    for b in range(B):
                        n = B * (e - 1) + b
                        dve.wait_ge(s.y_mm, n + 1)
                        if e - 1 >= 2:
                            dve.wait_ge(s.comb, e - 2)
                        dve.tensor_tensor(y1[:, (e - 1) % 2, b, :], bank[4 + b][0:CAP, 0:D],
                                          wk("b2", (e - 1) * D, D)[0:CAP, :], ALU.add).then_inc(s.y_ready, 1)
            dve.wait_ge(s.comb, E1)
            for b in range(B):
                xs = X[:, b * TPB:(b + 1) * TPB, :].rearrange("p j d -> p (j d)")
                dve.tensor_tensor(xs, xs, bank[6 + b][:, :], ALU.add).then_inc(s.final, 1)

        @block.tensor
        def _(pe):
            def mm(o, l, r, start=True, stop=True, **kw):
                return pe.matmul(o, lhsT=l, rhs=r, start=start, stop=stop, **kw)

            def ln(k, b):
                i = 2 * k + b
                pe.wait_ge(s.normed, i + 1)
                if i:
                    pe.wait_ge(s.nT, i)
                for j in range(TPB):
                    last = pe.transpose(bank[7][:, j * P:(j + 1) * P], N[:, b * TPB + j, :], ident)
                last.then_inc(s.turned, 1)
                pe.wait_ge(s.nT, i + 1)

            pe.wait_ge(s.early_in, 16)
            for b in range(B):
                ln(LN_X, b)
            for b in range(B):
                if b:
                    pe.wait_ge(s.k_ready, b)
                mm(bank[1][:, :], ea("win", 2 * D, D), seq(nT, b)).then_inc(s.p_lg, 1)
                if b:
                    pe.wait_ge(s.q_ready, b)
                mm(bank[0][:, :], ea("win", D, D), seq(nT, b)).then_inc(s.p_q, 1)
                if b:
                    pe.wait_ge(s.g1_ready, b)
                mm(bank[2][:, :], ea("wg1"), seq(nT, b)).then_inc(s.p_g1, 1)
                if b:
                    pe.wait_ge(s.v_ready, b)
                for j in range(TPB):
                    last = mm(bank[3][:, j * P:(j + 1) * P], tile(nT, b * TPB + j), ea("win", 0, D))
                last.then_inc(s.p_v, 1)
                pe.wait_ge(s.g1_ready, b + 1)
                if b:
                    pe.wait_ge(s.gate_ready, b)
                for j in range(TPB):
                    last = mm(bank[4][:, j * P:(j + 1) * P], tile(g1T, b * TPB + j), ea("wg2"))
                last.then_inc(s.p_gate, 1)
            for lv in range(LEVELS):
                for b in range(B):
                    i = B * lv + b
                    if lv == 0:
                        pe.wait_ge(s.k_ready, b + 1)
                        pe.wait_ge(s.q_ready, b + 1)
                    else:
                        pe.wait_ge(s.level_kept, i - B + 1)
                        pe.wait_ge(s.qp_step, i - B + 1)
                        if lv >= 2:
                            pe.wait_ge(s.ks_step, i - 2 * B + 1)
                    for j in range(TPB):
                        t = b * TPB + j
                        last = mm(bank[5 + b][:, j * P:(j + 1) * P], tile(ks, t), tile(qp, t))
                    last.then_inc(s.level_mm, 1)
                if lv == 1:
                    pe.wait_ge(s.work_in, 16)
                    pe.wait_ge(s.g1_ready, B)
                    pe.wait_ge(s.v_ready, B)
                    at = WORK["ctx0"][0]
                    both = work_sb[:, at:at + 6 * KEYS].rearrange("p (b n) -> p b n", b=B)
                    for l in range(2):
                        mm(bank[2 + l][:, 0:B * KEYS].rearrange("p (b k) -> p b k", b=B), wk(f"wk{l}"), both[:, :, 0:KEYS]).then_inc(s.kT_mm, 1)
                    pe.wait_ge(s.kT_ready, 2)
                    pe.wait_ge(s.gate_ready, B)
                    wv = work_sb[:, WORK["wv0"][0]:WORK["wv0"][0] + 2 * D].rearrange("p (l d) -> p l d", l=2)
                    for b in range(B):
                        for c in range(NCH):
                            n = 2 * NHC * HD
                            last = mm(bank[3 + b][:, c * n:(c + 1) * n].rearrange("p (l f) -> p l f", l=2),
                                      both[:, b, P * c % KEYS:P * c % KEYS + P], wv[:, :, HLO[c] * HD:(HLO[c] + NHC) * HD])
                        last.then_inc(s.vrep, 1)
            pe.wait_ge(s.q_ready, B)
            for b in range(B):
                pe.wait_ge(s.ks_step, B * (LEVELS - 2) + b + 1)
                for c in range(3):
                    last = pe.transpose(bank[b][:, c * P:(c + 1) * P], tile(ks, b * TPB + c), ident)
                last.then_inc(s.khat_T, 1)
            pe.wait_ge(s.kT_ready, 2)
            for b in range(B):
                pe.wait_ge(s.khat_ready, b + 1)
                if b:
                    pe.wait_ge(s.khat_ready, 1)
                for c in range(3):
                    mm(bank[2 if b == 0 else 0][:, c * P:(c + 1) * P], tile(khat, b * TPB + c), tile(v, b * TPB + c)).then_inc(s.upd, 1)
            for b in range(B):
                pe.wait_ge(s.level_kept, B * (LEVELS - 1) + b + 1)
                pe.wait_ge(s.qp_step, B * (LEVELS - 1) + b + 1)
                for j in range(TPB):
                    t = b * TPB + j
                    o = bank[5 + b][:, j * P:(j + 1) * P]
                    last = mm(o, tile(A, t), tile(v, t), stop=(j == 0))
                    if j:
                        pe.wait_ge(s.state_ready, B * (j - 1) + b + 1)
                        last = mm(o, tile(qp, t), state[:, b, j - 1, :], start=False)
                last.then_inc(s.o_ready, 1)
            for b in range(B):
                ln(LN_GLA, b)
                if b == 0:
                    pe.wait_ge(s.state_ready, 3 * B)
                for j in range(TPB):
                    last = mm(bank[b][:, j * P:(j + 1) * P], tile(nT, b * TPB + j), ea("wout"))
                last.then_inc(s.p_out, 1)

            def cross(l):
                for b in range(B):
                    if b == 0 and l == 1:
                        pe.wait_ge(s.x_att, B)
                    ln(LN_X0 if l == 0 else LN_X1, b)
                    if b or l == 0:
                        if b:
                            pe.wait_ge(s.qT_ready, 2 * l + b)
                        else:
                            pe.wait_ge(s.og_ready, B)
                    mm(bank[6][:, :], wk(f"wq{l}"), seq(nT, b)).then_inc(s.q_mm, 1)
                if l == 0:
                    pe.wait_ge(s.x_gla, B)
                    pe.wait_ge(s.half_in, 16)
                pe.wait_ge(s.maskT, 3)
                pe.wait_ge(s.vb_ready, 2 * B)
                for i in range(NT + 2):
                    if i < NT:
                        g, b = l * NT + i, i // TPB
                        pe.wait_ge(s.qT_ready, 2 * l + b + 1)
                        pe.wait_ge(s.kblk_ready, 2 * l + b + 1)
                        for k, (n, h0) in enumerate(zip(HEADS_OF_BANK, HEAD_BASE)):
                            if g:
                                pe.wait_ge(s.score_free, 3 * (g - 1) + k + 1)
                            o = bank[k][:, 0:n * KEYS]
                            cols = slice(h0 * KEYS, (h0 + n) * KEYS)
                            mm(o, tile(qT, i), kblk[:, l, b, cols], stop=False)
                            mT = tile(maskT0, i) if l == 0 else maskT1[:, b, :]
                            mm(o, mT, hf("maskout", KEYS)[:, cols], start=False).then_inc(s.score, 1)
                    if 1 <= i <= NT:
                        g, b = l * NT + i - 1, (i - 1) // TPB
                        pe.wait_ge(s.exp_ready, g + 1)
                        for k in range(3):
                            if g:
                                pe.wait_ge(s.pT_ready, 3 * (g - 1) + k + 1)
                            for c in range(4 * k, min(4 * k + 4, NCH)):
                                rows = P if c < NCH - 1 else LASTR
                                last = pe.transpose(bank[3 + k][0:rows, (c % 4) * P:(c % 4 + 1) * P],
                                                    probs[:, g % 2, c * P:c * P + rows], ident)
                            last.then_inc(s.pT, 1)
                        if g:
                            pe.wait_ge(s.heads_r, g)
                        for c in range(NCH):
                            pe.wait_ge(s.pT_ready, 3 * g + c // 4 + 1)
                            rows = P if c < NCH - 1 else LASTR
                            lo = HLO[c] * (HD + 1)
                            last = mm(bank[6][:, lo:lo + NHC * (HD + 1)], ptT[0:rows, c, :],
                                      vblk[0:rows, l, b, c * NHC:(c + 1) * NHC, :].rearrange("p h f -> p (h f)"),
                                      start=(c == 0), stop=(c == NCH - 1), skip_group_check=True)
                        last.then_inc(s.pv, 1)
                    if i >= 2:
                        g = l * NT + i - 2
                        pe.wait_ge(s.heads_r, g + 1)
                        if g:
                            pe.wait_ge(s.x_res, g)
                        pe.transpose(bank[7][:, 0:P], heads[:, :, :].rearrange("p h f -> p (h f)"), ident).then_inc(s.hT, 1)
                        pe.wait_ge(s.hT_ready, g + 1)
                        mm(bank[7][:, P:2 * P], headsT[:, :], wk(f"wo{l}")).then_inc(s.wo, 1)
                pe.wait_ge(s.x_res, (l + 1) * NT)

            def router(l):
                for j in range(NT):
                    last = mm(bank[6][:, j * E0:(j + 1) * E0], tile(nT, j), wk(f"wr{l}"))
                last.then_inc(s.r_mm, 1)

            cross(0)
            for b in range(B):
                ln(LN_F0, b)
            router(0)
            pe.wait_ge(s.ffn0_in, 16)
            units = [(e, b) for e in range(E0) for b in range(B)]
            for i in range(len(units) + 1):
                if i < len(units):
                    e, b = units[i]
                    for c in range(C0):
                        u = C0 * i + c
                        if u >= 2:
                            pe.wait_ge(s.hid, u - 1)
                        for m in range(2):
                            last = mm(bank[2 * (u % 2) + m][:, :], ffn0_sb[:, e, m, c * P:(c + 1) * P], seq(nT, b))
                        last.then_inc(s.gu, 1)
                if i >= 1:
                    e, b = units[i - 1]
                    pe.wait_ge(s.hid, C0 * i)
                    if i >= 3:
                        pe.wait_ge(s.x_ffn, i - 2)
                    for j in range(TPB):
                        for c in range(C0):
                            last = mm(bank[4 + (i - 1) % 2][:, j * P:(j + 1) * P], hid[:, (i - 1) % 2, c, j * P:(j + 1) * P],
                                      ffn0_sb[:, e, 2, c * P:(c + 1) * P], start=(c == 0), stop=(c == C0 - 1))
                    last.then_inc(s.down, 1)
            pe.wait_ge(s.hid, len(units) * C0)
            for b in range(B):
                ln(LN_ATT, b)
                if b:
                    pe.wait_ge(s.a_q, b)
                mm(bank[0][:, :], wk("aq"), seq(nT, b)).then_inc(s.a_qk, 1)
                if b:
                    pe.wait_ge(s.a_k, b)
                mm(bank[1][:, :], wk("ak"), seq(nT, b)).then_inc(s.a_qk, 1)
                if b:
                    pe.wait_ge(s.av_ready, b)
                for j in range(TPB):
                    last = mm(bank[2][:, j * P:(j + 1) * P], tile(nT, b * TPB + j), wk("av"))
                last.then_inc(s.a_v, 1)
            place = {0: (0, 0), 1: (1, 0), 3: (1, 3 * P), 2: (2, 0)}
            for b in range(B):
                pe.wait_ge(s.a_q, b + 1)
                pe.wait_ge(s.a_k, b + 1)
                if b == 0:
                    pe.wait_ge(s.x_ffn, len(units))
                else:
                    pe.wait_ge(s.a_exp, 3 * b)
                for kt in (0, 1, 3, 2):
                    k, at = place[kt]
                    n = S - kt * P
                    q0 = b * S + kt * P
                    o = bank[3 + k][:, at:at + n]
                    mm(o[:, 0:P], tile(akT, b * TPB + kt), qT[:, q0:q0 + P], stop=False)
                    last = mm(o[:, 0:P], hf("ident"), hf("future"), start=False)
                    if n > P:
                        last = mm(o[:, P:n], tile(akT, b * TPB + kt), qT[:, q0 + P:q0 + n])
                    if kt != 1:
                        last.then_inc(s.a_score, 1)
                pe.wait_ge(s.a_exp, 3 * b + 3)
                pe.wait_ge(s.av_ready, b + 1)
                if b:
                    pe.wait_ge(s.x_att, b)
                for j in range(TPB):
                    for kt in range(j + 1):
                        k, at = place[kt]
                        c = at + (j - kt) * P
                        last = mm(bank[6][:, j * P:(j + 1) * P], expo[:, b, k, c:c + P], av_sb[:, b * TPB + kt, :],
                                  start=(kt == 0), stop=(kt == j))
                last.then_inc(s.a_pv, 1)
            cross(1)
            for b in range(B):
                ln(LN_F1, b)
            router(1)
            pe.wait_ge(s.selh, 1)
            for j in range(NT):
                first = j // TPB * TPB
                for i in range(first, j + 1):
                    last = mm(bank[5][:, j * E1:(j + 1) * E1], hf("below") if i == j else hf("ones"), selh[:, i, :],
                              start=(i == first), stop=(i == j))
            last.then_inc(s.pos, 1)
            for b in range(B):
                pe.wait_ge(s.disp, (b + 1) * TPB)
                for half_ in range(2):
                    if b:
                        pe.wait_ge(s.xd_ready, half_ + 1)
                    for j in range(TPB):
                        t = b * TPB + j
                        last = mm(bank[half_][:, 0:4 * CAP], N[:, t, :],
                                  disp[:, t, 4 * half_:4 * half_ + 4, :].rearrange("p e c -> p (e c)"), start=(j == 0), stop=(j == TPB - 1))
                    last.then_inc(s.xd, 1)
                pe.wait_ge(s.wdisp, (b + 1) * TPB)
                for e in range(E1):
                    n = b * E1 + e
                    if n >= 2:
                        pe.wait_ge(s.dpT_ready, n - 1)
                    for j in range(TPB):
                        last = pe.transpose(bank[2 + e % 2][0:CAP, j * P:(j + 1) * P], wdisp[:, b * TPB + j, e, :], ident)
                    last.then_inc(s.dpT, 1)
            pe.wait_ge(s.dpT_ready, B * E1)
            pe.wait_ge(s.xd_ready, 2 * B)
            pe.wait_ge(s.ffn1_in, 16)
            pe.wait_ge(s.slot, 1)
            for e in range(E1 + 2):
                if e < E1:
                    for c in range(C1):
                        q = e * C1 + c
                        if e and c % 2 == 0:
                            pe.wait_ge(s.h_ready, q // 2 - 1)
                        last = mm(bank[2 + c // 2][:, (c % 2) * B * CAP:(c % 2 + 1) * B * CAP], ffn1_sb[:, e, 0, c * P:(c + 1) * P],
                                  xd[:, e, :, :].rearrange("p b c -> p (b c)"))
                        if c % 2:
                            last.then_inc(s.h_mm, 1)
                if 1 <= e <= E1:
                    pe.wait_ge(s.h_ready, 2 * e)
                    for b in range(B):
                        if e >= 2:
                            pe.wait_ge(s.y_ready, B * (e - 2) + b + 1)
                        for c in range(C1):
                            last = mm(bank[4 + b][0:CAP, 0:D], h1[:, (e - 1) % 2, c, b * CAP:(b + 1) * CAP],
                                      ffn1_sb[:, e - 1, 1, c * P:(c + 1) * P], start=(c == 0), stop=(c == C1 - 1))
                        last.then_inc(s.y_mm, 1)
                if e >= 2:
                    for b in range(B):
                        pe.wait_ge(s.y_ready, B * (e - 2) + b + 1)
                        for j in range(TPB):
                            last = mm(bank[6 + b][:, j * P:(j + 1) * P], dpT[:, b, e - 2, j * P:(j + 1) * P], y1[:, (e - 2) % 2, b, :],
                                      start=(e == 2 and j == 0), stop=(e == E1 + 1), skip_group_check=True)
                    last.then_inc(s.comb, 1)


def constants():
    r = np.arange(P)
    levels = np.zeros((P, LEVELS, P), np.float32)
    levels[r, 0, r] = 1.0
    for lv in range(1, LEVELS):
        seg = 1 << (lv - 1)
        key, query = r[:, None] // seg, r[None, :] // seg
        levels[:, lv, :] = (query == key + 1) & (key % 2 == 0)
    head = (np.arange(P)[:, None] // HD == np.arange(H)[None, :]).astype(np.float32)
    rows = np.zeros((P, NCH, NHC), np.float32)
    for c in range(NCH):
        for k in range(NHC):
            rows[:, c, k] = (P * c + r) // KEYS == HLO[c] + k
    both = lambda n, base=0.0: np.broadcast_to(np.arange(n, dtype=np.float32) + np.float32(base), (P, n))
    half = np.zeros((P, HALF_N), np.float32)
    def put(name, a):
        at, n = HALF[name]
        half[:a.shape[0], at:at + n] = a
    put("ident", np.eye(P))
    put("below", r[:, None] < r[None, :])
    put("ones", np.ones((P, P)))
    put("future", np.where(r[None, :] < r[:, None], -1e30, 0.0))
    put("maskout", np.tile(-1e18 * np.eye(KEYS), (1, H)))
    return levels.reshape(P, -1), head, rows.reshape(P, -1), both, (half.view(np.uint32) >> 16).astype(np.uint16)


def kernel(**a):
    import concourse.bacc as bacc
    from concourse.bass_utils import run_bass_kernel_spmd

    a = {k: np.asarray(v) for k, v in a.items()}
    levels, head, rows, both, half = constants()
    row = lambda v: np.broadcast_to(v.reshape(1, -1), (P, v.size))
    col = lambda v: v.reshape(P, 1)

    def pack(index, total, values):
        out = np.zeros((P, total), np.float32)
        for name, (at, n) in index.items():
            out[:, at:at + n] = values[name]
        return out

    early = pack(EARLY, EARLY_N, {
        "win": a["L0_attn_W_in"].T, "wg1": a["L0_attn_W_g1"].T, "wg2": a["L0_attn_W_g2"].T,
        "wout": a["L0_attn_W_out"].T, "lnw": col(a["L0_attn_ln_w"]), "ident": np.eye(P, dtype=np.float32)})
    ctxT = [np.tile(a["ctx_1024"][b].T, (1, 3)) for b in range(B)]
    work = pack(WORK, WORK_N, {
        "wv0": a["L0_xattn_Wv"], "wv1": a["L1_xattn_Wv"].T, "wk0": a["L0_xattn_Wk"], "wk1": a["L1_xattn_Wk"].T,
        "ctx0": ctxT[0], "ctx1": ctxT[1],
        "wq0": a["L0_xattn_Wq"], "wo0": a["L0_xattn_Wo"], "wq1": a["L1_xattn_Wq"].T, "wo1": a["L1_xattn_Wo"].T,
        "aq": a["L1_attn_Wq"], "ak": a["L1_attn_Wk"], "av": a["L1_attn_Wv"],
        "wr0": a["L0_ffn_Wr"], "wr1": a["L1_ffn_Wr"],
        "bq0": col(a["L0_xattn_bq"]), "bk0": col(a["L0_xattn_bk"]), "bv0": col(a["L0_xattn_bv"]),
        "bq1": col(a["L1_xattn_bq"]), "bk1": col(a["L1_xattn_bk"]), "bv1": col(a["L1_xattn_bv"]),
        "abq": col(a["L1_attn_bq"]), "abk": col(a["L1_attn_bk"]),
        "b1": a["L1_ffn_b1"].reshape(E1 * C1, P).T,
        "bo0": row(a["L0_xattn_bo"]), "bo1": row(a["L1_xattn_bo"]), "abv": row(a["L1_attn_bv"]),
        "br0": row(a["L0_ffn_br"]), "b2": row(a["L1_ffn_b2"]),
        "headmask": head, "rowmask": rows, "slots": both(CAP, -BIG), "experts": both(E0)})
    chunks = lambda w, n: w.reshape(w.shape[0], n, P, D).transpose(2, 0, 1, 3).reshape(P, w.shape[0], n * D)
    ffn0 = np.stack([a["L0_ffn_W1"].transpose(1, 0, 2), a["L0_ffn_W3"].transpose(1, 0, 2), chunks(a["L0_ffn_W2"], C0)], 2)
    ffn1 = np.stack([a["L1_ffn_W1"].transpose(1, 0, 2), chunks(a["L1_ffn_W2"], C1)], 2)
    padmask = a["mask_BxSxS2_bk1"].transpose(2, 0, 1).reshape(KEYS, B * S).copy().view(np.uint32)
    key = a["mask_Bx1x1xS2_if1"].reshape(B, KEYS)
    keyrows = key[:, np.arange(NCH * P) % KEYS].reshape(B, NCH, P).transpose(2, 0, 1)

    arrays = {
        "x": a["x"], "early": early, "glamask": levels, "work": work, "half": half, "padmask": padmask,
        "keymask": key.T, "keyrows": keyrows, "ffn0": ffn0.reshape(P, -1), "ffn1": ffn1.reshape(P, -1)}
    arrays = {k: np.ascontiguousarray(v) for k, v in arrays.items()}
    nc = bacc.Bacc("TRN2", target_bir_lowering=False, num_devices=1)
    args = [nc.dram_tensor(f"in_{n}", v.shape, mybir.dt.from_np(v.dtype), kind="ExternalInput").ap() for n, v in arrays.items()]
    out = nc.dram_tensor("out", (B, S, D), F32, kind="ExternalOutput").ap()
    program(nc, *args, out)
    r = run_bass_kernel_spmd(nc, [{f"in_{n}": v for n, v in arrays.items()}], core_ids=[0])
    return r.results[0]["out"]
```

```python
from collections import namedtuple
from contextlib import ExitStack

import numpy as np

import concourse.bass as bass
from concourse import mybir

ALU = mybir.AluOpType
ACT = mybir.ActivationFunctionType
AX = mybir.AxisListType
F32 = mybir.dt.float32
BF16 = mybir.dt.bfloat16
U32 = mybir.dt.uint32
I32 = mybir.dt.int32
U8 = mybir.dt.uint8

B, S, D = 2, 512, 128
P = 128
TPB = S // P
NT = B * TPB
KEYS, H, HD = 77, 16, 8
HK = H * KEYS
NCH = -(-HK // P)
LASTR = HK - (NCH - 1) * P
NHC = 3
E0, I0 = 8, 256
C0 = I0 // P
E1, I1 = 8, 512
C1 = I1 // P
CAP = int(S / E1 * 1.25)
LEVELS = 8
EPS = 1e-5
BIG = 1024.0
HEADS_OF_BANK = (6, 6, 4)
HEAD_BASE = (0, 6, 12)
HLO = [min(P * c // KEYS, H - NHC) for c in range(NCH)]
XSCALE = float(HD) ** -0.5
ASCALE = float(D) ** -0.5


LN_X, LN_GLA, LN_X0, LN_F0, LN_ATT, LN_X1, LN_F1 = range(7)
LN_AT = {kb: n for n, kb in enumerate([
    (LN_X, 0), (LN_X, 1), (LN_GLA, 0), (LN_GLA, 1), (LN_X0, 0), (LN_X0, 1), (LN_F0, 0), (LN_F0, 1),
    (LN_ATT, 0), (LN_X1, 0), (LN_ATT, 1), (LN_X1, 1), (LN_F1, 0), (LN_F1, 1)])}
LN_BEFORE = [[LN_AT[LN_X0, 1] + 1 + (i > 6) for i in range(NT + 2)],
             [LN_AT[LN_ATT, 1] + 1 + (i > 3) + (i > 6) for i in range(NT + 2)]]
UNITS = [(b, e) for b in range(B) for e in range(E0)]
LEVEL_BANK = ((5, 6), (7, 4))
VREP_BANK = (3, 1)
A_TILES = ((0,), (1, 3), (2,))
A_COLS = (S, S, 2 * P)
A_PLACE = {0: (0, 0), 1: (1, 0), 3: (1, 3 * P), 2: (2, 0)}


def columns(*parts):
    at, out = 0, {}
    for name, n in parts:
        out[name] = (at, n)
        at += n
    return out, at


EARLY, EARLY_N = columns(("win", 3 * D), ("wg1", D), ("wg2", D), ("wout", D), ("lnw", 1), ("ident", P))
GLA_MASK_N = LEVELS * P
WORK, WORK_N = columns(
    ("wv0", D), ("wv1", D), ("wk0", D), ("wk1", D), ("ctx0", 3 * KEYS), ("ctx1", 3 * KEYS),
    ("wq0", D), ("wo0", D), ("wq1", D), ("wo1", D), ("aq", D), ("ak", D), ("av", D),
    ("wr0", E0), ("wr1", E1),
    ("bq0", 1), ("bk0", 1), ("bv0", 1), ("bq1", 1), ("bk1", 1), ("bv1", 1), ("abq", 1), ("abk", 1),
    ("b1", E1 * C1),
    ("bo0", D), ("bo1", D), ("abv", D), ("br0", E0), ("b2", E1 * D),
    ("headmask", H), ("rowmask", NCH * NHC), ("slots", CAP), ("experts", E0),
)
HALF, HALF_N = columns(("ident", P), ("below", P), ("ones", P), ("future", P), ("maskout", HK))


def program(nc, x, early, glamask, work, half, padmask, keymask, keyrows, ffn0, ffn1, out):
    ctx = ExitStack()
    with ctx:
        def sb(name, shape, dt=F32):
            return ctx.enter_context(nc.sbuf_tensor(name, shape, dt))

        X = sb("X", [P, NT, D])
        N = sb("N", [P, NT, D])
        nT = sb("nT", [P, NT * P])
        early_sb = sb("early_sb", [P, EARLY_N])
        work_sb = sb("work_sb", [P, WORK_N])
        half_sb = sb("half_sb", [P, HALF_N], mybir.dt.uint16)
        ffn1_sb = sb("ffn1_sb", [P, E1, 2, I1])
        stats = sb("stats", [P, TPB, 6])
        moments = sb("moments", [P, TPB, 2])
        logvar = sb("logvar", [P, TPB])
        rstd = sb("rstd", [P, TPB])
        tiny = sb("tiny", [P, 1])

        def wk(name, lo=0, n=None):
            at, size = WORK[name]
            return work_sb[:, at + lo:at + (size if n is None else lo + n)]

        def ea(name, lo=0, n=None):
            at, size = EARLY[name]
            return early_sb[:, at + lo:at + (size if n is None else lo + n)]

        def hf(name, rows=P):
            at, size = HALF[name]
            return half_sb[0:rows, at:at + size].bitcast(BF16)

        region_a = sb("region_a", [P, 11 * NT * P + 3 * B * D])
        gla = [region_a[:, i * NT * P:(i + 1) * NT * P] for i in range(11)]
        decay, qp, ks, sig, A, v, gate, khat, g1T, og, glam = gla
        state = region_a[:, 11 * NT * P:].rearrange("p (b c e) -> p b c e", b=B, c=3)
        dpT = region_a[0:CAP, 0:B * E1 * S].rearrange("p (b e t) -> p b e t", b=B, e=E1)
        region_b = sb("region_b", [P, E0 * 3 * I0])
        ffn0_sb = region_b[:, :].rearrange("p (e m i) -> p e m i", e=E0, m=3)
        disp = region_b[:, 0:NT * E1 * CAP].rearrange("p (j e c) -> p j e c", j=NT, e=E1)
        region_c = sb("region_c", [P, 6 * HK])
        kblk = region_c[:, 0:4 * HK].rearrange("p (l b n) -> p l b n", l=2, b=B)
        probs = region_c[:, 4 * HK:].rearrange("p (i n) -> p i n", i=2)
        wdisp = region_c[:, 0:NT * E1 * CAP].rearrange("p (j e c) -> p j e c", j=NT, e=E1)

        totals = sb("totals", [P, 2 * NT * P])
        vblk = sb("vblk", [P, 2, B, NCH * NHC, HD + 1])
        rowm1 = sb("rowm1", [P, B, NCH * NHC])
        keep1 = sb("keep1", [P, B, NCH])
        keyrows_sb = sb("keyrows_sb", [P, B, NCH], I32)
        keymask_sb = sb("keymask_sb", [KEYS, B], I32)
        padmask_sb = sb("padmask_sb", [KEYS, NT * P // 4], U32)
        maskT0 = sb("maskT0", [KEYS, NT * P], BF16)
        maskT1 = sb("maskT1", [KEYS, B, P], BF16)
        keyoff = sb("keyoff", [KEYS, B])
        kT = sb("kT", [P, 2, B, KEYS])
        qT = sb("qT", [P, NT * P])
        ptT = sb("ptT", [P, NCH, P])
        rowmax = sb("rowmax", [P, H])
        rsum = sb("rsum", [P, H])
        heads = sb("heads", [P, H, HD])
        headsT = sb("headsT", [P, P])
        logits = sb("logits", [P, NT, E0])
        top = sb("top", [P, NT, 8])
        topi = sb("topi", [P, NT, 8], U32)
        topf = sb("topf", [P, NT, 2])
        two = sb("two", [P, 3, NT])
        sel = sb("sel", [P, 2, NT, E0])
        coef = sb("coef", [P, NT, E0])
        selh = sb("selh", [P, NT, E1], BF16)
        slot = sb("slot", [P, NT, E1])
        late = 8 * NT * P
        gact = region_a[:, late:late + 2 * S].rearrange("p (i t) -> p i t", i=2)
        hid = region_a[:, late + 2 * S:late + 2 * S + 2 * C0 * S].rearrange("p (i c t) -> p i c t", i=2, c=C0)
        akT = region_a[:, 0:NT * P]
        aqT = region_a[:, 2 * NT * P:3 * NT * P]
        av_sb = region_a[:, NT * P:2 * NT * P].rearrange("p (j d) -> p j d", j=NT)
        expo = region_a[:, 3 * NT * P:3 * NT * P + B * 3 * S].rearrange("p (b k t) -> p b k t", b=B, k=3)
        amax = sb("amax", [P, B, 4])
        gmax = sb("gmax", [P, B])
        nmax = sb("nmax", [P, B])
        asum = sb("asum", [P, B, 4])
        gsum = sb("gsum", [P, B])
        rtot = sb("rtot", [P, B])
        xd = sb("xd", [P, E1, B, CAP])
        h1 = sb("h1", [P, 2, C1, B * CAP])
        y1 = sb("y1", [CAP, 2, B, D])

        bank = [ctx.enter_context(nc.psum_tensor(f"bank{i}", [P, 512], F32)) for i in range(8)]

        names = """early_in glam_in work_in half_in masks_in ffn0_in ffn1_in out_done
        x_in0 x_in1 stats moments logvar rstd normed turned nT
        p_lg p_q p_g1 p_v p_gate f_ready k_ready sigq q_ready g1_ready v_ready gate_ready
        A_zero level_mm level_kept qp_step ks_step tot_step khat_T khat_ready upd state_ready
        o_ready og_ready x_gla p_out
        kT_mm kT_ready vrep vb_ready kblk_ready setup keyoff rowm maskT
        q_mm qT_ready score score_free rmax probs_ready exp_ready pT pT_ready pv heads_r rsum_r hT hT_ready
        wo x_bias x_res
        r_mm logit top topi topf diff ediff one w1 w2 eq1 coef_p coef
        gu act hid down x_ffn act_free
        a_q a_k a_qk a_v av_ready a_score a_raw a_pmax a_max a_gmax a_nmax a_exp a_sum a_gsum a_rtot a_pv x_att
        b_shift b_exp b_sum b_rec b_prob selp selh pos slot disp wdisp xd xd_ready dpT dpT_ready
        h_mm h_ready y_mm y_ready comb final""".split()
        s = namedtuple("Signals", names)(*[ctx.enter_context(nc.semaphore(n)) for n in names])
        block = ctx.enter_context(nc.Block())

        tile = lambda t, j: t[:, j * P:(j + 1) * P]
        seq = lambda t, b: t[:, b * S:(b + 1) * S]
        ident = ea("ident")

        def total(level, b):
            if level == 0:
                return seq(decay, b)
            at = sum(NT * P >> i for i in range(1, level))
            n = S >> level
            return totals[:, at + b * n:at + (b + 1) * n]

        @block.sync
        def _(sp):
            sp.dma_start(X[:, 0:TPB, :], x[0].rearrange("(j p) d -> p j d", p=P)).then_inc(s.x_in0, 16)
            sp.dma_start(early_sb[:, :], early).then_inc(s.early_in, 16)
            sp.dma_start(X[:, TPB:NT, :], x[1].rearrange("(j p) d -> p j d", p=P)).then_inc(s.x_in1, 16)
            sp.dma_start(glam[:, 0:GLA_MASK_N], glamask).then_inc(s.glam_in, 16)
            sp.dma_start(work_sb[:, :], work).then_inc(s.work_in, 16)
            sp.wait_ge(s.work_in, 16)
            sp.dma_start(ffn0_sb[:, :, :, :], ffn0.rearrange("p (e m i) -> p e m i", e=E0, m=3)).then_inc(s.ffn0_in, 16)
            sp.wait_ge(s.ffn0_in, 16)
            sp.dma_start(ffn1_sb[:, :, :, :], ffn1.rearrange("p (e m i) -> p e m i", e=E1, m=2)).then_inc(s.ffn1_in, 16)
            for b in range(B):
                sp.wait_ge(s.final, b + 1)
                sp.dma_start(out[b].rearrange("(j p) d -> p j d", p=P),
                             X[:, b * TPB:(b + 1) * TPB, :]).then_inc(s.out_done, 16)
            sp.wait_ge(s.out_done, 16 * B)

        @block.gpsimd
        def _(pool):
            pool.dma_start(half_sb[:, :], half).then_inc(s.half_in, 16)
            pool.dma_start(padmask_sb[:, :], padmask).then_inc(s.masks_in, 16)
            pool.dma_start(keymask_sb[:, :], keymask).then_inc(s.masks_in, 16)
            pool.dma_start(keyrows_sb[:, :, :], keyrows).then_inc(s.masks_in, 16)
            pool.memset(A, 0.0).then_inc(s.A_zero, 1)
            for lv in range(1, LEVELS):
                for b in range(B):
                    if lv == 1:
                        pool.wait_ge(s.f_ready, b + 1)
                        pool.wait_ge(s.k_ready, b + 1)
                    else:
                        pool.wait_ge(s.tot_step, B * (lv - 2) + b + 1)
                    t = total(lv - 1, b).rearrange("p (n two) -> p n two", two=2)
                    pool.tensor_tensor(total(lv, b), t[:, :, 0], t[:, :, 1], ALU.mult).then_inc(s.tot_step, 1)
                    pool.wait_ge(s.level_mm, B * lv + b + 1)
                    seg = 1 << (lv - 1)
                    kv = seq(ks, b).rearrange("p (n two g) -> p n two g", two=2, g=seg)[:, :, 0, :]
                    right = t[:, :, 1].rearrange("p (n one) -> p n one", one=1).broadcast_to([P, S // (2 * seg), seg])
                    pool.tensor_tensor(kv, kv, right, ALU.mult).then_inc(s.ks_step, 1)
            for l in range(2):
                for b in range(B):
                    pool.wait_ge(s.kT_ready, 1)
                    pool.wait_ge(s.work_in, 16)
                    pool.tensor_tensor(
                        kblk[:, l, b, :].rearrange("p (h k) -> p h k", h=H),
                        kT[:, l, b, :].rearrange("p (one k) -> p one k", one=1).broadcast_to([P, H, KEYS]),
                        wk("headmask").rearrange("p (h one) -> p h one", one=1).broadcast_to([P, H, KEYS]),
                        ALU.mult).then_inc(s.kblk_ready, 1)

            def add_bias(l, b):
                pool.wait_ge(s.normed, LN_AT[LN_X1 if l else LN_X0, b] + 1)
                xs = X[:, b * TPB:(b + 1) * TPB, :]
                bo = wk("bo1" if l else "bo0").rearrange("p (one d) -> p one d", one=1).broadcast_to([P, TPB, D])
                pool.tensor_tensor(xs, xs, bo, ALU.add).then_inc(s.x_bias, 1)

            def attention(b):
                pool.wait_ge(s.a_max, b + 1)
                pool.partition_all_reduce(gmax[:, b:b + 1], amax[:, b, 3:4], P, bass.bass_isa.ReduceOp.max).then_inc(s.a_gmax, 1)
                pool.wait_ge(s.a_sum, b + 1)
                pool.partition_all_reduce(gsum[:, b:b + 1], asum[:, b, 3:4], P, bass.bass_isa.ReduceOp.add).then_inc(s.a_gsum, 1)

            add_bias(0, 0)
            add_bias(0, 1)
            attention(0)
            add_bias(1, 0)
            attention(1)
            add_bias(1, 1)
            for j in range(NT):
                pool.wait_ge(s.disp, j + 1)
                if j == 0:
                    pool.wait_ge(s.pT, 3 * 2 * NT)
                pool.tensor_tensor(
                    wdisp[:, j, :, :], disp[:, j, :, :],
                    coef[:, j, :].rearrange("p (e one) -> p e one", one=1).broadcast_to([P, E1, CAP]),
                    ALU.mult).then_inc(s.wdisp, 1)

        @block.scalar
        def _(act):
            def ln_rstd(k, b):
                i = LN_AT[k, b]
                act.wait_ge(s.moments, i + 1)
                if i:
                    act.wait_ge(s.normed, i)
                act.activation(logvar[:, :], moments[:, :, 1], ACT.Ln, bias=tiny[:, 0:1]).then_inc(s.logvar, 1)
                act.wait_ge(s.logvar, i + 1)
                act.activation(rstd[:, :], logvar[:, :], ACT.Exp, scale=-0.5).then_inc(s.rstd, 1)

            def ln_out(k, b, scale=1.0):
                act.wait_ge(s.turned, LN_AT[k, b] + 1)
                act.activation(seq(nT, b), bank[7][:, :], ACT.Copy, scale=scale).then_inc(s.nT, 1)

            act.wait_ge(s.setup, 1)
            act.preload_act_table_set("natural_log_exp_and_others")
            for b in range(B):
                ln_rstd(LN_X, b)
                ln_out(LN_X, b)
            for b in range(B):
                act.wait_ge(s.p_lg, b + 1)
                act.activation(seq(decay, b), bank[1][:, :], ACT.Sigmoid).then_inc(s.f_ready, 1)
                act.activation(seq(ks, b), bank[1][:, :], ACT.Sigmoid, scale=-1.0).then_inc(s.k_ready, 1)
                act.wait_ge(s.p_q, b + 1)
                act.activation(seq(sig, b), bank[0][:, :], ACT.Sigmoid).then_inc(s.sigq, 1)
                act.wait_ge(s.p_g1, b + 1)
                act.copy(seq(g1T, b), bank[2][:, :]).then_inc(s.g1_ready, 1)
                act.wait_ge(s.p_v, b + 1)
                act.copy(seq(v, b), bank[3][:, :]).then_inc(s.v_ready, 1)
                act.wait_ge(s.p_gate, b + 1)
                act.activation(seq(gate, b), bank[4][:, :], ACT.Sigmoid).then_inc(s.gate_ready, 1)
            act.wait_ge(s.kT_mm, 1)
            for l in range(2):
                last = act.activation(kT[:, l, :, :], bank[2][:, l * B * KEYS:(l + 1) * B * KEYS].rearrange("p (b k) -> p b k", b=B),
                                      ACT.Identity, bias=wk(f"bk{l}"))
            last.then_inc(s.kT_ready, 1)
            act.preload_act_table_set("natural_log_exp_and_others")
            for b in range(B):
                act.wait_ge(s.khat_T, b + 1)
                act.copy(seq(khat, b)[:, 0:3 * P], bank[2 * b][:, 0:3 * P]).then_inc(s.khat_ready, 1)
            for b in range(B):
                ln_rstd(LN_GLA, b)
                ln_out(LN_GLA, b, scale=ea("lnw"))

            def query(l, b):
                act.wait_ge(s.q_mm, 2 * l + b + 1)
                act.activation(seq(qT, b), bank[5][:, :], ACT.Identity, bias=wk(f"bq{l}")).then_inc(s.qT_ready, 1)

            def attention(b, part):
                if part == 0:
                    act.wait_ge(s.a_qk, 2 * b + 1)
                    act.activation(seq(aqT, b), bank[5][:, :], ACT.Identity, bias=wk("abq")).then_inc(s.a_q, 1)
                elif part == 1:
                    act.wait_ge(s.a_qk, 2 * b + 2)
                    act.activation(seq(akT, b), bank[5][:, :], ACT.Identity, bias=wk("abk")).then_inc(s.a_k, 1)
                elif part < 5:
                    k = part - 2
                    act.wait_ge(s.a_score, 3 * b + k + 1)
                    act.copy(expo[:, b, k, 0:A_COLS[k]], bank[5][:, 0:A_COLS[k]]).then_inc(s.a_raw, 1)
                else:
                    act.wait_ge(s.a_gmax, b + 1)
                    act.mul(nmax[:, b:b + 1], gmax[:, b:b + 1], -ASCALE).then_inc(s.a_nmax, 1)
                    act.wait_ge(s.a_nmax, b + 1)
                    for k, n in enumerate(A_COLS):
                        act.activation(expo[:, b, k, 0:n], expo[:, b, k, 0:n], ACT.Exp, bias=nmax[:, b:b + 1],
                                       scale=ASCALE, accum_out=asum[:, b, k:k + 1]).then_inc(s.a_exp, 1)

            def router_exp(b):
                cf = coef[:, b * TPB:(b + 1) * TPB, :]
                act.wait_ge(s.b_shift, b + 1)
                act.activation(cf, cf, ACT.Exp).then_inc(s.b_exp, 1)

            def cross(l):
                for i in range(NT + 2):
                    if l == 0:
                        if i == 2:
                            ln_out(LN_X0, 1)
                        if i == 3:
                            query(0, 1)
                        if i == 7:
                            ln_out(LN_F0, 0)
                    else:
                        if i == 1:
                            attention(1, 2)
                        if i == 2:
                            attention(1, 4)
                        if i == 7:
                            ln_out(LN_F1, 0)
                    for k in range(3):
                        if k == 2 and i >= 2:
                            g = l * NT + i - 2
                            act.wait_ge(s.hT, g + 1)
                            act.activation(headsT[:, :], bank[7][:, 0:P], ACT.Identity, bias=wk(f"bv{l}")).then_inc(s.hT_ready, 1)
                        if 1 <= i <= NT:
                            g = l * NT + i - 1
                            if g and k == 0:
                                act.wait_ge(s.pv, g)
                            act.wait_ge(s.pT, 3 * g + k + 1)
                            pt = bank[3 + (3 * g + k) % 2]
                            if k < 2:
                                act.copy(ptT[:, 4 * k:4 * k + 4, :].rearrange("p c q -> p (c q)"), pt[:, :]).then_inc(s.pT_ready, 1)
                            else:
                                act.copy(ptT[:, 8, :], pt[:, 0:P])
                                act.copy(ptT[0:LASTR, 9, :], pt[0:LASTR, P:2 * P]).then_inc(s.pT_ready, 1)
                    if i < NT:
                        g = l * NT + i
                        act.wait_ge(s.probs_ready, 3 * g + 3)
                        act.activation(probs[:, g % 2, :], probs[:, g % 2, :], ACT.Exp, scale=XSCALE).then_inc(s.exp_ready, 1)
                    if l == 0:
                        if i == 0:
                            ln_rstd(LN_X0, 1)
                        if i == 5:
                            ln_rstd(LN_F0, 0)
                    if l == 1:
                        if i == 5:
                            ln_rstd(LN_F1, 0)
                        if i == 0:
                            ln_out(LN_ATT, 1)
                            attention(1, 0)
                            attention(1, 1)
                        if i == 1:
                            attention(1, 3)
                        if i == 2:
                            attention(1, 5)
                        if i == 3:
                            ln_rstd(LN_X1, 1)
                            ln_out(LN_X1, 1)
                            query(1, 1)
                        if i == 8:
                            router_exp(0)

            ln_rstd(LN_X0, 0)
            ln_out(LN_X0, 0)
            query(0, 0)
            cross(0)
            act.wait_ge(s.diff, 1)
            act.activation(two[:, 1, 0:TPB], two[:, 0, 0:TPB], ACT.Exp).then_inc(s.ediff, 1)
            ln_rstd(LN_F0, 1)
            for i in range(len(UNITS)):
                for u in range(C0 * i, C0 * i + C0):
                    act.wait_ge(s.gu, u + 1)
                    if u >= 2:
                        act.wait_ge(s.hid, u - 1)
                    act.activation(gact[:, u % 2, :], bank[2 * (u % 2)][:, :], ACT.Silu).then_inc(s.act, 1)
                    if (i, u % C0) == (E0 + 2, 0):
                        attention(0, 0)
                    if (i, u % C0) == (E0 + 2, 1):
                        attention(0, 1)
                    if (i, u % C0) == (E0 + 3, 0):
                        attention(0, 2)
                    if (i, u % C0) == (E0 + 3, 1):
                        attention(0, 3)
                    if (i, u % C0) == (E0 + 4, 0):
                        attention(0, 4)
                    if (i, u % C0) == (E0 + 6, 1):
                        ln_out(LN_X1, 0)
                    if (i, u % C0) == (E0 + 7, 1):
                        query(1, 0)
                if i == 1:
                    ln_out(LN_F0, 1)
                if i == 2:
                    act.preload_act_table_set("natural_log_exp_and_others")
                    act.wait_ge(s.diff, 2)
                    act.activation(two[:, 1, TPB:NT], two[:, 0, TPB:NT], ACT.Exp).then_inc(s.ediff, 1)
                if i == E0:
                    act.preload_act_table_set("natural_log_exp_and_others")
                    ln_rstd(LN_ATT, 0)
                if i == E0 + 1:
                    ln_out(LN_ATT, 0)
                if i == E0 + 4:
                    act.preload_act_table_set("natural_log_exp_and_others")
                    attention(0, 5)
                if i == E0 + 5:
                    act.preload_act_table_set("natural_log_exp_and_others")
                    ln_rstd(LN_X1, 0)
            act.preload_act_table_set("natural_log_exp_and_others")
            ln_rstd(LN_ATT, 1)
            cross(1)
            ln_rstd(LN_F1, 1)
            ln_out(LN_F1, 1)

            def dispatched(b):
                for hf_ in range(2):
                    act.wait_ge(s.xd, 2 * b + hf_ + 1)
                    act.copy(xd[:, 4 * hf_:4 * hf_ + 4, b, :],
                             bank[hf_][:, 0:4 * CAP].rearrange("p (e c) -> p e c", e=4)).then_inc(s.xd_ready, 1)

            def weights_turned(b):
                for e in range(E1):
                    act.wait_ge(s.dpT, b * E1 + e + 1)
                    act.copy(dpT[:, b, e, :], bank[2 + e % 2][0:CAP, :]).then_inc(s.dpT_ready, 1)

            dispatched(0)
            router_exp(1)
            weights_turned(0)
            dispatched(1)
            weights_turned(1)

        @block.vector
        def _(dve):
            def ln_moments(k, b, src):
                i = LN_AT[k, b]
                if i:
                    dve.wait_ge(s.normed, i)
                for j in range(TPB):
                    last = dve.bn_stats(stats[:, j, :], src[:, b * TPB + j, :])
                last.then_inc(s.stats, 1)
                dve.wait_ge(s.stats, i + 1)
                for j in range(TPB):
                    last = dve.bn_aggr(moments[:, j, :], stats[:, j, :])
                last.then_inc(s.moments, 1)

            def ln_norm(k, b, src):
                i = LN_AT[k, b]
                dve.wait_ge(s.rstd, i + 1)
                if i:
                    dve.wait_ge(s.turned, i)
                for j in range(TPB):
                    last = dve.tensor_scalar(N[:, b * TPB + j, :], src[:, b * TPB + j, :], moments[:, j, 0:1],
                                             rstd[:, j:j + 1], ALU.subtract, ALU.mult)
                last.then_inc(s.normed, 1)

            def ln(k, b, src):
                ln_moments(k, b, src)
                ln_norm(k, b, src)

            dve.memset(tiny[:, :], EPS).then_inc(s.setup, 1)
            dve.wait_ge(s.x_in0, 16)
            ln(LN_X, 0, X)
            dve.wait_ge(s.x_in1, 16)
            ln(LN_X, 1, X)
            for b in range(B):
                dve.wait_ge(s.sigq, b + 1)
                dve.tensor_tensor(seq(qp, b), bank[0][:, :], seq(sig, b), ALU.mult).then_inc(s.q_ready, 1)
            dve.wait_ge(s.glam_in, 16)
            dve.wait_ge(s.A_zero, 1)
            for lv in range(LEVELS):
                for b in range(B):
                    i = B * lv + b
                    dve.wait_ge(s.level_mm, i + 1)
                    if lv == 0:
                        dve.wait_ge(s.f_ready, b + 1)
                        dve.tensor_tensor(seq(qp, b), seq(qp, b), seq(decay, b), ALU.mult).then_inc(s.qp_step, 1)
                    else:
                        seg = 1 << (lv - 1)
                        if lv >= 2:
                            dve.wait_ge(s.tot_step, B * (lv - 2) + b + 1)
                        dve.wait_ge(s.qp_step, i - B + 1)
                        qv = seq(qp, b).rearrange("p (n two g) -> p n two g", two=2, g=seg)[:, :, 1, :]
                        left = total(lv - 1, b).rearrange("p (n two) -> p n two", two=2)[:, :, 0]
                        left = left.rearrange("p (n one) -> p n one", one=1).broadcast_to([P, S // (2 * seg), seg])
                        dve.tensor_tensor(qv, qv, left, ALU.mult).then_inc(s.qp_step, 1)
                    if lv:
                        dve.wait_ge(s.level_kept, i - B + 1)
                    dve.copy_predicated(
                        seq(A, b).rearrange("p (j t) -> p j t", j=TPB),
                        tile(glam, lv).rearrange("p (one t) -> p one t", one=1).broadcast_to([P, TPB, P]).bitcast(U32),
                        bank[LEVEL_BANK[lv % 2][b]][:, :].rearrange("p (j t) -> p j t", j=TPB)).then_inc(s.level_kept, 1)
            for c in range(3):
                for b in range(B):
                    dve.wait_ge(s.upd, 3 * (b + 1))
                    u = bank[2 * b][:, c * P:(c + 1) * P]
                    if c == 0:
                        dve.tensor_copy(state[:, b, 0, :], u).then_inc(s.state_ready, 1)
                    else:
                        if c == 1:
                            dve.wait_ge(s.tot_step, B * (LEVELS - 2) + b + 1)
                        dve.wait_ge(s.state_ready, B * (c - 1) + b + 1)
                        dve.scalar_tensor_tensor(out=state[:, b, c, :], in0=state[:, b, c - 1, :],
                                                 scalar=total(LEVELS - 1, b)[:, c:c + 1], in1=u,
                                                 op0=ALU.mult, op1=ALU.add).then_inc(s.state_ready, 1)
            dve.wait_ge(s.work_in, 16)
            dve.wait_ge(s.masks_in, 48)
            dve.tensor_scalar(keep1[:, :, :], keyrows_sb[:, :, :], 0.0, None, ALU.not_equal).then_inc(s.rowm, 1)
            dve.tensor_scalar(keyoff[:, :], keymask_sb[:, :], 0.0, None, ALU.is_equal).then_inc(s.keyoff, 1)
            dve.tensor_copy(maskT0[:, :], padmask_sb[:, :].bitcast(U8)).then_inc(s.maskT, 1)
            dve.wait_ge(s.rowm, 1)
            for b in range(B):
                dve.tensor_tensor(
                    rowm1[:, b, :].rearrange("p (c h) -> p c h", c=NCH),
                    wk("rowmask").rearrange("p (c h) -> p c h", c=NCH),
                    keep1[:, b, :].rearrange("p (c one) -> p c one", one=1).broadcast_to([P, NCH, NHC]),
                    ALU.mult).then_inc(s.rowm, 1)
            dve.wait_ge(s.keyoff, 1)
            for b in range(B):
                dve.tensor_copy(maskT1[:, b, :], keyoff[:, b:b + 1].broadcast_to([KEYS, P])).then_inc(s.maskT, 1)
            ogv = og.rearrange("p (j d) -> p j d", j=NT)
            for b in range(B):
                dve.wait_ge(s.o_ready, b + 1)
                dve.wait_ge(s.gate_ready, b + 1)
                dve.tensor_tensor(seq(og, b), bank[5 + b][:, :], seq(gate, b), ALU.mult).then_inc(s.og_ready, 1)
                dve.wait_ge(s.og_ready, b + 1)
                ln(LN_GLA, b, ogv)
            dve.wait_ge(s.rowm, 1 + B)
            for b in range(B):
                dve.wait_ge(s.vrep, b + 1)
                for l in range(2):
                    m = wk("rowmask") if l == 0 else rowm1[:, b, :]
                    m = m.rearrange("p (n one) -> p n one", one=1)
                    pv = bank[VREP_BANK[b]][:, 0:NCH * 2 * NHC * HD].rearrange("p (c l n) -> p c l n", c=NCH, l=2)[:, :, l, :]
                    dve.tensor_tensor(
                        vblk[:, l, b, :, 0:HD].rearrange("p (c h) f -> p c h f", c=NCH),
                        pv.rearrange("p c (h f) -> p c h f", h=NHC),
                        m.broadcast_to([P, NCH * NHC, HD]).rearrange("p (c h) f -> p c h f", c=NCH), ALU.mult)
                    dve.tensor_copy(vblk[:, l, b, :, HD:HD + 1], m).then_inc(s.vb_ready, 1)
                if b == 0:
                    add_gla = lambda b: dve.tensor_tensor(
                        X[:, b * TPB:(b + 1) * TPB, :].rearrange("p j d -> p (j d)"),
                        X[:, b * TPB:(b + 1) * TPB, :].rearrange("p j d -> p (j d)"), bank[2 * b][:, :], ALU.add)
                    dve.wait_ge(s.p_out, 1)
                    add_gla(0).then_inc(s.x_gla, 1)
                    dve.wait_ge(s.x_gla, 1)
                    ln_moments(LN_X0, 0, X)
            ln_norm(LN_X0, 0, X)
            dve.wait_ge(s.p_out, 2)
            add_gla(1).then_inc(s.x_gla, 1)

            def router(k, b):
                n = B * k + b
                tb = slice(b * TPB, (b + 1) * TPB)
                dve.wait_ge(s.r_mm, n + 1)
                lg = bank[5][:, 0:TPB * E0].rearrange("p (j e) -> p j e", j=TPB)
                if k == 0:
                    dve.tensor_tensor(logits[:, tb, :], lg, wk("br0").rearrange("p (one e) -> p one e", one=1).broadcast_to([P, TPB, E0]),
                                      ALU.add).then_inc(s.logit, 1)
                else:
                    dve.tensor_copy(logits[:, tb, :], lg).then_inc(s.logit, 1)
                dve.wait_ge(s.logit, n + 1)
                for j in range(TPB):
                    last = dve.max(top[:, b * TPB + j, :], logits[:, b * TPB + j, :])
                last.then_inc(s.top, 1)
                dve.wait_ge(s.top, n + 1)
                if k == 0:
                    dve.tensor_tensor(two[:, 0, tb], top[:, tb, 1], top[:, tb, 0], ALU.subtract).then_inc(s.diff, 1)
                else:
                    dve.tensor_tensor(coef[:, tb, :], logits[:, tb, :], top[:, tb, 0:1].broadcast_to([P, TPB, E1]),
                                      ALU.subtract).then_inc(s.b_shift, 1)
                for j in range(TPB):
                    last = dve.max_index(topi[:, b * TPB + j, :], top[:, b * TPB + j, :], logits[:, b * TPB + j, :])
                last.then_inc(s.topi, 1)
                dve.wait_ge(s.topi, n + 1)
                dve.tensor_copy(topf[:, tb, :], topi[:, tb, 0:2]).then_inc(s.topf, 1)
                dve.wait_ge(s.topf, n + 1)
                ex = wk("experts").rearrange("p (one e) -> p one e", one=1).broadcast_to([P, TPB, E0])
                for r in range(2):
                    last = dve.tensor_tensor(sel[:, r, tb, :], ex, topf[:, tb, r:r + 1].broadcast_to([P, TPB, E0]), ALU.is_equal)
                last.then_inc(s.eq1, 1)
                dve.wait_ge(s.eq1, n + 1)

            def softmax_two(b):
                tb = slice(b * TPB, (b + 1) * TPB)
                dve.wait_ge(s.ediff, b + 1)
                dve.tensor_scalar(two[:, 2, tb], two[:, 1, tb], 1.0, None, ALU.add).then_inc(s.one, 1)
                dve.wait_ge(s.one, b + 1)
                dve.reciprocal(two[:, 0, tb], two[:, 2, tb]).then_inc(s.w1, 1)
                dve.wait_ge(s.w1, b + 1)
                dve.tensor_tensor(two[:, 2, tb], two[:, 0, tb], two[:, 1, tb], ALU.mult).then_inc(s.w2, 1)
                dve.wait_ge(s.w2, b + 1)
                for r, w in ((0, 0), (1, 2)):
                    last = dve.tensor_tensor(sel[:, r, tb, :], sel[:, r, tb, :],
                                             two[:, w, tb].rearrange("p (j one) -> p j one", one=1).broadcast_to([P, TPB, E0]), ALU.mult)
                last.then_inc(s.coef_p, 1)
                dve.wait_ge(s.coef_p, b + 1)
                dve.tensor_tensor(coef[:, tb, :], sel[:, 0, tb, :], sel[:, 1, tb, :], ALU.add).then_inc(s.coef, 1)

            def chosen(b):
                tb = slice(b * TPB, (b + 1) * TPB)
                dve.tensor_tensor(selh[:, tb, :], sel[:, 0, tb, :], sel[:, 1, tb, :], ALU.add).then_inc(s.selh, 1)

            def softmax_all(b):
                tb = slice(b * TPB, (b + 1) * TPB)
                dve.wait_ge(s.b_exp, b + 1)
                dve.tensor_reduce(two[:, 0, tb], coef[:, tb, :], AX.X, ALU.add).then_inc(s.b_sum, 1)
                dve.wait_ge(s.b_sum, b + 1)
                dve.reciprocal(two[:, 1, tb], two[:, 0, tb]).then_inc(s.b_rec, 1)
                dve.wait_ge(s.b_rec, b + 1)
                dve.tensor_tensor(coef[:, tb, :], coef[:, tb, :], two[:, 1, tb].rearrange("p (j one) -> p j one", one=1).broadcast_to([P, TPB, E1]),
                                  ALU.mult).then_inc(s.b_prob, 1)
                dve.wait_ge(s.b_prob, b + 1)
                dve.wait_ge(s.pos, b + 1)
                dve.wait_ge(s.selh, b + 1)
                dve.scalar_tensor_tensor(out=slot[:, tb, :], in0=selh[:, tb, :], scalar=-BIG,
                                         in1=bank[5][:, 0:TPB * E1].rearrange("p (j e) -> p j e", j=TPB),
                                         op0=ALU.mult, op1=ALU.add).then_inc(s.slot, 1)
                dve.wait_ge(s.slot, b + 1)
                for j in range(b * TPB, (b + 1) * TPB):
                    dve.tensor_tensor(disp[:, j, :, :],
                                      wk("slots").rearrange("p (one c) -> p one c", one=1).broadcast_to([P, E1, CAP]),
                                      slot[:, j, :].rearrange("p (e one) -> p e one", one=1).broadcast_to([P, E1, CAP]),
                                      ALU.is_equal).then_inc(s.disp, 1)

            def attention(b, part):
                if part == 0:
                    dve.wait_ge(s.a_v, b + 1)
                    dve.tensor_tensor(av_sb[:, b * TPB:(b + 1) * TPB, :], bank[5][:, :].rearrange("p (j d) -> p j d", j=TPB),
                                      wk("abv").rearrange("p (one d) -> p one d", one=1).broadcast_to([P, TPB, D]),
                                      ALU.add).then_inc(s.av_ready, 1)
                elif part == 1:
                    for k, n in enumerate(A_COLS):
                        dve.wait_ge(s.a_raw, 3 * b + k + 1)
                        dve.tensor_reduce(amax[:, b, k:k + 1], expo[:, b, k, 0:n], AX.X, ALU.max).then_inc(s.a_pmax, 1)
                    dve.wait_ge(s.a_pmax, 3 * b + 3)
                    dve.tensor_reduce(amax[:, b, 3:4], amax[:, b, 0:3], AX.X, ALU.max).then_inc(s.a_max, 1)
                elif part == 2:
                    dve.wait_ge(s.a_exp, 3 * b + 3)
                    dve.tensor_reduce(asum[:, b, 3:4], asum[:, b, 0:3], AX.X, ALU.add).then_inc(s.a_sum, 1)
                else:
                    dve.wait_ge(s.a_gsum, b + 1)
                    dve.reciprocal(rtot[:, b:b + 1], gsum[:, b:b + 1]).then_inc(s.a_rtot, 1)
                    dve.wait_ge(s.a_rtot, b + 1)
                    dve.wait_ge(s.a_pv, b + 1)
                    xs = X[:, b * TPB:(b + 1) * TPB, :].rearrange("p j d -> p (j d)")
                    dve.scalar_tensor_tensor(out=xs, in0=bank[5][:, :], scalar=rtot[:, b:b + 1], in1=xs,
                                             op0=ALU.mult, op1=ALU.add).then_inc(s.x_att, 1)

            def cross(l):
                for i in range(NT + 2):
                    if i < NT:
                        g = l * NT + i
                        if g >= 2:
                            dve.wait_ge(s.pT, 3 * (g - 1))
                        for k, (n, h0) in enumerate(zip(HEADS_OF_BANK, HEAD_BASE)):
                            dve.wait_ge(s.score, 3 * g + k + 1)
                            sc = bank[k][:, 0:n * KEYS].rearrange("p (h k) -> p h k", h=n)
                            dve.tensor_reduce(rowmax[:, h0:h0 + n], sc, AX.X, ALU.max).then_inc(s.rmax, 1)
                            dve.wait_ge(s.rmax, 3 * g + k + 1)
                            dve.tensor_tensor(
                                probs[:, g % 2, h0 * KEYS:(h0 + n) * KEYS].rearrange("p (h k) -> p h k", h=n), sc,
                                rowmax[:, h0:h0 + n].rearrange("p (h one) -> p h one", one=1).broadcast_to([P, n, KEYS]),
                                ALU.subtract).then_inc(s.probs_ready, 1)
                    if 1 <= i <= NT:
                        g = l * NT + i - 1
                        dve.wait_ge(s.pv, g + 1)
                        pvv = bank[6][:, 0:H * (HD + 1)].rearrange("p (h f) -> p h f", h=H)
                        if g:
                            dve.wait_ge(s.heads_r, g)
                        dve.reciprocal(rsum[:, :], pvv[:, :, HD]).then_inc(s.rsum_r, 1)
                        dve.wait_ge(s.rsum_r, g + 1)
                        if g:
                            dve.wait_ge(s.hT, g)
                        dve.tensor_tensor(heads[:, :, :], pvv[:, :, 0:HD],
                                          rsum[:, :].rearrange("p (h one) -> p h one", one=1).broadcast_to([P, H, HD]),
                                          ALU.mult).then_inc(s.heads_r, 1)
                    if i >= 2:
                        g = l * NT + i - 2
                        dve.wait_ge(s.wo, g + 1)
                        dve.wait_ge(s.x_bias, B * l + (i - 2) // TPB + 1)
                        dve.tensor_tensor(X[:, i - 2, :], X[:, i - 2, :], bank[7][:, P:2 * P], ALU.add).then_inc(s.x_res, 1)
                    if l == 0:
                        if i == 0:
                            dve.wait_ge(s.x_gla, B)
                            ln_moments(LN_X0, 1, X)
                        if i == 1:
                            ln_norm(LN_X0, 1, X)
                        if i == 5:
                            dve.wait_ge(s.x_res, TPB)
                            ln_moments(LN_F0, 0, X)
                        if i == 6:
                            ln_norm(LN_F0, 0, X)
                        if i == 8:
                            router(0, 0)
                    else:
                        if i == 0:
                            attention(1, 0)
                        if i == 2:
                            attention(1, 1)
                        if i == 3:
                            attention(1, 2)
                            attention(1, 3)
                            dve.wait_ge(s.x_att, B)
                            ln(LN_X1, 1, X)
                        if i == 5:
                            dve.wait_ge(s.x_res, NT + TPB)
                            ln_moments(LN_F1, 0, X)
                        if i == 6:
                            ln_norm(LN_F1, 0, X)
                        if i == 8:
                            router(1, 0)
                            chosen(0)

            cross(0)
            softmax_two(0)
            dve.wait_ge(s.x_res, NT)
            ln(LN_F0, 1, X)
            dve.wait_ge(s.coef, 1)
            for i in range(len(UNITS) + 1):
                if i < len(UNITS):
                    for c in range(C0):
                        u = C0 * i + c
                        dve.wait_ge(s.act, u + 1)
                        if i >= 2:
                            dve.wait_ge(s.down, i - 1)
                        dve.tensor_tensor(hid[:, i % 2, c, :], bank[2 * (u % 2) + 1][:, :], gact[:, u % 2, :], ALU.mult).then_inc(s.hid, 1)
                if i >= 1:
                    b, e = UNITS[i - 1]
                    dve.wait_ge(s.down, i)
                    if i >= 2:
                        dve.wait_ge(s.x_ffn, i - 1)
                    for j in range(TPB):
                        t = b * TPB + j
                        last = dve.scalar_tensor_tensor(out=X[:, t, :], in0=bank[4][:, j * P:(j + 1) * P],
                                                        scalar=coef[:, t, e:e + 1], in1=X[:, t, :], op0=ALU.mult, op1=ALU.add)
                    last.then_inc(s.x_ffn, 1)
                if i == 2:
                    router(0, 1)
                if i == 3:
                    softmax_two(1)
                    dve.wait_ge(s.coef, B)
                if i == E0:
                    dve.wait_ge(s.x_ffn, E0)
                    ln_moments(LN_ATT, 0, X)
                    ln_norm(LN_ATT, 0, X)
                if i == E0 + 2:
                    attention(0, 0)
                if i == E0 + 4:
                    attention(0, 1)
                if i == E0 + 5:
                    attention(0, 2)
                    attention(0, 3)
                    dve.wait_ge(s.x_att, 1)
                    ln_moments(LN_X1, 0, X)
                if i == E0 + 5:
                    ln_norm(LN_X1, 0, X)
            dve.wait_ge(s.x_ffn, len(UNITS))
            ln(LN_ATT, 1, X)
            cross(1)
            dve.wait_ge(s.x_res, 2 * NT)
            ln_moments(LN_F1, 1, X)
            softmax_all(0)
            ln_norm(LN_F1, 1, X)
            router(1, 1)
            chosen(1)
            softmax_all(1)
            for e in range(E1 + 1):
                if e < E1:
                    for c in range(C1):
                        q = e * C1 + c
                        dve.wait_ge(s.h_mm, q // 2 + 1)
                        if e >= 2 and c == 0:
                            dve.wait_ge(s.y_mm, B * (e - 1))
                        last = dve.tensor_scalar(h1[:, e % 2, c, :], bank[2 + c // 2][:, (c % 2) * B * CAP:(c % 2 + 1) * B * CAP],
                                                 wk("b1", q, 1), 0.0, ALU.add, ALU.max)
                        if c % 2:
                            last.then_inc(s.h_ready, 1)
                if e >= 1:
                    for b in range(B):
                        n = B * (e - 1) + b
                        dve.wait_ge(s.y_mm, n + 1)
                        if e - 1 >= 2:
                            dve.wait_ge(s.comb, e - 2)
                        dve.tensor_tensor(y1[:, (e - 1) % 2, b, :], bank[4 + b][0:CAP, 0:D],
                                          wk("b2", (e - 1) * D, D)[0:CAP, :], ALU.add).then_inc(s.y_ready, 1)
            for b in range(B):
                dve.wait_ge(s.comb, E1 + b)
                xs = X[:, b * TPB:(b + 1) * TPB, :].rearrange("p j d -> p (j d)")
                dve.tensor_tensor(xs, xs, bank[6 + b][:, :], ALU.add).then_inc(s.final, 1)

        @block.tensor
        def _(pe):
            def mm(o, l, r, start=True, stop=True, **kw):
                return pe.matmul(o, lhsT=l, rhs=r, start=start, stop=stop, **kw)

            def ln(k, b, residuals=0):
                i = LN_AT[k, b]
                pe.wait_ge(s.normed, i + 1)
                if i:
                    pe.wait_ge(s.nT, i)
                if residuals:
                    pe.wait_ge(s.x_res, residuals)
                for j in range(TPB):
                    last = pe.transpose(bank[7][:, j * P:(j + 1) * P], N[:, b * TPB + j, :], ident)
                last.then_inc(s.turned, 1)

            def turned(k, b):
                pe.wait_ge(s.nT, LN_AT[k, b] + 1)

            pe.wait_ge(s.early_in, 16)
            ln(LN_X, 0)
            for b in range(B):
                turned(LN_X, b)
                if b:
                    pe.wait_ge(s.k_ready, b)
                mm(bank[1][:, :], ea("win", 2 * D, D), seq(nT, b)).then_inc(s.p_lg, 1)
                if b:
                    pe.wait_ge(s.q_ready, b)
                mm(bank[0][:, :], ea("win", D, D), seq(nT, b)).then_inc(s.p_q, 1)
                if b:
                    pe.wait_ge(s.g1_ready, b)
                mm(bank[2][:, :], ea("wg1"), seq(nT, b)).then_inc(s.p_g1, 1)
                if b == 0:
                    ln(LN_X, 1)
                if b:
                    pe.wait_ge(s.v_ready, b)
                for j in range(TPB):
                    last = mm(bank[3][:, j * P:(j + 1) * P], tile(nT, b * TPB + j), ea("win", 0, D))
                last.then_inc(s.p_v, 1)
                pe.wait_ge(s.g1_ready, b + 1)
                if b:
                    pe.wait_ge(s.gate_ready, b)
                for j in range(TPB):
                    last = mm(bank[4][:, j * P:(j + 1) * P], tile(g1T, b * TPB + j), ea("wg2"))
                last.then_inc(s.p_gate, 1)
            for lv in range(LEVELS):
                for b in range(B):
                    i = B * lv + b
                    if lv == 0:
                        pe.wait_ge(s.k_ready, b + 1)
                        pe.wait_ge(s.q_ready, b + 1)
                    else:
                        pe.wait_ge(s.qp_step, i - B + 1)
                        if lv >= 2:
                            pe.wait_ge(s.ks_step, i - 2 * B + 1)
                            pe.wait_ge(s.level_kept, i - 2 * B + 1)
                    if lv == 1 and b == 1:
                        pe.wait_ge(s.gate_ready, B)
                    for j in range(TPB):
                        t = b * TPB + j
                        last = mm(bank[LEVEL_BANK[lv % 2][b]][:, j * P:(j + 1) * P], tile(ks, t), tile(qp, t))
                    last.then_inc(s.level_mm, 1)
                both = work_sb[:, WORK["ctx0"][0]:WORK["ctx0"][0] + 6 * KEYS].rearrange("p (b n) -> p b n", b=B)
                if lv == 0:
                    pe.wait_ge(s.work_in, 16)
                    pe.wait_ge(s.g1_ready, B)
                    for l in range(2):
                        last = mm(bank[2][:, l * B * KEYS:(l + 1) * B * KEYS].rearrange("p (b k) -> p b k", b=B), wk(f"wk{l}"), both[:, :, 0:KEYS])
                    last.then_inc(s.kT_mm, 1)
                if 1 <= lv <= 2:
                    b = lv - 1
                    pe.wait_ge(s.v_ready, B)
                    pe.wait_ge(s.k_ready, B)
                    wv = work_sb[:, WORK["wv0"][0]:WORK["wv0"][0] + 2 * D].rearrange("p (l d) -> p l d", l=2)
                    for c in range(NCH):
                        n = 2 * NHC * HD
                        last = mm(bank[VREP_BANK[b]][:, c * n:(c + 1) * n].rearrange("p (l f) -> p l f", l=2),
                                  both[:, b, P * c % KEYS:P * c % KEYS + P], wv[:, :, HLO[c] * HD:(HLO[c] + NHC) * HD])
                    last.then_inc(s.vrep, 1)
            pe.wait_ge(s.q_ready, B)
            pe.wait_ge(s.kT_ready, 1)
            for b in range(B):
                pe.wait_ge(s.ks_step, B * (LEVELS - 2) + b + 1)
                for c in range(3):
                    last = pe.transpose(bank[2 * b][:, c * P:(c + 1) * P], tile(ks, b * TPB + c), ident)
                last.then_inc(s.khat_T, 1)
            for b in range(B):
                pe.wait_ge(s.khat_ready, b + 1)
                for c in range(3):
                    mm(bank[2 * b][:, c * P:(c + 1) * P], tile(khat, b * TPB + c), tile(v, b * TPB + c)).then_inc(s.upd, 1)
            for b in range(B):
                pe.wait_ge(s.level_kept, B * (LEVELS - 1) + b + 1)
                pe.wait_ge(s.qp_step, B * (LEVELS - 1) + b + 1)
                for j in range(TPB):
                    t = b * TPB + j
                    o = bank[5 + b][:, j * P:(j + 1) * P]
                    last = mm(o, tile(A, t), tile(v, t), stop=(j == 0))
                    if j:
                        pe.wait_ge(s.state_ready, B * (j - 1) + b + 1)
                        last = mm(o, tile(qp, t), state[:, b, j - 1, :], start=False)
                last.then_inc(s.o_ready, 1)
            pe.wait_ge(s.state_ready, 3 * B)
            for b in range(B):
                ln(LN_GLA, b)
                turned(LN_GLA, b)
                for j in range(TPB):
                    last = mm(bank[2 * b][:, j * P:(j + 1) * P], tile(nT, b * TPB + j), ea("wout"))
                last.then_inc(s.p_out, 1)

            def query(l, b):
                turned(LN_X1 if l else LN_X0, b)
                mm(bank[5][:, :], wk(f"wq{l}"), seq(nT, b)).then_inc(s.q_mm, 1)

            def router(l, b):
                turned(LN_F1 if l else LN_F0, b)
                for j in range(TPB):
                    last = mm(bank[5][:, j * E0:(j + 1) * E0], tile(nT, b * TPB + j), wk(f"wr{l}"))
                last.then_inc(s.r_mm, 1)

            def attention(b, part):
                if part == 0:
                    turned(LN_ATT, b)
                    mm(bank[5][:, :], wk("aq"), seq(nT, b)).then_inc(s.a_qk, 1)
                elif part == 1:
                    pe.wait_ge(s.a_q, b + 1)
                    mm(bank[5][:, :], wk("ak"), seq(nT, b)).then_inc(s.a_qk, 1)
                elif part == 2:
                    pe.wait_ge(s.a_k, b + 1)
                    for j in range(TPB):
                        last = mm(bank[5][:, j * P:(j + 1) * P], tile(nT, b * TPB + j), wk("av"))
                    last.then_inc(s.a_v, 1)
                elif part < 6:
                    k = part - 3
                    if k == 0:
                        pe.wait_ge(s.av_ready, b + 1)
                    else:
                        pe.wait_ge(s.a_raw, 3 * b + k)
                    for kt in A_TILES[k]:
                        at, n, q0 = A_PLACE[kt][1], S - kt * P, b * S + kt * P
                        o = bank[5][:, at:at + n]
                        mm(o[:, 0:P], tile(akT, b * TPB + kt), aqT[:, q0:q0 + P], stop=False)
                        last = mm(o[:, 0:P], hf("ident"), hf("future"), start=False)
                        if n > P:
                            last = mm(o[:, P:n], tile(akT, b * TPB + kt), aqT[:, q0 + P:q0 + n])
                    last.then_inc(s.a_score, 1)
                else:
                    pe.wait_ge(s.a_exp, 3 * b + 3)
                    for j in range(TPB):
                        for kt in range(j + 1):
                            k, at = A_PLACE[kt]
                            c = at + (j - kt) * P
                            last = mm(bank[5][:, j * P:(j + 1) * P], expo[:, b, k, c:c + P], av_sb[:, b * TPB + kt, :],
                                      start=(kt == 0), stop=(kt == j))
                    last.then_inc(s.a_pv, 1)

            def cross(l):
                for i in range(NT + 2):
                    if i < NT:
                        g, b = l * NT + i, i // TPB
                        if i % TPB == 0:
                            pe.wait_ge(s.qT_ready, 2 * l + b + 1)
                            pe.wait_ge(s.kblk_ready, 2 * l + b + 1)
                        for k, (n, h0) in enumerate(zip(HEADS_OF_BANK, HEAD_BASE)):
                            if g:
                                pe.wait_ge(s.probs_ready, 3 * (g - 1) + k + 1)
                            o = bank[k][:, 0:n * KEYS]
                            cols = slice(h0 * KEYS, (h0 + n) * KEYS)
                            mm(o, tile(qT, i), kblk[:, l, b, cols], stop=False)
                            mT = tile(maskT0, i) if l == 0 else maskT1[:, b, :]
                            mm(o, mT, hf("maskout", KEYS)[:, cols], start=False).then_inc(s.score, 1)
                    done = l * NT + max(i - 2, 0)
                    if l == 0:
                        if i == 2:
                            ln(LN_X0, 1, done)
                        if i == 3:
                            query(0, 1)
                        if i == 7:
                            ln(LN_F0, 0, done)
                        if i == 8:
                            router(0, 0)
                    else:
                        if i == 0:
                            ln(LN_ATT, 1)
                            for part in range(3):
                                attention(1, part)
                        if i == 1:
                            attention(1, 3)
                        if i == 2:
                            attention(1, 5)
                        if i == 3:
                            attention(1, 6)
                        if i == 7:
                            ln(LN_F1, 0, done)
                        if i == 8:
                            router(1, 0)
                    for k in range(3):
                        if k == 2 and i >= 2:
                            g = l * NT + i - 2
                            pe.wait_ge(s.heads_r, g + 1)
                            if g:
                                pe.wait_ge(s.x_res, g)
                            pe.wait_ge(s.nT, LN_BEFORE[l][i])
                            pe.transpose(bank[7][:, 0:P], heads[:, :, :].rearrange("p h f -> p (h f)"), ident).then_inc(s.hT, 1)
                        if 1 <= i <= NT:
                            g, b = l * NT + i - 1, (i - 1) // TPB
                            if k == 0:
                                pe.wait_ge(s.exp_ready, g + 1)
                            n = 3 * g + k
                            if n >= 2:
                                pe.wait_ge(s.pT_ready, n - 1)
                            for c in range(4 * k, min(4 * k + 4, NCH)):
                                rows = P if c < NCH - 1 else LASTR
                                last = pe.transpose(bank[3 + n % 2][0:rows, (c % 4) * P:(c % 4 + 1) * P],
                                                    probs[:, g % 2, c * P:c * P + rows], ident)
                            last.then_inc(s.pT, 1)
                    if 1 <= i <= NT:
                        g, b = l * NT + i - 1, (i - 1) // TPB
                        if g:
                            pe.wait_ge(s.heads_r, g)
                        for c in range(NCH):
                            if c % 4 == 0:
                                pe.wait_ge(s.pT_ready, 3 * g + c // 4 + 1)
                            rows = P if c < NCH - 1 else LASTR
                            lo = HLO[c] * (HD + 1)
                            last = mm(bank[6][:, lo:lo + NHC * (HD + 1)], ptT[0:rows, c, :],
                                      vblk[0:rows, l, b, c * NHC:(c + 1) * NHC, :].rearrange("p h f -> p (h f)"),
                                      start=(c == 0), stop=(c == NCH - 1), skip_group_check=True)
                        last.then_inc(s.pv, 1)
                    if i >= 2:
                        g = l * NT + i - 2
                        pe.wait_ge(s.hT_ready, g + 1)
                        mm(bank[7][:, P:2 * P], headsT[:, :], wk(f"wo{l}")).then_inc(s.wo, 1)
                    if l == 1:
                        if i == 1:
                            attention(1, 4)
                        if i == 3:
                            ln(LN_X1, 1, l * NT + i - 1)
                            query(1, 1)
                        if i == 8:
                            positions(0)

            def positions(b):
                pe.wait_ge(s.selh, b + 1)
                for j in range(TPB):
                    for i in range(j + 1):
                        last = mm(bank[5][:, j * E1:(j + 1) * E1], hf("below") if i == j else hf("ones"), selh[:, b * TPB + i, :],
                                  start=(i == 0), stop=(i == j))
                last.then_inc(s.pos, 1)

            pe.wait_ge(s.x_gla, 1)
            ln(LN_X0, 0)
            query(0, 0)
            pe.wait_ge(s.x_gla, B)
            pe.wait_ge(s.half_in, 16)
            pe.wait_ge(s.maskT, 3)
            pe.wait_ge(s.vb_ready, 2 * B)
            cross(0)
            pe.wait_ge(s.ffn0_in, 16)
            for i in range(len(UNITS) + 1):
                if i < len(UNITS):
                    b, e = UNITS[i]
                    for c in range(C0):
                        u = C0 * i + c
                        if u >= 2:
                            pe.wait_ge(s.hid, u - 1)
                        for m in range(2):
                            last = mm(bank[2 * (u % 2) + m][:, :], ffn0_sb[:, e, m, c * P:(c + 1) * P], seq(nT, b))
                        last.then_inc(s.gu, 1)
                        if (i, c) == (1, 1):
                            ln(LN_F0, 1, NT)
                        if (i, c) == (2, 1):
                            pe.wait_ge(s.logit, 1)
                            router(0, 1)
                        if (i, c) == (E0 + 1, 1):
                            ln(LN_ATT, 0)
                            pe.wait_ge(s.logit, 2)
                        if (i, c) == (E0 + 2, 0):
                            attention(0, 0)
                        if (i, c) == (E0 + 2, 1):
                            attention(0, 1)
                        if (i, c) == (E0 + 3, 0):
                            attention(0, 3)
                        if (i, c) == (E0 + 3, 1):
                            attention(0, 4)
                        if (i, c) == (E0 + 4, 0):
                            attention(0, 5)
                        if (i, c) == (E0 + 5, 1):
                            attention(0, 6)
                        if (i, c) == (E0 + 6, 1):
                            ln(LN_X1, 0)
                        if (i, c) == (E0 + 7, 1):
                            query(1, 0)
                if i >= 1:
                    b, e = UNITS[i - 1]
                    pe.wait_ge(s.hid, C0 * i)
                    if i >= 2:
                        pe.wait_ge(s.x_ffn, i - 1)
                    for j in range(TPB):
                        for c in range(C0):
                            last = mm(bank[4][:, j * P:(j + 1) * P], hid[:, (i - 1) % 2, c, j * P:(j + 1) * P],
                                      ffn0_sb[:, e, 2, c * P:(c + 1) * P], start=(c == 0), stop=(c == C0 - 1))
                    last.then_inc(s.down, 1)
                if i == E0 + 2:
                    attention(0, 2)
            cross(1)
            ln(LN_F1, 1, 2 * NT)

            def dispatch(b):
                pe.wait_ge(s.disp, (b + 1) * TPB)
                for half_ in range(2):
                    if b:
                        pe.wait_ge(s.xd_ready, half_ + 1)
                    for j in range(TPB):
                        t = b * TPB + j
                        last = mm(bank[half_][:, 0:4 * CAP], N[:, t, :],
                                  disp[:, t, 4 * half_:4 * half_ + 4, :].rearrange("p e c -> p (e c)"), start=(j == 0), stop=(j == TPB - 1))
                    last.then_inc(s.xd, 1)

            def turn_weights(b):
                pe.wait_ge(s.wdisp, (b + 1) * TPB)
                for e in range(E1):
                    n = b * E1 + e
                    if n >= 2:
                        pe.wait_ge(s.dpT_ready, n - 1)
                    for j in range(TPB):
                        last = pe.transpose(bank[2 + e % 2][0:CAP, j * P:(j + 1) * P], wdisp[:, b * TPB + j, e, :], ident)
                    last.then_inc(s.dpT, 1)

            pe.wait_ge(s.slot, 1)
            router(1, 1)
            dispatch(0)
            pe.wait_ge(s.logit, 4)
            positions(1)
            turn_weights(0)
            dispatch(1)
            turn_weights(1)
            pe.wait_ge(s.dpT_ready, B * E1)
            pe.wait_ge(s.xd_ready, 2 * B)
            pe.wait_ge(s.ffn1_in, 16)
            pe.wait_ge(s.slot, 2)
            for e in range(E1 + 2):
                if e < E1:
                    for c in range(C1):
                        q = e * C1 + c
                        if e and c % 2 == 0:
                            pe.wait_ge(s.h_ready, q // 2 - 1)
                        last = mm(bank[2 + c // 2][:, (c % 2) * B * CAP:(c % 2 + 1) * B * CAP], ffn1_sb[:, e, 0, c * P:(c + 1) * P],
                                  xd[:, e, :, :].rearrange("p b c -> p (b c)"))
                        if c % 2:
                            last.then_inc(s.h_mm, 1)
                if 1 <= e <= E1:
                    pe.wait_ge(s.h_ready, 2 * e)
                    for b in range(B):
                        if e >= 2:
                            pe.wait_ge(s.y_ready, B * (e - 2) + b + 1)
                        for c in range(C1):
                            last = mm(bank[4 + b][0:CAP, 0:D], h1[:, (e - 1) % 2, c, b * CAP:(b + 1) * CAP],
                                      ffn1_sb[:, e - 1, 1, c * P:(c + 1) * P], start=(c == 0), stop=(c == C1 - 1))
                        last.then_inc(s.y_mm, 1)
                if e >= 2:
                    for b in range(B):
                        pe.wait_ge(s.y_ready, B * (e - 2) + b + 1)
                        for j in range(TPB):
                            last = mm(bank[6 + b][:, j * P:(j + 1) * P], dpT[:, b, e - 2, j * P:(j + 1) * P], y1[:, (e - 2) % 2, b, :],
                                      start=(e == 2 and j == 0), stop=(e == E1 + 1), skip_group_check=True)
                        if b == B - 1 or e == E1 + 1:
                            last.then_inc(s.comb, 1)


def constants():
    r = np.arange(P)
    levels = np.zeros((P, LEVELS, P), np.float32)
    levels[r, 0, r] = 1.0
    for lv in range(1, LEVELS):
        seg = 1 << (lv - 1)
        key, query = r[:, None] // seg, r[None, :] // seg
        levels[:, lv, :] = (query == key + 1) & (key % 2 == 0)
    head = (np.arange(P)[:, None] // HD == np.arange(H)[None, :]).astype(np.float32)
    rows = np.zeros((P, NCH, NHC), np.float32)
    for c in range(NCH):
        for k in range(NHC):
            rows[:, c, k] = (P * c + r) // KEYS == HLO[c] + k
    both = lambda n, base=0.0: np.broadcast_to(np.arange(n, dtype=np.float32) + np.float32(base), (P, n))
    half = np.zeros((P, HALF_N), np.float32)
    def put(name, a):
        at, n = HALF[name]
        half[:a.shape[0], at:at + n] = a
    put("ident", np.eye(P))
    put("below", r[:, None] < r[None, :])
    put("ones", np.ones((P, P)))
    put("future", np.where(r[None, :] < r[:, None], -1e30, 0.0))
    put("maskout", np.tile(-1e18 * np.eye(KEYS), (1, H)))
    return levels.reshape(P, -1), head, rows.reshape(P, -1), both, (half.view(np.uint32) >> 16).astype(np.uint16)


def kernel(**a):
    import concourse.bacc as bacc
    from concourse.bass_utils import run_bass_kernel_spmd

    a = {k: np.asarray(v) for k, v in a.items()}
    levels, head, rows, both, half = constants()
    row = lambda v: np.broadcast_to(v.reshape(1, -1), (P, v.size))
    col = lambda v: v.reshape(P, 1)

    def pack(index, total, values):
        out = np.zeros((P, total), np.float32)
        for name, (at, n) in index.items():
            out[:, at:at + n] = values[name]
        return out

    early = pack(EARLY, EARLY_N, {
        "win": a["L0_attn_W_in"].T, "wg1": a["L0_attn_W_g1"].T, "wg2": a["L0_attn_W_g2"].T,
        "wout": a["L0_attn_W_out"].T, "lnw": col(a["L0_attn_ln_w"]), "ident": np.eye(P, dtype=np.float32)})
    ctxT = [np.tile(a["ctx_1024"][b].T, (1, 3)) for b in range(B)]
    work = pack(WORK, WORK_N, {
        "wv0": a["L0_xattn_Wv"], "wv1": a["L1_xattn_Wv"].T, "wk0": a["L0_xattn_Wk"], "wk1": a["L1_xattn_Wk"].T,
        "ctx0": ctxT[0], "ctx1": ctxT[1],
        "wq0": a["L0_xattn_Wq"], "wo0": a["L0_xattn_Wo"], "wq1": a["L1_xattn_Wq"].T, "wo1": a["L1_xattn_Wo"].T,
        "aq": a["L1_attn_Wq"], "ak": a["L1_attn_Wk"], "av": a["L1_attn_Wv"],
        "wr0": a["L0_ffn_Wr"], "wr1": a["L1_ffn_Wr"],
        "bq0": col(a["L0_xattn_bq"]), "bk0": col(a["L0_xattn_bk"]), "bv0": col(a["L0_xattn_bv"]),
        "bq1": col(a["L1_xattn_bq"]), "bk1": col(a["L1_xattn_bk"]), "bv1": col(a["L1_xattn_bv"]),
        "abq": col(a["L1_attn_bq"]), "abk": col(a["L1_attn_bk"]),
        "b1": a["L1_ffn_b1"].reshape(E1 * C1, P).T,
        "bo0": row(a["L0_xattn_bo"]), "bo1": row(a["L1_xattn_bo"]), "abv": row(a["L1_attn_bv"]),
        "br0": row(a["L0_ffn_br"]), "b2": row(a["L1_ffn_b2"]),
        "headmask": head, "rowmask": rows, "slots": both(CAP, -BIG), "experts": both(E0)})
    chunks = lambda w, n: w.reshape(w.shape[0], n, P, D).transpose(2, 0, 1, 3).reshape(P, w.shape[0], n * D)
    ffn0 = np.stack([a["L0_ffn_W1"].transpose(1, 0, 2), a["L0_ffn_W3"].transpose(1, 0, 2), chunks(a["L0_ffn_W2"], C0)], 2)
    ffn1 = np.stack([a["L1_ffn_W1"].transpose(1, 0, 2), chunks(a["L1_ffn_W2"], C1)], 2)
    padmask = a["mask_BxSxS2_bk1"].transpose(2, 0, 1).reshape(KEYS, B * S).copy().view(np.uint32)
    key = a["mask_Bx1x1xS2_if1"].reshape(B, KEYS)
    keyrows = key[:, np.arange(NCH * P) % KEYS].reshape(B, NCH, P).transpose(2, 0, 1)

    arrays = {
        "x": a["x"], "early": early, "glamask": levels, "work": work, "half": half, "padmask": padmask,
        "keymask": key.T, "keyrows": keyrows, "ffn0": ffn0.reshape(P, -1), "ffn1": ffn1.reshape(P, -1)}
    arrays = {k: np.ascontiguousarray(v) for k, v in arrays.items()}
    nc = bacc.Bacc("TRN2", target_bir_lowering=False, num_devices=1)
    args = [nc.dram_tensor(f"in_{n}", v.shape, mybir.dt.from_np(v.dtype), kind="ExternalInput").ap() for n, v in arrays.items()]
    out = nc.dram_tensor("out", (B, S, D), F32, kind="ExternalOutput").ap()
    program(nc, *args, out)
    r = run_bass_kernel_spmd(nc, [{f"in_{n}": v for n, v in arrays.items()}], core_ids=[0])
    return r.results[0]["out"]
```

```python
from collections import namedtuple
from contextlib import ExitStack

import numpy as np

import concourse.bass as bass
from concourse import mybir

ALU = mybir.AluOpType
ACT = mybir.ActivationFunctionType
AX = mybir.AxisListType
F32 = mybir.dt.float32
F32R = mybir.dt.float32r
BF16 = mybir.dt.bfloat16
U32 = mybir.dt.uint32
I32 = mybir.dt.int32
U8 = mybir.dt.uint8

B, S, D = 2, 512, 128
P = 128
TPB = S // P
NT = B * TPB
KEYS, H, HD = 77, 16, 8
HK = H * KEYS
NCH = -(-HK // P)
LASTR = HK - (NCH - 1) * P
NHC = 3
E0, I0 = 8, 256
C0 = I0 // P
E1, I1 = 8, 512
C1 = I1 // P
CAP = int(S / E1 * 1.25)
LEVELS = 8
EPS = 1e-5
BIG = 1024.0
HEADS_OF_BANK = (5, 5, 6)
HEAD_BASE = (0, 5, 10)
PK = KEYS + 1
GH = 5
GROUPS = [(g * GH * HD, min(GH * HD, D - g * GH * HD)) for g in range(-(-H // GH))]
GROUP_COLS = [3 * n + P for _, n in GROUPS]
Q_WINDOWS, K_WINDOWS = (2, 0), (1, 3)
STACK_BANKS = {(0, 0): (3, 4, 6, 1), (0, 1): (5, 3, 4, 6), (1, 0): (3, 2, 1, 0), (1, 1): (5, 3, 4, 6)}
BY_DVE = (1, 3)
HLO = [min(P * c // KEYS, H - NHC) for c in range(NCH)]
XSCALE = float(HD) ** -0.5
ASCALE = float(D) ** -0.5


LN_X, LN_GLA, LN_X0, LN_F0, LN_ATT, LN_X1, LN_F1 = range(7)
LN_AT = {kb: n for n, kb in enumerate([
    (LN_X, 0), (LN_X, 1), (LN_GLA, 0), (LN_GLA, 1), (LN_X0, 0), (LN_X0, 1), (LN_F0, 0), (LN_F0, 1),
    (LN_ATT, 0), (LN_X1, 0), (LN_ATT, 1), (LN_X1, 1), (LN_F1, 0), (LN_F1, 1)])}
def norm_before(k, b):
    return max([n + 1 for (_, bb), n in LN_AT.items() if bb == b and n < LN_AT[k, b]], default=0)


LN_BEFORE = [[LN_AT[LN_X0, 1] + 1 + (i > 6) for i in range(NT + 2)],
             [LN_AT[LN_ATT, 1] + 1 + (i > 2) + (i > 6) for i in range(NT + 2)]]
UNITS = [(b, e) for b in range(B) for e in range(E0)]
LEVEL_BANK = ((5, 6), (7, 4))
VREP_BANK = (3, 1)
A_TILES = ((0,), (1, 3), (2,))
A_COLS = (S, S, 2 * P)
A_PLACE = {0: (0, 0), 1: (1, 0), 3: (1, 3 * P), 2: (2, 0)}
A_BANK = ((5, 5, 5, 5, 5, 5, 5), (5, 3, 4, 5, 6, 3, 5))


def columns(*parts):
    at, out = 0, {}
    for name, n in parts:
        out[name] = (at, n)
        at += n
    return out, at


EARLY, EARLY_N = columns(("win", 3 * D), ("wg1", D), ("wg2", D), ("wout", D), ("lnw", 1), ("ident", P))
GLA_MASK_N = LEVELS * P
WORK, WORK_N = columns(
    ("wv0", D), ("wv1", D), ("wk0", D), ("wk1", D), ("ctx0", 3 * KEYS), ("ctx1", 3 * KEYS),
    ("wq0", D), ("wo0", D), ("wq1", D), ("wo1", D), ("aq", D), ("ak", D), ("av", D),
    ("wr0", E0), ("wr1", E1),
    ("bq0", 1), ("bk0", 1), ("bv0", 1), ("bq1", 1), ("bk1", 1), ("bv1", 1), ("abq", 1), ("abk", 1),
    ("b1", E1 * C1),
    ("bo0", D), ("bo1", D), ("abv", D), ("br0", E0), ("b2", E1 * D),
    ("stackmask", GH), ("rowmask", NCH * NHC), ("slots", CAP), ("experts", E0),
)
HALF, HALF_N = columns(("ident", P), ("below", P), ("ones", P), ("future", P), ("maskout", H * PK))
COPIES = 3
FILL_START = 7
FILL_GLA = (10, 3, 4, 3, 4)
FILL_ROUTING = (12, 8, 4, 6)
WX = 1



def program(nc, x, early, glamask, work, half, padmask, keymask, keyrows, selection, ffn0, ffn1, out):
    ctx = ExitStack()
    with ctx:
        def sb(name, shape, dt=F32):
            return ctx.enter_context(nc.sbuf_tensor(name, shape, dt))

        X = sb("X", [P, NT, D])
        N = sb("N", [P, NT, D])
        nT = sb("nT", [P, NT * P])
        early_sb = sb("early_sb", [P, EARLY_N])
        work_sb = sb("work_sb", [P, WORK_N])
        half_sb = sb("half_sb", [P, HALF_N], mybir.dt.uint16)
        stats2 = sb("stats", [P, 2, TPB, 6])
        moments2 = sb("moments", [P, 2, TPB, 2])
        logvar2 = sb("logvar", [P, 2, TPB])
        rstd2 = sb("rstd", [P, 2, TPB])
        tiny = sb("tiny", [P, 1])

        def wk(name, lo=0, n=None):
            at, size = WORK[name]
            return work_sb[:, at + lo:at + (size if n is None else lo + n)]

        def ea(name, lo=0, n=None):
            at, size = EARLY[name]
            return early_sb[:, at + lo:at + (size if n is None else lo + n)]

        def hf(name, rows=P):
            at, size = HALF[name]
            return half_sb[0:rows, at:at + size].bitcast(BF16)

        def arena(name, cols):
            offset = -(-nc.sbuf_base // 32) * 32
            return sb(name, [P, cols]), offset

        region_a, offset_a = arena("region_a", 11 * NT * P + 3 * B * D)
        gla = [region_a[:, i * NT * P:(i + 1) * NT * P] for i in range(11)]
        decay, qp, ks, sig, A, v, gate, khat, g1T, og, glam = gla
        state = region_a[:, 11 * NT * P:].rearrange("p (b c e) -> p b c e", b=B, c=3)
        dpT = region_a[0:CAP, 0:B * E1 * S].rearrange("p (b e t) -> p b e t", b=B, e=E1)
        region_b, offset_b = arena("region_b", E0 * 3 * I0)
        ffn0_sb = region_b[:, :].rearrange("p (e m i) -> p e m i", e=E0, m=3)
        disp = nc.alloc_sbuf_tensor_at("disp", [P, NT, E1, CAP], F32R, offset=offset_b)
        region_e, offset_e = arena("region_e", E1 * 2 * I1)
        ffn1_sb = region_e[:, :].rearrange("p (e m i) -> p e m i", e=E1, m=2)
        whi = nc.alloc_sbuf_tensor_at("whi", [P, E0, 2 * I0], F32R, offset=offset_e)
        wlo = nc.alloc_sbuf_tensor_at("wlo", [P, E0, 2 * I0], F32R, offset=offset_e + 4 * E0 * 2 * I0)
        region_c, offset_c = arena("region_c", 4 * H * PK + 2 * HK)
        kblk = nc.alloc_sbuf_tensor_at("kblk", [P, 2, B, H * PK], F32R, offset=offset_c)
        probs = region_c[:, 4 * H * PK:].rearrange("p (i n) -> p i n", i=2)
        wdisp = region_c[:, 0:NT * E1 * CAP].rearrange("p (j e c) -> p j e c", j=NT, e=E1)

        totals, offset_t = arena("totals", 2 * NT * P)
        xhi = nc.alloc_sbuf_tensor_at("xhi", [P, B, S], F32R, offset=offset_t)
        xlo = nc.alloc_sbuf_tensor_at("xlo", [P, B, S], F32R, offset=offset_t + 4 * B * S)
        vblk = sb("vblk", [P, 2, B, NCH * NHC, HD + 1])
        rowm1 = sb("rowm1", [P, B, NCH * NHC])
        keep1 = sb("keep1", [P, B, NCH])
        keyrows_sb = sb("keyrows_sb", [P, B, NCH], I32)
        keymask_sb = sb("keymask_sb", [1, B * PK], I32)
        padmask_sb = sb("padmask_sb", [KEYS, NT * P // 4], U32)
        maskT0 = sb("maskT0", [KEYS, NT * P], BF16)
        qhi = sb("qhi", [P, S], F32R)
        qlo = sb("qlo", [P, S], F32R)
        ptT = sb("ptT", [P, NCH, P])
        nv = NCH * 2 * NHC * HD
        vrep_sb = ptT[:, :, :].rearrange("p c q -> p (c q)")[:, 0:B * nv].rearrange("p (b n) -> p b n", b=B)
        rowmax = sb("rowmax", [P, H])
        rsum = sb("rsum", [P, H])
        heads = sb("heads", [P, H, HD])
        headsT = sb("headsT", [P, P])
        logits = sb("logits", [P, NT, E0])
        top = sb("top", [P, NT, 8])
        topi = sb("topi", [P, NT, 8], U32)
        topf = sb("topf", [P, NT, 2])
        two = sb("two", [P, 3, NT])
        sel = sb("sel", [P, 2, NT, E0])
        coef = sb("coef", [P, NT, E0])
        selh = sb("selh", [P, NT, E1], BF16)
        slot = sb("slot", [P, NT, E1])
        late = 8 * NT * P
        gact = region_a[:, late:late + 2 * S].rearrange("p (i t) -> p i t", i=2)
        hid = region_a[:, late + 2 * S:late + 2 * S + 2 * C0 * S].rearrange("p (i c t) -> p i c t", i=2, c=C0)
        akT = region_a[:, 0:NT * P]
        aqT = region_a[:, 2 * NT * P:3 * NT * P]
        av_sb = region_a[:, NT * P:2 * NT * P].rearrange("p (j d) -> p j d", j=NT)
        expo = region_a[:, 3 * NT * P:3 * NT * P + B * 3 * S].rearrange("p (b k t) -> p b k t", b=B, k=3)
        amax = sb("amax", [P, B, 4])
        gmax = sb("gmax", [P, B])
        nmax = sb("nmax", [P, B])
        asum = sb("asum", [P, B, 4])
        gsum = sb("gsum", [P, B])
        rtot = sb("rtot", [P, B])
        nx, nh = E1 * B * CAP, 2 * C1 * B * CAP
        region_d, offset_d = arena("region_d", nx + nh + 2 * B * D)
        xd = region_d[:, 0:nx].rearrange("p (e b c) -> p e b c", e=E1, b=B)
        h1 = region_d[:, nx:nx + nh].rearrange("p (i c n) -> p i c n", i=2, c=C1)
        y1 = region_d[0:CAP, nx + nh:].rearrange("p (i b d) -> p i b d", i=2, b=B)
        nk = 2 * B * PK
        ns = sum(GROUP_COLS)
        kstack = nc.alloc_sbuf_tensor_at("kstack", [P, len(GROUPS), nk], F32R, offset=offset_d)
        pick = nc.alloc_sbuf_tensor_at("pick", [P, ns], F32R, offset=offset_d + 16 * nk)
        maskrow = nc.alloc_sbuf_tensor_at("maskrow", [1, B * PK], F32R, offset=offset_d + 16 * nk + 4 * ns)
        qstack = [nc.alloc_sbuf_tensor_at(f"qstack{b}", [P, len(GROUPS), S], F32R,
                                          offset=offset_a + 4 * (6 * NT * P + b * len(GROUPS) * S)) for b in range(B)]

        bank = [ctx.enter_context(nc.psum_tensor(f"bank{i}", [P, 512], F32)) for i in range(8)]

        names = """early_in glam_in work_in half_in masks_in ffn0_in ffn1_in out_done
        x_in0 x_in1 stats moments logvar rstd normed turned nT
        p_lg p_q p_g1 p_v p_gate f_ready k_ready sigq q_ready g1_ready v_ready gate_ready
        A_zero level_mm level_kept qp_step ks_step tot_step khat_T khat_ready upd state_ready
        o_ready og_ready x_gla p_out
        kT_mm kT_ready vrep vr_kept vb_ready kblk_ready setup pick_in k_row maskrow ones_row rowm maskT
        k_hi k_lo k_pick k_stack q_mm q_hi q_lo q_pick q_stack_act q_stack_dve score score_free rmax probs_ready exp_ready pT pT_ready pv heads_r rsum_r hT hT_ready
        wo x_bias x_res
        r_mm logit top topi topf diff ediff one w1 w2 eq1 coef_p coef
        w_hi w_lo x_hi x_lo gu act hid down x_ffn act_free
        a_q a_k a_qk a_v av_ready a_score a_raw a_pmax a_max a_gmax a_nmax a_exp a_sum a_gsum a_rtot a_pv x_att
        b_shift b_exp b_sum b_rec b_prob selp selh pos slot n_hi n_lo disp wdisp xd xd_ready dpT dpT_ready
        h_mm h_ready y_mm y_ready comb final""".split()
        s = namedtuple("Signals", names)(*[ctx.enter_context(nc.semaphore(n)) for n in names])
        block = ctx.enter_context(nc.Block())

        tile = lambda t, j: t[:, j * P:(j + 1) * P]
        seq = lambda t, b: t[:, b * S:(b + 1) * S]
        ident = ea("ident")

        def total(level, b):
            if level == 0:
                return seq(decay, b)
            at = sum(NT * P >> i for i in range(1, level))
            n = S >> level
            return totals[:, at + b * n:at + (b + 1) * n]

        def window(g, w):
            f0, n = GROUPS[g]
            at = sum(GROUP_COLS[:g]) + w * n
            return pick[:, at:at + P]

        @block.sync
        def _(sp):
            sp.dma_start(X[:, 0:TPB, :], x[0].rearrange("(j p) d -> p j d", p=P)).then_inc(s.x_in0, 16)
            sp.dma_start(early_sb[:, :], early).then_inc(s.early_in, 16)
            sp.dma_start(X[:, TPB:NT, :], x[1].rearrange("(j p) d -> p j d", p=P)).then_inc(s.x_in1, 16)
            sp.dma_start(glam[:, 0:GLA_MASK_N], glamask).then_inc(s.glam_in, 16)
            sp.dma_start(work_sb[:, :], work).then_inc(s.work_in, 16)
            sp.wait_ge(s.work_in, 16)
            sp.dma_start(ffn0_sb[:, :, :, :], ffn0.rearrange("p (e m i) -> p e m i", e=E0, m=3)).then_inc(s.ffn0_in, 16)
            sp.wait_ge(s.maskrow, 1)
            for g, (f0, n) in enumerate(GROUPS):
                sp.dma_start(kstack[3 * n:3 * n + 1, g, nk // 2:].bitcast(F32), maskrow[:, :].bitcast(F32)).then_inc(s.k_row, 16)
            sp.wait_ge(s.gu, C0 * len(UNITS))
            sp.dma_start(ffn1_sb[:, :, :, :], ffn1.rearrange("p (e m i) -> p e m i", e=E1, m=2)).then_inc(s.ffn1_in, 16)
            for b in range(B):
                sp.wait_ge(s.final, b + 1)
                sp.dma_start(out[b].rearrange("(j p) d -> p j d", p=P),
                             X[:, b * TPB:(b + 1) * TPB, :]).then_inc(s.out_done, 16)
            sp.wait_ge(s.out_done, 16 * B)

        @block.gpsimd
        def _(pool):
            pool.dma_start(half_sb[:, :], half).then_inc(s.half_in, 16)
            pool.dma_start(padmask_sb[:, :], padmask).then_inc(s.masks_in, 16)
            pool.dma_start(keymask_sb[:, :], keymask).then_inc(s.masks_in, 16)
            pool.dma_start(keyrows_sb[:, :, :], keyrows).then_inc(s.masks_in, 16)
            pool.dma_start(pick[:, :], selection).then_inc(s.pick_in, 16)
            pool.memset(A, 0.0).then_inc(s.A_zero, 1)
            for lv in range(1, LEVELS):
                for b in range(B):
                    if lv == 1:
                        pool.wait_ge(s.f_ready, b + 1)
                        pool.wait_ge(s.k_ready, b + 1)
                    else:
                        pool.wait_ge(s.tot_step, B * (lv - 2) + b + 1)
                    t = total(lv - 1, b).rearrange("p (n two) -> p n two", two=2)
                    pool.tensor_tensor(total(lv, b), t[:, :, 0], t[:, :, 1], ALU.mult).then_inc(s.tot_step, 1)
                    pool.wait_ge(s.level_mm, B * lv + b + 1)
                    seg = 1 << (lv - 1)
                    kv = seq(ks, b).rearrange("p (n two g) -> p n two g", two=2, g=seg)[:, :, 0, :]
                    right = t[:, :, 1].rearrange("p (n one) -> p n one", one=1).broadcast_to([P, S // (2 * seg), seg])
                    pool.tensor_tensor(kv, kv, right, ALU.mult).then_inc(s.ks_step, 1)
            pool.wait_ge(s.work_in, 16)
            pool.wait_ge(s.k_stack, len(GROUPS))
            full = len(GROUPS) - 1

            def values(l, b):
                pool.wait_ge(s.vr_kept, b + 1)
                m = wk("rowmask") if l == 0 else rowm1[:, b, :]
                m = m.rearrange("p (n one) -> p n one", one=1)
                pv = vrep_sb[:, b, :].rearrange("p (c l n) -> p c l n", c=NCH, l=2)[:, :, l, :]
                pool.tensor_tensor(
                    vblk[:, l, b, :, 0:HD].rearrange("p (c h) f -> p c h f", c=NCH),
                    pv.rearrange("p c (h f) -> p c h f", h=NHC),
                    m.broadcast_to([P, NCH * NHC, HD]).rearrange("p (c h) f -> p c h f", c=NCH), ALU.mult)
                pool.tensor_copy(vblk[:, l, b, :, HD:HD + 1], m).then_inc(s.vb_ready, 1)

            for l in range(2):
                rows = 3 * GH * HD + l
                last_rows = 3 * GROUPS[-1][1] + l
                if l:
                    pool.wait_ge(s.k_row, 16 * len(GROUPS))
                for b in range(B):
                    at = (l * B + b) * PK
                    for g in range(full):
                        pool.tensor_tensor(
                            kblk[0:rows, l, b, g * GH * PK:(g + 1) * GH * PK].rearrange("p (h k) -> p h k", h=GH),
                            kstack[0:rows, g, at:at + PK].rearrange("p (one k) -> p one k", one=1).broadcast_to([rows, GH, PK]),
                            wk("stackmask")[0:rows, :].rearrange("p (h one) -> p h one", one=1).broadcast_to([rows, GH, PK]), ALU.mult)
                    pool.tensor_copy(kblk[0:last_rows, l, b, full * GH * PK:],
                                     kstack[0:last_rows, full, at:at + PK]).then_inc(s.kblk_ready, 1)
                    if (l, b) == (0, 0):
                        pool.wait_ge(s.rowm, 1 + B)
                        for vl in range(2):
                            for vb in range(B):
                                values(vl, vb)

            def add_bias(l, b):
                pool.wait_ge(s.normed, LN_AT[LN_X1 if l else LN_X0, b] + 1)
                xs = X[:, b * TPB:(b + 1) * TPB, :]
                bo = wk("bo1" if l else "bo0").rearrange("p (one d) -> p one d", one=1).broadcast_to([P, TPB, D])
                pool.tensor_tensor(xs, xs, bo, ALU.add).then_inc(s.x_bias, 1)

            def attention(b):
                pool.wait_ge(s.a_max, b + 1)
                pool.partition_all_reduce(gmax[:, b:b + 1], amax[:, b, 3:4], P, bass.bass_isa.ReduceOp.max).then_inc(s.a_gmax, 1)
                pool.wait_ge(s.a_sum, b + 1)
                pool.partition_all_reduce(gsum[:, b:b + 1], asum[:, b, 3:4], P, bass.bass_isa.ReduceOp.add).then_inc(s.a_gsum, 1)

            def ones_row(b):
                pool.tensor_scalar(
                    qstack[b][:, :, :].rearrange("p g (j t) -> p (g j) t", j=TPB),
                    ident.rearrange("p (one t) -> p one t", one=1).broadcast_to([P, len(GROUPS) * TPB, P]),
                    0.0, 1.0, ALU.mult, ALU.add).then_inc(s.ones_row, 1)

            pool.dma_start(whi[:, :, :], ffn0.rearrange("p (e m i) -> p e (m i)", e=E0, m=3)[:, :, 0:2 * I0]).then_inc(s.w_hi, 16)
            add_bias(0, 0)
            add_bias(0, 1)
            pool.wait_ge(s.score, 3 * TPB)
            ones_row(0)
            pool.wait_ge(s.ffn0_in, 16)
            pool.wait_ge(s.w_hi, 16)
            for e in range(E0):
                pool.tensor_tensor(wlo[:, e, :], ffn0_sb[:, e, 0:2, :].rearrange("p m i -> p (m i)"), whi[:, e, :], ALU.subtract).then_inc(s.w_lo, 1)
            for b in range(B):
                pool.wait_ge(s.x_hi, b + 1)
                pool.wait_ge(s.nT, LN_AT[LN_F0, b] + 1)
                pool.tensor_tensor(xlo[:, b, :], seq(nT, b), xhi[:, b, :], ALU.subtract).then_inc(s.x_lo, 1)
            attention(0)
            add_bias(1, 0)
            pool.wait_ge(s.down, len(UNITS))
            ones_row(1)
            attention(1)
            add_bias(1, 1)
            for b in range(B):
                pool.wait_ge(s.n_hi, b + 1)
                pool.tensor_tensor(xlo[:, b, :], N[:, b * TPB:(b + 1) * TPB, :].rearrange("p j d -> p (j d)"),
                                   xhi[:, b, :], ALU.subtract).then_inc(s.n_lo, 1)
            for j in range(NT):
                pool.wait_ge(s.disp, j + 1)
                if j == 0:
                    pool.wait_ge(s.pT, 3 * 2 * NT)
                pool.tensor_tensor(
                    wdisp[:, j, :, :], disp[:, j, :, :],
                    coef[:, j, :].rearrange("p (e one) -> p e one", one=1).broadcast_to([P, E1, CAP]),
                    ALU.mult).then_inc(s.wdisp, 1)

        @block.scalar
        def _(act):
            def ln_rstd(k, b):
                i = LN_AT[k, b]
                moments, logvar, rstd = moments2[:, i % 2], logvar2[:, i % 2], rstd2[:, i % 2]
                act.wait_ge(s.moments, i + 1)
                if i >= 2:
                    act.wait_ge(s.normed, i - 1)
                act.activation(logvar[:, :], moments[:, :, 1], ACT.Ln, bias=tiny[:, 0:1]).then_inc(s.logvar, 1)
                act.wait_ge(s.logvar, i + 1)
                act.activation(rstd[:, :], logvar[:, :], ACT.Exp, scale=-0.5).then_inc(s.rstd, 1)

            def ln_out(k, b, scale=1.0):
                act.wait_ge(s.turned, LN_AT[k, b] + 1)
                if k == LN_F0:
                    act.copy(xhi[:, b, :], bank[7][:, :]).then_inc(s.x_hi, 1)
                act.activation(seq(nT, b), bank[7][:, :], ACT.Copy, scale=scale).then_inc(s.nT, 1)

            act.wait_ge(s.setup, 1)
            act.preload_act_table_set("natural_log_exp_and_others")
            ln_rstd(LN_X, 0)
            ln_out(LN_X, 0)
            ln_rstd(LN_X, 1)
            for b in range(B):
                act.wait_ge(s.p_lg, b + 1)
                act.activation(seq(decay, b), bank[1][:, :], ACT.Sigmoid).then_inc(s.f_ready, 1)
                act.activation(seq(ks, b), bank[1][:, :], ACT.Sigmoid, scale=-1.0).then_inc(s.k_ready, 1)
                act.wait_ge(s.p_q, b + 1)
                act.activation(seq(sig, b), bank[0][:, :], ACT.Sigmoid).then_inc(s.sigq, 1)
                if b == 0:
                    ln_out(LN_X, 1)
                act.wait_ge(s.p_g1, b + 1)
                act.copy(seq(g1T, b), bank[2][:, :]).then_inc(s.g1_ready, 1)
                act.wait_ge(s.p_v, b + 1)
                act.copy(seq(v, b), bank[3][:, :]).then_inc(s.v_ready, 1)
                act.wait_ge(s.p_gate, b + 1)
                act.activation(seq(gate, b), bank[4][:, :], ACT.Sigmoid).then_inc(s.gate_ready, 1)
            act.wait_ge(s.kT_mm, 1)
            for l in range(2):
                cols = slice(l * B * PK, (l + 1) * B * PK)
                last = act.activation(qhi[:, cols], bank[2][:, cols], ACT.Identity, bias=wk(f"bk{l}"))
            last.then_inc(s.k_hi, 1)
            for b in range(B):
                act.wait_ge(s.vrep, b + 1)
                act.copy(vrep_sb[:, b, :], bank[VREP_BANK[b]][:, 0:NCH * 2 * NHC * HD]).then_inc(s.vr_kept, 1)
            for g, (f0, n) in enumerate(GROUPS):
                act.wait_ge(s.k_pick, g + 1)
                act.copy(kstack[0:3 * n, g, :], bank[2 * (g % 2)][0:3 * n, 0:nk]).then_inc(s.k_stack, 1)
            act.preload_act_table_set("natural_log_exp_and_others")
            for b in range(B):
                act.wait_ge(s.khat_T, b + 1)
                act.copy(seq(khat, b)[:, 0:3 * P], bank[2 * b][:, 0:3 * P]).then_inc(s.khat_ready, 1)
            for b in range(B):
                ln_rstd(LN_GLA, b)
                ln_out(LN_GLA, b, scale=ea("lnw"))

            def norm_hi(b):
                act.wait_ge(s.normed, LN_AT[LN_F1, b] + 1)
                act.copy(xhi[:, b, :], N[:, b * TPB:(b + 1) * TPB, :].rearrange("p j d -> p (j d)")).then_inc(s.n_hi, 1)

            def query(l, b):
                act.wait_ge(s.q_mm, 2 * l + b + 1)
                if 2 * l + b:
                    act.wait_ge(s.q_pick, len(GROUPS) * (2 * l + b))
                act.activation(qhi[:, :], bank[5][:, :], ACT.Identity, bias=wk(f"bq{l}")).then_inc(s.q_hi, 1)

            def stack(l, b, g):
                n = GROUPS[g][1]
                act.wait_ge(s.q_pick, len(GROUPS) * (2 * l + b) + g + 1)
                if l:
                    act.wait_ge(s.ones_row, b + 1)
                act.copy(qstack[b][0:3 * n, g, :], bank[STACK_BANKS[l, b][g]][0:3 * n, :]).then_inc(s.q_stack_act, 1)

            def attention(b, part):
                if part == 0:
                    act.wait_ge(s.a_qk, 2 * b + 1)
                    act.activation(seq(aqT, b), bank[A_BANK[b][0]][:, :], ACT.Identity, bias=wk("abq")).then_inc(s.a_q, 1)
                elif part == 1:
                    act.wait_ge(s.a_qk, 2 * b + 2)
                    act.activation(seq(akT, b), bank[A_BANK[b][1]][:, :], ACT.Identity, bias=wk("abk")).then_inc(s.a_k, 1)
                elif part < 5:
                    k = part - 2
                    act.wait_ge(s.a_score, 3 * b + k + 1)
                    act.copy(expo[:, b, k, 0:A_COLS[k]], bank[A_BANK[b][3 + k]][:, 0:A_COLS[k]]).then_inc(s.a_raw, 1)
                else:
                    act.wait_ge(s.a_gmax, b + 1)
                    act.mul(nmax[:, b:b + 1], gmax[:, b:b + 1], -ASCALE).then_inc(s.a_nmax, 1)
                    act.wait_ge(s.a_nmax, b + 1)
                    for k, n in enumerate(A_COLS):
                        act.activation(expo[:, b, k, 0:n], expo[:, b, k, 0:n], ACT.Exp, bias=nmax[:, b:b + 1],
                                       scale=ASCALE, accum_out=asum[:, b, k:k + 1]).then_inc(s.a_exp, 1)

            def router_exp(b):
                cf = coef[:, b * TPB:(b + 1) * TPB, :]
                act.wait_ge(s.b_shift, b + 1)
                act.activation(cf, cf, ACT.Exp).then_inc(s.b_exp, 1)

            def cross(l):
                for i in range(NT + 2):
                    if i == TPB:
                        stack(l, 1, 0)
                        stack(l, 1, 2)
                    if l == 0:
                        if i == 2:
                            ln_out(LN_X0, 1)
                        if i == 7:
                            ln_out(LN_F0, 0)
                    else:
                        if i == 0:
                            ln_out(LN_ATT, 1)
                            attention(1, 0)
                            attention(1, 1)
                        if i == 3:
                            ln_out(LN_X1, 1)
                        if i == 7:
                            ln_out(LN_F1, 0)
                        if i == 8:
                            norm_hi(0)
                    for k in range(3):
                        if k == 2 and i >= 2:
                            g = l * NT + i - 2
                            act.wait_ge(s.hT, g + 1)
                            act.activation(headsT[:, :], bank[7][:, 0:P], ACT.Identity, bias=wk(f"bv{l}")).then_inc(s.hT_ready, 1)
                        if 1 <= i <= NT:
                            g = l * NT + i - 1
                            if g and k == 0:
                                act.wait_ge(s.pv, g)
                            act.wait_ge(s.pT, 3 * g + k + 1)
                            pt = bank[3 + (3 * g + k) % 2]
                            if k < 2:
                                act.copy(ptT[:, 4 * k:4 * k + 4, :].rearrange("p c q -> p (c q)"), pt[:, :]).then_inc(s.pT_ready, 1)
                            else:
                                act.copy(ptT[:, 8, :], pt[:, 0:P])
                                act.copy(ptT[0:LASTR, 9, :], pt[0:LASTR, P:2 * P]).then_inc(s.pT_ready, 1)
                    if i == TPB - 1:
                        query(l, 1)
                    if (l, i) == (1, 1):
                        attention(1, 5)
                    if i < NT:
                        g = l * NT + i
                        act.wait_ge(s.probs_ready, 3 * g + 3)
                        act.activation(probs[:, g % 2, :], probs[:, g % 2, :], ACT.Exp, scale=XSCALE).then_inc(s.exp_ready, 1)
                    if l == 0:
                        if i == 0:
                            ln_rstd(LN_X0, 1)
                        if i == 5:
                            ln_rstd(LN_F0, 0)
                    if l == 1:
                        if i == 5:
                            ln_rstd(LN_F1, 0)
                        if i == 0:
                            for part in range(2, 5):
                                attention(1, part)
                        if i == 2:
                            ln_rstd(LN_X1, 1)
                        if i == 8:
                            router_exp(0)

            ln_rstd(LN_X0, 0)
            ln_out(LN_X0, 0)
            query(0, 0)
            stack(0, 0, 0)
            stack(0, 0, 2)
            cross(0)
            act.wait_ge(s.diff, 1)
            act.activation(two[:, 1, 0:TPB], two[:, 0, 0:TPB], ACT.Exp).then_inc(s.ediff, 1)
            ln_rstd(LN_F0, 1)
            for i in range(len(UNITS)):
                for u in range(C0 * i, C0 * i + C0):
                    act.wait_ge(s.gu, u + 1)
                    if u >= 2:
                        act.wait_ge(s.hid, u - 1)
                    act.activation(gact[:, u % 2, :], bank[2 * (u % 2)][:, :], ACT.Silu).then_inc(s.act, 1)
                    if (i, u % C0) == (E0 + 1, 0):
                        act.preload_act_table_set("natural_log_exp_and_others")
                        ln_rstd(LN_ATT, 0)
                    if (i, u % C0) == (E0 + 2, 0):
                        attention(0, 0)
                    if (i, u % C0) == (E0 + 2, 1):
                        attention(0, 1)
                    if (i, u % C0) == (E0 + 3, 0):
                        attention(0, 2)
                    if (i, u % C0) == (E0 + 3, 1):
                        attention(0, 3)
                    if (i, u % C0) == (E0 + 4, 0):
                        attention(0, 4)
                    if (i, u % C0) == (E0 + 5, 0):
                        act.preload_act_table_set("natural_log_exp_and_others")
                        attention(0, 5)
                if i == 1:
                    ln_out(LN_F0, 1)
                if i == 2:
                    act.preload_act_table_set("natural_log_exp_and_others")
                    act.wait_ge(s.diff, 2)
                    act.activation(two[:, 1, TPB:NT], two[:, 0, TPB:NT], ACT.Exp).then_inc(s.ediff, 1)
                if i == E0 + 1:
                    ln_out(LN_ATT, 0)
            act.preload_act_table_set("natural_log_exp_and_others")
            ln_rstd(LN_X1, 0)
            ln_out(LN_X1, 0)
            query(1, 0)
            stack(1, 0, 0)
            stack(1, 0, 2)
            ln_rstd(LN_ATT, 1)
            cross(1)

            def dispatched(b):
                for hf_ in range(2):
                    act.wait_ge(s.xd, 2 * b + hf_ + 1)
                    act.copy(xd[:, 4 * hf_:4 * hf_ + 4, b, :],
                             bank[hf_][:, 0:4 * CAP].rearrange("p (e c) -> p e c", e=4)).then_inc(s.xd_ready, 1)

            ln_rstd(LN_F1, 1)
            norm_hi(1)
            ln_out(LN_F1, 1)
            router_exp(1)
            dispatched(0)
            dispatched(1)
            for n in range(E1 * B):
                e, b = n // B, n % B
                act.wait_ge(s.dpT, n + 1)
                act.copy(dpT[:, b, e, :], bank[b][0:CAP, :]).then_inc(s.dpT_ready, 1)

        @block.vector
        def _(dve):
            def ln_moments(k, b, src):
                i = LN_AT[k, b]
                stats, moments = stats2[:, i % 2], moments2[:, i % 2]
                if i >= 2:
                    dve.wait_ge(s.normed, i - 1)
                for j in range(TPB):
                    last = dve.bn_stats(stats[:, j, :], src[:, b * TPB + j, :])
                last.then_inc(s.stats, 1)
                dve.wait_ge(s.stats, i + 1)
                for j in range(TPB):
                    last = dve.bn_aggr(moments[:, j, :], stats[:, j, :])
                last.then_inc(s.moments, 1)

            def ln_norm(k, b, src):
                i = LN_AT[k, b]
                moments, rstd = moments2[:, i % 2], rstd2[:, i % 2]
                dve.wait_ge(s.rstd, i + 1)
                if norm_before(k, b):
                    dve.wait_ge(s.turned, norm_before(k, b))
                for j in range(TPB):
                    last = dve.tensor_scalar(N[:, b * TPB + j, :], src[:, b * TPB + j, :], moments[:, j, 0:1],
                                             rstd[:, j:j + 1], ALU.subtract, ALU.mult)
                last.then_inc(s.normed, 1)

            def ln(k, b, src):
                ln_moments(k, b, src)
                ln_norm(k, b, src)

            dve.memset(tiny[:, :], EPS).then_inc(s.setup, 1)
            dve.wait_ge(s.x_in0, 16)
            ln(LN_X, 0, X)
            dve.wait_ge(s.x_in1, 16)
            ln(LN_X, 1, X)
            for b in range(B):
                dve.wait_ge(s.sigq, b + 1)
                dve.tensor_tensor(seq(qp, b), bank[0][:, :], seq(sig, b), ALU.mult).then_inc(s.q_ready, 1)
            dve.wait_ge(s.glam_in, 16)
            dve.wait_ge(s.A_zero, 1)
            for lv in range(LEVELS):
                for b in range(B):
                    i = B * lv + b
                    dve.wait_ge(s.level_mm, i + 1)
                    if lv == 0:
                        dve.wait_ge(s.f_ready, b + 1)
                        dve.tensor_tensor(seq(qp, b), seq(qp, b), seq(decay, b), ALU.mult).then_inc(s.qp_step, 1)
                    else:
                        seg = 1 << (lv - 1)
                        if lv >= 2:
                            dve.wait_ge(s.tot_step, B * (lv - 2) + b + 1)
                        dve.wait_ge(s.qp_step, i - B + 1)
                        qv = seq(qp, b).rearrange("p (n two g) -> p n two g", two=2, g=seg)[:, :, 1, :]
                        left = total(lv - 1, b).rearrange("p (n two) -> p n two", two=2)[:, :, 0]
                        left = left.rearrange("p (n one) -> p n one", one=1).broadcast_to([P, S // (2 * seg), seg])
                        dve.tensor_tensor(qv, qv, left, ALU.mult).then_inc(s.qp_step, 1)
                    if lv:
                        dve.wait_ge(s.level_kept, i - B + 1)
                    dve.copy_predicated(
                        seq(A, b).rearrange("p (j t) -> p j t", j=TPB),
                        tile(glam, lv).rearrange("p (one t) -> p one t", one=1).broadcast_to([P, TPB, P]).bitcast(U32),
                        bank[LEVEL_BANK[lv % 2][b]][:, :].rearrange("p (j t) -> p j t", j=TPB)).then_inc(s.level_kept, 1)
                if lv == 1:
                    dve.wait_ge(s.k_hi, 1)
                    for l in range(2):
                        cols = slice(l * B * PK, (l + 1) * B * PK)
                        last = dve.scalar_tensor_tensor(out=qlo[:, cols], in0=bank[2][:, cols], scalar=wk(f"bk{l}"), in1=qhi[:, cols],
                                                        op0=ALU.add, op1=ALU.subtract)
                    last.then_inc(s.k_lo, 1)
            for c in range(3):
                for b in range(B):
                    dve.wait_ge(s.upd, 3 * (b + 1))
                    u = bank[2 * b][:, c * P:(c + 1) * P]
                    if c == 0:
                        dve.tensor_copy(state[:, b, 0, :], u).then_inc(s.state_ready, 1)
                    else:
                        if c == 1:
                            dve.wait_ge(s.tot_step, B * (LEVELS - 2) + b + 1)
                        dve.wait_ge(s.state_ready, B * (c - 1) + b + 1)
                        dve.scalar_tensor_tensor(out=state[:, b, c, :], in0=state[:, b, c - 1, :],
                                                 scalar=total(LEVELS - 1, b)[:, c:c + 1], in1=u,
                                                 op0=ALU.mult, op1=ALU.add).then_inc(s.state_ready, 1)
            dve.wait_ge(s.work_in, 16)
            dve.wait_ge(s.masks_in, 48)
            dve.tensor_scalar(keep1[:, :, :], keyrows_sb[:, :, :], 0.0, None, ALU.not_equal).then_inc(s.rowm, 1)
            dve.tensor_scalar(maskrow[:, :], keymask_sb[:, :], 0.0, -1e18, ALU.is_equal, ALU.mult).then_inc(s.maskrow, 1)
            dve.tensor_copy(maskT0[:, :], padmask_sb[:, :].bitcast(U8)).then_inc(s.maskT, 1)
            dve.wait_ge(s.rowm, 1)
            for b in range(B):
                dve.tensor_tensor(
                    rowm1[:, b, :].rearrange("p (c h) -> p c h", c=NCH),
                    wk("rowmask").rearrange("p (c h) -> p c h", c=NCH),
                    keep1[:, b, :].rearrange("p (c one) -> p c one", one=1).broadcast_to([P, NCH, NHC]),
                    ALU.mult).then_inc(s.rowm, 1)
            ogv = og.rearrange("p (j d) -> p j d", j=NT)
            def query_rest(l, b):
                dve.wait_ge(s.q_hi, 2 * l + b + 1)
                dve.scalar_tensor_tensor(out=qlo[:, :], in0=bank[5][:, :], scalar=wk(f"bq{l}"), in1=qhi[:, :],
                                         op0=ALU.add, op1=ALU.subtract).then_inc(s.q_lo, 1)

            def stack(l, b):
                for g in BY_DVE:
                    n = GROUPS[g][1]
                    dve.wait_ge(s.q_pick, len(GROUPS) * (2 * l + b) + g + 1)
                    if l:
                        dve.wait_ge(s.ones_row, b + 1)
                    dve.tensor_copy(qstack[b][0:3 * n, g, :], bank[STACK_BANKS[l, b][g]][0:3 * n, :]).then_inc(s.q_stack_dve, 1)

            def gated(b):
                dve.wait_ge(s.o_ready, b + 1)
                dve.wait_ge(s.gate_ready, b + 1)
                dve.tensor_tensor(seq(og, b), bank[5 + b][:, :], seq(gate, b), ALU.mult).then_inc(s.og_ready, 1)

            def add_gla(b):
                dve.wait_ge(s.p_out, b + 1)
                xs = X[:, b * TPB:(b + 1) * TPB, :].rearrange("p j d -> p (j d)")
                dve.tensor_tensor(xs, xs, bank[2 * b][:, :], ALU.add).then_inc(s.x_gla, 1)

            gated(0)
            dve.wait_ge(s.og_ready, 1)
            ln_moments(LN_GLA, 0, ogv)
            gated(1)
            ln_norm(LN_GLA, 0, ogv)
            dve.wait_ge(s.og_ready, B)
            ln_moments(LN_GLA, 1, ogv)
            ln_norm(LN_GLA, 1, ogv)
            add_gla(0)
            dve.wait_ge(s.x_gla, 1)
            ln_moments(LN_X0, 0, X)
            ln_norm(LN_X0, 0, X)
            add_gla(1)
            query_rest(0, 0)
            stack(0, 0)

            def router(k, b):
                n = B * k + b
                tb = slice(b * TPB, (b + 1) * TPB)
                dve.wait_ge(s.r_mm, n + 1)
                lg = bank[5][:, 0:TPB * E0].rearrange("p (j e) -> p j e", j=TPB)
                if k == 0:
                    dve.tensor_tensor(logits[:, tb, :], lg, wk("br0").rearrange("p (one e) -> p one e", one=1).broadcast_to([P, TPB, E0]),
                                      ALU.add).then_inc(s.logit, 1)
                else:
                    dve.tensor_copy(logits[:, tb, :], lg).then_inc(s.logit, 1)
                dve.wait_ge(s.logit, n + 1)
                for j in range(TPB):
                    last = dve.max(top[:, b * TPB + j, :], logits[:, b * TPB + j, :])
                last.then_inc(s.top, 1)
                dve.wait_ge(s.top, n + 1)
                if k == 0:
                    dve.tensor_tensor(two[:, 0, tb], top[:, tb, 1], top[:, tb, 0], ALU.subtract).then_inc(s.diff, 1)
                else:
                    dve.tensor_tensor(coef[:, tb, :], logits[:, tb, :], top[:, tb, 0:1].broadcast_to([P, TPB, E1]),
                                      ALU.subtract).then_inc(s.b_shift, 1)
                for j in range(TPB):
                    last = dve.max_index(topi[:, b * TPB + j, :], top[:, b * TPB + j, :], logits[:, b * TPB + j, :])
                last.then_inc(s.topi, 1)
                dve.wait_ge(s.topi, n + 1)
                dve.tensor_copy(topf[:, tb, :], topi[:, tb, 0:2]).then_inc(s.topf, 1)
                dve.wait_ge(s.topf, n + 1)
                ex = wk("experts").rearrange("p (one e) -> p one e", one=1).broadcast_to([P, TPB, E0])
                for r in range(2):
                    last = dve.tensor_tensor(sel[:, r, tb, :], ex, topf[:, tb, r:r + 1].broadcast_to([P, TPB, E0]), ALU.is_equal)
                last.then_inc(s.eq1, 1)
                dve.wait_ge(s.eq1, n + 1)

            def softmax_two(b):
                tb = slice(b * TPB, (b + 1) * TPB)
                dve.wait_ge(s.ediff, b + 1)
                dve.tensor_scalar(two[:, 2, tb], two[:, 1, tb], 1.0, None, ALU.add).then_inc(s.one, 1)
                dve.wait_ge(s.one, b + 1)
                dve.reciprocal(two[:, 0, tb], two[:, 2, tb]).then_inc(s.w1, 1)
                dve.wait_ge(s.w1, b + 1)
                dve.tensor_tensor(two[:, 2, tb], two[:, 0, tb], two[:, 1, tb], ALU.mult).then_inc(s.w2, 1)
                dve.wait_ge(s.w2, b + 1)
                for r, w in ((0, 0), (1, 2)):
                    last = dve.tensor_tensor(sel[:, r, tb, :], sel[:, r, tb, :],
                                             two[:, w, tb].rearrange("p (j one) -> p j one", one=1).broadcast_to([P, TPB, E0]), ALU.mult)
                last.then_inc(s.coef_p, 1)
                dve.wait_ge(s.coef_p, b + 1)
                dve.tensor_tensor(coef[:, tb, :], sel[:, 0, tb, :], sel[:, 1, tb, :], ALU.add).then_inc(s.coef, 1)

            def chosen(b):
                tb = slice(b * TPB, (b + 1) * TPB)
                dve.tensor_tensor(selh[:, tb, :], sel[:, 0, tb, :], sel[:, 1, tb, :], ALU.add).then_inc(s.selh, 1)

            def softmax_all(b):
                tb = slice(b * TPB, (b + 1) * TPB)
                dve.wait_ge(s.b_exp, b + 1)
                dve.tensor_reduce(two[:, 0, tb], coef[:, tb, :], AX.X, ALU.add).then_inc(s.b_sum, 1)
                dve.wait_ge(s.b_sum, b + 1)
                dve.reciprocal(two[:, 1, tb], two[:, 0, tb]).then_inc(s.b_rec, 1)
                dve.wait_ge(s.b_rec, b + 1)
                dve.tensor_tensor(coef[:, tb, :], coef[:, tb, :], two[:, 1, tb].rearrange("p (j one) -> p j one", one=1).broadcast_to([P, TPB, E1]),
                                  ALU.mult).then_inc(s.b_prob, 1)
                dve.wait_ge(s.b_prob, b + 1)
                dve.wait_ge(s.pos, b + 1)
                dve.wait_ge(s.selh, b + 1)
                dve.scalar_tensor_tensor(out=slot[:, tb, :], in0=selh[:, tb, :], scalar=-BIG,
                                         in1=bank[5][:, 0:TPB * E1].rearrange("p (j e) -> p j e", j=TPB),
                                         op0=ALU.mult, op1=ALU.add).then_inc(s.slot, 1)

            def dispatch_rows(b, tiles):
                dve.wait_ge(s.slot, b + 1)
                for j in range(b * TPB + tiles[0], b * TPB + tiles[1]):
                    dve.tensor_tensor(disp[:, j, :, :],
                                      wk("slots").rearrange("p (one c) -> p one c", one=1).broadcast_to([P, E1, CAP]),
                                      slot[:, j, :].rearrange("p (e one) -> p e one", one=1).broadcast_to([P, E1, CAP]),
                                      ALU.is_equal).then_inc(s.disp, 1)

            def attention(b, part):
                if part == 0:
                    dve.wait_ge(s.a_v, b + 1)
                    dve.tensor_tensor(av_sb[:, b * TPB:(b + 1) * TPB, :], bank[A_BANK[b][2]][:, :].rearrange("p (j d) -> p j d", j=TPB),
                                      wk("abv").rearrange("p (one d) -> p one d", one=1).broadcast_to([P, TPB, D]),
                                      ALU.add).then_inc(s.av_ready, 1)
                elif part == 1:
                    for k, n in enumerate(A_COLS):
                        dve.wait_ge(s.a_raw, 3 * b + k + 1)
                        dve.tensor_reduce(amax[:, b, k:k + 1], expo[:, b, k, 0:n], AX.X, ALU.max).then_inc(s.a_pmax, 1)
                    dve.wait_ge(s.a_pmax, 3 * b + 3)
                    dve.tensor_reduce(amax[:, b, 3:4], amax[:, b, 0:3], AX.X, ALU.max).then_inc(s.a_max, 1)
                elif part == 2:
                    dve.wait_ge(s.a_exp, 3 * b + 3)
                    dve.tensor_reduce(asum[:, b, 3:4], asum[:, b, 0:3], AX.X, ALU.add).then_inc(s.a_sum, 1)
                else:
                    dve.wait_ge(s.a_gsum, b + 1)
                    dve.reciprocal(rtot[:, b:b + 1], gsum[:, b:b + 1]).then_inc(s.a_rtot, 1)
                    dve.wait_ge(s.a_rtot, b + 1)
                    dve.wait_ge(s.a_pv, b + 1)
                    xs = X[:, b * TPB:(b + 1) * TPB, :].rearrange("p j d -> p (j d)")
                    dve.scalar_tensor_tensor(out=xs, in0=bank[A_BANK[b][6]][:, :], scalar=rtot[:, b:b + 1], in1=xs,
                                             op0=ALU.mult, op1=ALU.add).then_inc(s.x_att, 1)

            def cross(l):
                for i in range(NT + 2):
                    if l == 1 and i == NT + 1:
                        softmax_all(0)
                        dispatch_rows(0, (0, 1))
                    if i == TPB:
                        stack(l, 1)
                    if i < NT:
                        g = l * NT + i
                        if g >= 2:
                            dve.wait_ge(s.pT, 3 * (g - 1))
                        for k, (n, h0) in enumerate(zip(HEADS_OF_BANK, HEAD_BASE)):
                            dve.wait_ge(s.score, 3 * g + k + 1)
                            sc = bank[k][:, 0:n * PK].rearrange("p (h k) -> p h k", h=n)[:, :, 0:KEYS]
                            dve.tensor_reduce(rowmax[:, h0:h0 + n], sc, AX.X, ALU.max).then_inc(s.rmax, 1)
                            dve.wait_ge(s.rmax, 3 * g + k + 1)
                            dve.tensor_tensor(
                                probs[:, g % 2, h0 * KEYS:(h0 + n) * KEYS].rearrange("p (h k) -> p h k", h=n), sc,
                                rowmax[:, h0:h0 + n].rearrange("p (h one) -> p h one", one=1).broadcast_to([P, n, KEYS]),
                                ALU.subtract).then_inc(s.probs_ready, 1)
                    if i == TPB - 1:
                        query_rest(l, 1)
                    if i == NT:
                        router(l, 0)
                        if l:
                            chosen(0)
                    if 1 <= i <= NT:
                        g = l * NT + i - 1
                        dve.wait_ge(s.pv, g + 1)
                        pvv = bank[6][:, 0:H * (HD + 1)].rearrange("p (h f) -> p h f", h=H)
                        if g:
                            dve.wait_ge(s.heads_r, g)
                        dve.reciprocal(rsum[:, :], pvv[:, :, HD]).then_inc(s.rsum_r, 1)
                        dve.wait_ge(s.rsum_r, g + 1)
                        if g:
                            dve.wait_ge(s.hT, g)
                        dve.tensor_tensor(heads[:, :, :], pvv[:, :, 0:HD],
                                          rsum[:, :].rearrange("p (h one) -> p h one", one=1).broadcast_to([P, H, HD]),
                                          ALU.mult).then_inc(s.heads_r, 1)
                    if i >= 2:
                        g = l * NT + i - 2
                        dve.wait_ge(s.wo, g + 1)
                        dve.wait_ge(s.x_bias, B * l + (i - 2) // TPB + 1)
                        dve.tensor_tensor(X[:, i - 2, :], X[:, i - 2, :], bank[7][:, P:2 * P], ALU.add).then_inc(s.x_res, 1)
                    if l == 0:
                        if i == 0:
                            dve.wait_ge(s.x_gla, B)
                            ln_moments(LN_X0, 1, X)
                        if i == 1:
                            ln_norm(LN_X0, 1, X)
                        if i == 5:
                            dve.wait_ge(s.x_res, TPB)
                            ln_moments(LN_F0, 0, X)
                        if i == 6:
                            ln_norm(LN_F0, 0, X)
                    else:
                        if i == 0:
                            attention(1, 0)
                            attention(1, 1)
                        if i == 1:
                            attention(1, 2)
                        if i == 2:
                            attention(1, 3)
                            dve.wait_ge(s.x_att, B)
                            ln(LN_X1, 1, X)
                        if i == 5:
                            dve.wait_ge(s.x_res, NT + TPB)
                            ln_moments(LN_F1, 0, X)
                        if i == 6:
                            ln_norm(LN_F1, 0, X)

            cross(0)
            dve.wait_ge(s.x_res, NT)
            ln_moments(LN_F0, 1, X)
            softmax_two(0)
            dve.wait_ge(s.coef, 1)
            for i in range(len(UNITS) + 1):
                if i < len(UNITS):
                    for c in range(C0):
                        u = C0 * i + c
                        dve.wait_ge(s.act, u + 1)
                        if i >= 2:
                            dve.wait_ge(s.down, i - 1)
                        dve.tensor_tensor(hid[:, i % 2, c, :], bank[2 * (u % 2) + 1][:, :], gact[:, u % 2, :], ALU.mult).then_inc(s.hid, 1)
                        if (i, c) == (E0 + 1, 0):
                            ln_norm(LN_ATT, 0, X)
                if i >= 1:
                    b, e = UNITS[i - 1]
                    dve.wait_ge(s.down, i)
                    if i >= 2:
                        dve.wait_ge(s.x_ffn, i - 1)
                    for j in range(TPB):
                        t = b * TPB + j
                        last = dve.scalar_tensor_tensor(out=X[:, t, :], in0=bank[4][:, j * P:(j + 1) * P],
                                                        scalar=coef[:, t, e:e + 1], in1=X[:, t, :], op0=ALU.mult, op1=ALU.add)
                    last.then_inc(s.x_ffn, 1)
                if i == 0:
                    ln_norm(LN_F0, 1, X)
                if i == 2:
                    router(0, 1)
                if i == 3:
                    softmax_two(1)
                    dve.wait_ge(s.coef, B)
                if i == E0:
                    dve.wait_ge(s.x_ffn, E0)
                    ln_moments(LN_ATT, 0, X)
                if i == E0 + 2:
                    attention(0, 0)
                if i == E0 + 4:
                    attention(0, 1)
                if i == E0 + 7:
                    ln_norm(LN_X1, 0, X)
                if i == E0 + 6:
                    attention(0, 2)
                    attention(0, 3)
                    dve.wait_ge(s.x_att, 1)
                    ln_moments(LN_X1, 0, X)
            query_rest(1, 0)
            stack(1, 0)
            dve.wait_ge(s.x_ffn, len(UNITS))
            ln(LN_ATT, 1, X)
            cross(1)
            dve.wait_ge(s.x_res, 2 * NT)
            ln_moments(LN_F1, 1, X)
            dispatch_rows(0, (1, 2))
            ln_norm(LN_F1, 1, X)
            dispatch_rows(0, (2, TPB))
            router(1, 1)
            chosen(1)
            softmax_all(1)
            dispatch_rows(1, (0, TPB))
            for e in range(E1 + 1):
                if e < E1:
                    for c in range(C1):
                        q = e * C1 + c
                        dve.wait_ge(s.h_mm, q // 2 + 1)
                        if e >= 2 and c == 0:
                            dve.wait_ge(s.y_mm, B * (e - 1))
                        last = dve.tensor_scalar(h1[:, e % 2, c, :], bank[2 + c // 2][:, (c % 2) * B * CAP:(c % 2 + 1) * B * CAP],
                                                 wk("b1", q, 1), 0.0, ALU.add, ALU.max)
                        if c % 2:
                            last.then_inc(s.h_ready, 1)
                if e >= 1:
                    for b in range(B):
                        n = B * (e - 1) + b
                        dve.wait_ge(s.y_mm, n + 1)
                        if e - 1 >= 2:
                            dve.wait_ge(s.comb, e - 2)
                        dve.tensor_tensor(y1[:, (e - 1) % 2, b, :], bank[4 + b][0:CAP, 0:D],
                                          wk("b2", (e - 1) * D, D)[0:CAP, :], ALU.add).then_inc(s.y_ready, 1)
            for b in range(B):
                dve.wait_ge(s.comb, E1 + b)
                xs = X[:, b * TPB:(b + 1) * TPB, :].rearrange("p j d -> p (j d)")
                dve.tensor_tensor(xs, xs, bank[6 + b][:, :], ALU.add).then_inc(s.final, 1)

        @block.tensor
        def _(pe):
            def mm(o, l, r, start=True, stop=True, **kw):
                return pe.matmul(o, lhsT=l, rhs=r, start=start, stop=stop, **kw)

            def warm(n, o):
                for _ in range(n):
                    mm(o[:, 0:512], hf("ident"), half_sb[:, 0:512].bitcast(BF16))

            def ln(k, b, residuals=0):
                i = LN_AT[k, b]
                pe.wait_ge(s.normed, i + 1)
                if i:
                    pe.wait_ge(s.nT, i)
                if residuals:
                    pe.wait_ge(s.x_res, residuals)
                for j in range(TPB):
                    last = pe.transpose(bank[7][:, j * P:(j + 1) * P], N[:, b * TPB + j, :], ident)
                last.then_inc(s.turned, 1)

            def turned(k, b):
                pe.wait_ge(s.nT, LN_AT[k, b] + 1)

            pe.wait_ge(s.half_in, 16)
            warm(FILL_START, bank[6])
            pe.wait_ge(s.early_in, 16)
            ln(LN_X, 0)
            for b in range(B):
                turned(LN_X, b)
                if b:
                    pe.wait_ge(s.k_ready, b)
                mm(bank[1][:, :], ea("win", 2 * D, D), seq(nT, b)).then_inc(s.p_lg, 1)
                if b:
                    pe.wait_ge(s.q_ready, b)
                mm(bank[0][:, :], ea("win", D, D), seq(nT, b)).then_inc(s.p_q, 1)
                if b:
                    pe.wait_ge(s.g1_ready, b)
                mm(bank[2][:, :], ea("wg1"), seq(nT, b)).then_inc(s.p_g1, 1)
                if b == 0:
                    ln(LN_X, 1)
                if b:
                    pe.wait_ge(s.v_ready, b)
                for j in range(TPB):
                    last = mm(bank[3][:, j * P:(j + 1) * P], tile(nT, b * TPB + j), ea("win", 0, D))
                last.then_inc(s.p_v, 1)
                pe.wait_ge(s.g1_ready, b + 1)
                if b:
                    pe.wait_ge(s.gate_ready, b)
                for j in range(TPB):
                    last = mm(bank[4][:, j * P:(j + 1) * P], tile(g1T, b * TPB + j), ea("wg2"))
                last.then_inc(s.p_gate, 1)
            for lv in range(LEVELS):
                for b in range(B):
                    i = B * lv + b
                    if lv == 0:
                        pe.wait_ge(s.k_ready, b + 1)
                        pe.wait_ge(s.q_ready, b + 1)
                    else:
                        pe.wait_ge(s.qp_step, i - B + 1)
                        if lv >= 2:
                            pe.wait_ge(s.ks_step, i - 2 * B + 1)
                            pe.wait_ge(s.level_kept, i - 2 * B + 1)
                    if lv == 1 and b == 1:
                        pe.wait_ge(s.gate_ready, B)
                    for j in range(TPB):
                        t = b * TPB + j
                        last = mm(bank[LEVEL_BANK[lv % 2][b]][:, j * P:(j + 1) * P], tile(ks, t), tile(qp, t))
                    last.then_inc(s.level_mm, 1)
                both = work_sb[:, WORK["ctx0"][0]:WORK["ctx0"][0] + 6 * KEYS].rearrange("p (b n) -> p b n", b=B)
                if lv == 0:
                    pe.wait_ge(s.work_in, 16)
                    pe.wait_ge(s.g1_ready, B)
                    for l in range(2):
                        last = mm(bank[2][:, l * B * PK:(l + 1) * B * PK].rearrange("p (b k) -> p b k", b=B), wk(f"wk{l}"), both[:, :, 0:PK])
                    last.then_inc(s.kT_mm, 1)
                if 3 <= lv <= 4:
                    pe.wait_ge(s.pick_in, 16)
                    pe.wait_ge(s.k_lo, 1)
                    pe.wait_ge(s.q_ready, B)
                    for g in (2 * lv - 6, 2 * lv - 5):
                        if g >= 2:
                            pe.wait_ge(s.k_stack, g - 1)
                        n = GROUPS[g][1]
                        for w, src in zip(K_WINDOWS, (qhi, qlo)):
                            last = mm(bank[2 * (g % 2)][:, 0:nk], window(g, w), src[:, 0:nk], start=(src is qhi), stop=(src is qlo))
                        last.then_inc(s.k_pick, 1)
                if 1 <= lv <= 2:
                    b = lv - 1
                    pe.wait_ge(s.v_ready, B)
                    pe.wait_ge(s.k_ready, B)
                    wv = work_sb[:, WORK["wv0"][0]:WORK["wv0"][0] + 2 * D].rearrange("p (l d) -> p l d", l=2)
                    for c in range(NCH):
                        n = 2 * NHC * HD
                        last = mm(bank[VREP_BANK[b]][:, c * n:(c + 1) * n].rearrange("p (l f) -> p l f", l=2),
                                  both[:, b, P * c % KEYS:P * c % KEYS + P], wv[:, :, HLO[c] * HD:(HLO[c] + NHC) * HD])
                    last.then_inc(s.vrep, 1)
            pe.wait_ge(s.q_ready, B)
            pe.wait_ge(s.k_stack, len(GROUPS))
            for b in range(B):
                pe.wait_ge(s.ks_step, B * (LEVELS - 2) + b + 1)
                for c in range(3):
                    last = pe.transpose(bank[2 * b][:, c * P:(c + 1) * P], tile(ks, b * TPB + c), ident)
                last.then_inc(s.khat_T, 1)
            for b in range(B):
                pe.wait_ge(s.khat_ready, b + 1)
                for c in range(3):
                    mm(bank[2 * b][:, c * P:(c + 1) * P], tile(khat, b * TPB + c), tile(v, b * TPB + c)).then_inc(s.upd, 1)
            for b in range(B):
                pe.wait_ge(s.level_kept, B * (LEVELS - 1) + b + 1)
                pe.wait_ge(s.qp_step, B * (LEVELS - 1) + b + 1)
                for j in range(TPB):
                    t = b * TPB + j
                    o = bank[5 + b][:, j * P:(j + 1) * P]
                    last = mm(o, tile(A, t), tile(v, t), stop=(j == 0))
                    if j:
                        pe.wait_ge(s.state_ready, B * (j - 1) + b + 1)
                        last = mm(o, tile(qp, t), state[:, b, j - 1, :], start=False)
                last.then_inc(s.o_ready, 1)
            pe.wait_ge(s.state_ready, 3 * B)
            for b in range(B):
                warm(FILL_GLA[b], bank[4])
                ln(LN_GLA, b)
                turned(LN_GLA, b)
                for j in range(TPB):
                    last = mm(bank[2 * b][:, j * P:(j + 1) * P], tile(nT, b * TPB + j), ea("wout"))
                last.then_inc(s.p_out, 1)

            def query(l, b):
                turned(LN_X1 if l else LN_X0, b)
                mm(bank[5][:, :], wk(f"wq{l}"), seq(nT, b)).then_inc(s.q_mm, 1)

            def stack(l, b):
                pe.wait_ge(s.q_lo, 2 * l + b + 1)
                for g in range(len(GROUPS)):
                    o = bank[STACK_BANKS[l, b][g]][:, :]
                    mm(o, window(g, Q_WINDOWS[0]), qhi[:, :], stop=False)
                    mm(o, window(g, Q_WINDOWS[1]), qlo[:, :], start=False).then_inc(s.q_pick, 1)

            def router(l, b):
                turned(LN_F1 if l else LN_F0, b)
                for j in range(TPB):
                    last = mm(bank[5][:, j * E0:(j + 1) * E0], tile(nT, b * TPB + j), wk(f"wr{l}"))
                last.then_inc(s.r_mm, 1)

            def attention(b, part):
                o = bank[A_BANK[b][part]]
                if part == 0:
                    turned(LN_ATT, b)
                    mm(o[:, :], wk("aq"), seq(nT, b)).then_inc(s.a_qk, 1)
                elif part == 1:
                    if b == 0:
                        pe.wait_ge(s.a_q, b + 1)
                    mm(o[:, :], wk("ak"), seq(nT, b)).then_inc(s.a_qk, 1)
                elif part == 2:
                    if b == 0:
                        pe.wait_ge(s.a_k, b + 1)
                    for j in range(TPB):
                        last = mm(o[:, j * P:(j + 1) * P], tile(nT, b * TPB + j), wk("av"))
                    last.then_inc(s.a_v, 1)
                elif part < 6:
                    k = part - 3
                    if k == 0:
                        pe.wait_ge(s.a_k, b + 1)
                        if b == 0:
                            pe.wait_ge(s.av_ready, b + 1)
                    elif b == 0:
                        pe.wait_ge(s.a_raw, 3 * b + k)
                    for kt in A_TILES[k]:
                        at, n, q0 = A_PLACE[kt][1], S - kt * P, b * S + kt * P
                        ok = o[:, at:at + n]
                        mm(ok[:, 0:P], tile(akT, b * TPB + kt), aqT[:, q0:q0 + P], stop=False)
                        last = mm(ok[:, 0:P], hf("ident"), hf("future"), start=False)
                        if n > P:
                            last = mm(ok[:, P:n], tile(akT, b * TPB + kt), aqT[:, q0 + P:q0 + n])
                    last.then_inc(s.a_score, 1)
                else:
                    pe.wait_ge(s.a_exp, 3 * b + 3)
                    pe.wait_ge(s.av_ready, b + 1)
                    for j in range(TPB):
                        for kt in range(j + 1):
                            k, at = A_PLACE[kt]
                            c = at + (j - kt) * P
                            last = mm(o[:, j * P:(j + 1) * P], expo[:, b, k, c:c + P], av_sb[:, b * TPB + kt, :],
                                      start=(kt == 0), stop=(kt == j))
                    last.then_inc(s.a_pv, 1)

            def cross(l):
                for i in range(NT + 2):
                    if i == TPB:
                        pe.wait_ge(s.pT_ready, 3 * (l * NT + i - 1))
                        pe.wait_ge(s.heads_r, l * NT + i - 1)
                        stack(l, 1)
                    if i < NT:
                        g, b = l * NT + i, i // TPB
                        if i % TPB == 0:
                            pe.wait_ge(s.q_stack_act, 2 * (2 * l + b + 1))
                            pe.wait_ge(s.q_stack_dve, 2 * (2 * l + b + 1))
                            pe.wait_ge(s.kblk_ready, 2 * l + b + 1)
                        for k, (n, h0) in enumerate(zip(HEADS_OF_BANK, HEAD_BASE)):
                            if g:
                                pe.wait_ge(s.probs_ready, 3 * (g - 1) + k + 1)
                            at = 0
                            if i < TPB:
                                warm(1, bank[k])
                            for gr in ((k,) if k < 2 else (2, 3)):
                                rows, m = 3 * GROUPS[gr][1] + l, GROUPS[gr][1] // HD * PK
                                last = mm(bank[k][:, at:at + m], qstack[b][0:rows, gr, (i % TPB) * P:(i % TPB + 1) * P],
                                          kblk[0:rows, l, b, h0 * PK + at:h0 * PK + at + m], stop=(l == 1))
                                if l == 0:
                                    last = mm(bank[k][:, at:at + m], tile(maskT0, i),
                                              hf("maskout", KEYS)[:, h0 * PK + at:h0 * PK + at + m], start=False)
                                at += m
                            last.then_inc(s.score, 1)
                    done = l * NT + max(i - 2, 0)
                    if l == 0:
                        if i == 2:
                            ln(LN_X0, 1, done)
                        if i == 7:
                            ln(LN_F0, 0, done)
                        if i == 8:
                            router(0, 0)
                    else:
                        if i == 0:
                            warm(4, bank[5])
                            ln(LN_ATT, 1)
                            for part in range(6):
                                attention(1, part)
                        if i == 1:
                            pe.wait_ge(s.av_ready, B)
                            pe.wait_ge(s.a_raw, 3 * B)
                        if i == 2:
                            attention(1, 6)
                        if i == 3:
                            ln(LN_X1, 1, done)
                        if i == 7:
                            ln(LN_F1, 0, done)
                        if i == 8:
                            router(1, 0)
                    for k in range(3):
                        if k == 2 and i >= 2:
                            g = l * NT + i - 2
                            pe.wait_ge(s.heads_r, g + 1)
                            if g:
                                pe.wait_ge(s.x_res, g)
                            pe.wait_ge(s.nT, LN_BEFORE[l][i])
                            pe.transpose(bank[7][:, 0:P], heads[:, :, :].rearrange("p h f -> p (h f)"), ident).then_inc(s.hT, 1)
                        if 1 <= i <= NT:
                            g, b = l * NT + i - 1, (i - 1) // TPB
                            if k == 0:
                                pe.wait_ge(s.exp_ready, g + 1)
                            n = 3 * g + k
                            if n >= 2:
                                pe.wait_ge(s.pT_ready, n - 1)
                            for c in range(4 * k, min(4 * k + 4, NCH)):
                                rows = P if c < NCH - 1 else LASTR
                                last = pe.transpose(bank[3 + n % 2][0:rows, (c % 4) * P:(c % 4 + 1) * P],
                                                    probs[:, g % 2, c * P:c * P + rows], ident)
                            last.then_inc(s.pT, 1)
                    if i == TPB - 1:
                        query(l, 1)
                    if (l, i) == (1, NT):
                        positions(0)
                    if 1 <= i <= NT:
                        g, b = l * NT + i - 1, (i - 1) // TPB
                        if g:
                            pe.wait_ge(s.heads_r, g)
                        for c in range(NCH):
                            if c % 4 == 0:
                                pe.wait_ge(s.pT_ready, 3 * g + c // 4 + 1)
                            rows = P if c < NCH - 1 else LASTR
                            lo = HLO[c] * (HD + 1)
                            o = bank[6][:, 0:COPIES * H * (HD + 1)].rearrange("p (i n) -> p i n", i=COPIES)[:, :, lo:lo + NHC * (HD + 1)]
                            v = vblk[0:rows, l, b, c * NHC:(c + 1) * NHC, :].rearrange("p (one h) f -> p one (h f)", one=1)
                            last = mm(o, ptT[0:rows, c, :], v.broadcast_to([rows, COPIES, NHC * (HD + 1)]),
                                      start=(c == 0), stop=(c == NCH - 1), skip_group_check=True)
                        last.then_inc(s.pv, 1)
                    if i >= 2:
                        g = l * NT + i - 2
                        pe.wait_ge(s.hT_ready, g + 1)
                        mm(bank[7][:, P:2 * P], headsT[:, :], wk(f"wo{l}")).then_inc(s.wo, 1)

            def positions(b):
                pe.wait_ge(s.selh, b + 1)
                for j in range(TPB):
                    for i in range(j + 1):
                        last = mm(bank[5][:, j * E1:(j + 1) * E1], hf("below") if i == j else hf("ones"), selh[:, b * TPB + i, :],
                                  start=(i == 0), stop=(i == j))
                last.then_inc(s.pos, 1)

            pe.wait_ge(s.x_gla, 1)
            warm(FILL_GLA[2], bank[4])
            ln(LN_X0, 0)
            warm(FILL_GLA[3], bank[4])
            query(0, 0)
            pe.wait_ge(s.x_gla, B)
            pe.wait_ge(s.maskT, 1)
            pe.wait_ge(s.vr_kept, B)
            warm(FILL_GLA[4], bank[4])
            stack(0, 0)
            pe.wait_ge(s.vb_ready, 2 * B)
            cross(0)
            pe.wait_ge(s.ffn0_in, 16)
            for i in range(len(UNITS) + 1):
                if i < len(UNITS):
                    b, e = UNITS[i]
                    for c in range(C0):
                        u = C0 * i + c
                        if u >= 2:
                            pe.wait_ge(s.hid, u - 1)
                        if c == 0:
                            pe.wait_ge(s.x_lo, b + 1)
                            pe.wait_ge(s.w_lo, e + 1)
                        for m in range(2):
                            w = slice(m * I0 + c * P, m * I0 + (c + 1) * P)
                            o = bank[2 * (u % 2) + m][:, :]
                            mm(o, whi[:, e, w], xhi[:, b, :], stop=False)
                            mm(o, whi[:, e, w], xlo[:, b, :], start=False, stop=False)
                            last = mm(o, wlo[:, e, w], xhi[:, b, :], start=False)
                        last.then_inc(s.gu, 1)
                        if (i, c) == (1, 1):
                            ln(LN_F0, 1, NT)
                        if (i, c) == (2, 1):
                            pe.wait_ge(s.logit, 1)
                            router(0, 1)
                        if (i, c) == (E0 + 1, 1):
                            ln(LN_ATT, 0)
                            pe.wait_ge(s.logit, 2)
                        if (i, c) == (E0 + 2, 0):
                            attention(0, 0)
                        if (i, c) == (E0 + 2, 1):
                            attention(0, 1)
                        if (i, c) == (E0 + 3, 0):
                            attention(0, 3)
                        if (i, c) == (E0 + 3, 1):
                            attention(0, 4)
                        if (i, c) == (E0 + 4, 0):
                            attention(0, 5)
                        if (i, c) == (E0 + 6, 0):
                            attention(0, 6)
                if i >= 1:
                    b, e = UNITS[i - 1]
                    pe.wait_ge(s.hid, C0 * i)
                    if i >= 2:
                        pe.wait_ge(s.x_ffn, i - 1)
                    for j in range(TPB):
                        for c in range(C0):
                            last = mm(bank[4][:, j * P:(j + 1) * P], hid[:, (i - 1) % 2, c, j * P:(j + 1) * P],
                                      ffn0_sb[:, e, 2, c * P:(c + 1) * P], start=(c == 0), stop=(c == C0 - 1))
                    last.then_inc(s.down, 1)
                if i == E0 + 2:
                    attention(0, 2)
            ln(LN_X1, 0)
            query(1, 0)
            stack(1, 0)
            cross(1)

            def dispatch(b):
                if b:
                    pe.wait_ge(s.xd_ready, 2)
                pe.wait_ge(s.n_lo, b + 1)
                for j in range(TPB):
                    t = b * TPB + j
                    pe.wait_ge(s.disp, t + 1)
                    for half_ in range(2):
                        for part in (xhi, xlo):
                            last = mm(bank[half_][:, 0:4 * CAP], tile(part[:, b, :], j),
                                      disp[:, t, 4 * half_:4 * half_ + 4, :].rearrange("p e c -> p (e c)"),
                                      start=(j == 0 and part is xhi), stop=(j == TPB - 1 and part is xlo))
                        if j == TPB - 1:
                            last.then_inc(s.xd, 1)

            warm(FILL_ROUTING[0], bank[2])
            ln(LN_F1, 1, 2 * NT)
            warm(FILL_ROUTING[1], bank[2])
            router(1, 1)
            dispatch(0)
            warm(FILL_ROUTING[2], bank[2])
            pe.wait_ge(s.logit, 4)
            positions(1)
            warm(FILL_ROUTING[3], bank[2])
            dispatch(1)
            pe.wait_ge(s.xd_ready, 2 * B)
            pe.wait_ge(s.ffn1_in, 16)
            for e in range(E1 + 2):
                if e < E1:
                    for c in range(C1):
                        q = e * C1 + c
                        if e and c % 2 == 0:
                            pe.wait_ge(s.h_ready, q // 2 - 1)
                        last = mm(bank[2 + c // 2][:, (c % 2) * B * CAP:(c % 2 + 1) * B * CAP], ffn1_sb[:, e, 0, c * P:(c + 1) * P],
                                  xd[:, e, :, :].rearrange("p b c -> p (b c)"))
                        if c % 2:
                            last.then_inc(s.h_mm, 1)
                    for b in range(B):
                        if e:
                            pe.wait_ge(s.dpT_ready, B * (e - 1) + b + 1)
                        else:
                            pe.wait_ge(s.wdisp, (b + 1) * TPB)
                        for j in range(TPB):
                            last = pe.transpose(bank[b][0:CAP, j * P:(j + 1) * P], wdisp[:, b * TPB + j, e, :], ident)
                        last.then_inc(s.dpT, 1)
                if 1 <= e <= E1:
                    pe.wait_ge(s.h_ready, 2 * e)
                    for b in range(B):
                        if e >= 2:
                            pe.wait_ge(s.y_ready, B * (e - 2) + b + 1)
                        for c in range(C1):
                            last = mm(bank[4 + b][0:CAP, 0:D], h1[:, (e - 1) % 2, c, b * CAP:(b + 1) * CAP],
                                      ffn1_sb[:, e - 1, 1, c * P:(c + 1) * P], start=(c == 0), stop=(c == C1 - 1))
                        last.then_inc(s.y_mm, 1)
                if e >= 2:
                    for b in range(B):
                        pe.wait_ge(s.y_ready, B * (e - 2) + b + 1)
                        pe.wait_ge(s.dpT_ready, B * (e - 2) + b + 1)
                        for j in range(TPB):
                            last = mm(bank[6 + b][:, j * P:(j + 1) * P], dpT[:, b, e - 2, j * P:(j + 1) * P], y1[:, (e - 2) % 2, b, :],
                                      start=(e == 2 and j == 0), stop=(e == E1 + 1), skip_group_check=True)
                        if b == B - 1 or e == E1 + 1:
                            last.then_inc(s.comb, 1)


def constants():
    r = np.arange(P)
    levels = np.zeros((P, LEVELS, P), np.float32)
    levels[r, 0, r] = 1.0
    for lv in range(1, LEVELS):
        seg = 1 << (lv - 1)
        key, query = r[:, None] // seg, r[None, :] // seg
        levels[:, lv, :] = (query == key + 1) & (key % 2 == 0)
    head = np.ones((P, GH), np.float32)
    head[0:3 * GH * HD] = (r[0:3 * GH * HD, None] % (GH * HD)) // HD == np.arange(GH)[None, :]
    rows = np.zeros((P, NCH, NHC), np.float32)
    for c in range(NCH):
        for k in range(NHC):
            rows[:, c, k] = (P * c + r) // KEYS == HLO[c] + k
    both = lambda n, base=0.0: np.broadcast_to(np.arange(n, dtype=np.float32) + np.float32(base), (P, n))
    half = np.zeros((P, HALF_N), np.float32)
    def put(name, a):
        at, n = HALF[name]
        half[:a.shape[0], at:at + n] = a
    put("ident", np.eye(P))
    put("below", r[:, None] < r[None, :])
    put("ones", np.ones((P, P)))
    put("future", np.where(r[None, :] < r[:, None], -1e30, 0.0))
    put("maskout", np.tile(-1e18 * np.eye(KEYS, PK), (1, H)))
    selection = np.zeros((P, sum(GROUP_COLS)), np.float32)
    for g, (f0, n) in enumerate(GROUPS):
        for f in range(n):
            selection[f0 + f, sum(GROUP_COLS[:g]) + np.array([2 * n + f, 3 * n + f])] = 1.0
    return selection, levels.reshape(P, -1), head, rows.reshape(P, -1), both, (half.view(np.uint32) >> 16).astype(np.uint16)


def kernel(**a):
    import concourse.bacc as bacc
    from concourse.bass_utils import run_bass_kernel_spmd

    a = {k: np.asarray(v) for k, v in a.items()}
    selection, levels, head, rows, both, half = constants()
    row = lambda v: np.broadcast_to(v.reshape(1, -1), (P, v.size))
    col = lambda v: v.reshape(P, 1)

    def pack(index, total, values):
        out = np.zeros((P, total), np.float32)
        for name, (at, n) in index.items():
            out[:, at:at + n] = values[name]
        return out

    early = pack(EARLY, EARLY_N, {
        "win": a["L0_attn_W_in"].T, "wg1": a["L0_attn_W_g1"].T, "wg2": a["L0_attn_W_g2"].T,
        "wout": a["L0_attn_W_out"].T, "lnw": col(a["L0_attn_ln_w"]), "ident": np.eye(P, dtype=np.float32)})
    ctxT = [np.tile(a["ctx_1024"][b].T, (1, 3)) for b in range(B)]
    work = pack(WORK, WORK_N, {
        "wv0": a["L0_xattn_Wv"], "wv1": a["L1_xattn_Wv"].T, "wk0": a["L0_xattn_Wk"], "wk1": a["L1_xattn_Wk"].T,
        "ctx0": ctxT[0], "ctx1": ctxT[1],
        "wq0": a["L0_xattn_Wq"], "wo0": a["L0_xattn_Wo"], "wq1": a["L1_xattn_Wq"].T, "wo1": a["L1_xattn_Wo"].T,
        "aq": a["L1_attn_Wq"], "ak": a["L1_attn_Wk"], "av": a["L1_attn_Wv"],
        "wr0": a["L0_ffn_Wr"], "wr1": a["L1_ffn_Wr"],
        "bq0": col(a["L0_xattn_bq"]), "bk0": col(a["L0_xattn_bk"]), "bv0": col(a["L0_xattn_bv"]),
        "bq1": col(a["L1_xattn_bq"]), "bk1": col(a["L1_xattn_bk"]), "bv1": col(a["L1_xattn_bv"]),
        "abq": col(a["L1_attn_bq"]), "abk": col(a["L1_attn_bk"]),
        "b1": a["L1_ffn_b1"].reshape(E1 * C1, P).T,
        "bo0": row(a["L0_xattn_bo"]), "bo1": row(a["L1_xattn_bo"]), "abv": row(a["L1_attn_bv"]),
        "br0": row(a["L0_ffn_br"]), "b2": row(a["L1_ffn_b2"]),
        "stackmask": head, "rowmask": rows, "slots": both(CAP, -BIG), "experts": both(E0)})
    chunks = lambda w, n: w.reshape(w.shape[0], n, P, D).transpose(2, 0, 1, 3).reshape(P, w.shape[0], n * D)
    ffn0 = np.stack([a["L0_ffn_W1"].transpose(1, 0, 2), a["L0_ffn_W3"].transpose(1, 0, 2), chunks(a["L0_ffn_W2"], C0)], 2)
    ffn1 = np.stack([a["L1_ffn_W1"].transpose(1, 0, 2), chunks(a["L1_ffn_W2"], C1)], 2)
    padmask = a["mask_BxSxS2_bk1"].transpose(2, 0, 1).reshape(KEYS, B * S).copy().view(np.uint32)
    key = a["mask_Bx1x1xS2_if1"].reshape(B, KEYS)
    keyrows = key[:, np.arange(NCH * P) % KEYS].reshape(B, NCH, P).transpose(2, 0, 1)

    arrays = {
        "x": a["x"], "early": early, "glamask": levels, "work": work, "half": half, "padmask": padmask,
        "keymask": key[:, np.arange(PK) % KEYS].reshape(1, B * PK), "keyrows": keyrows, "selection": selection, "ffn0": ffn0.reshape(P, -1), "ffn1": ffn1.reshape(P, -1)}
    arrays = {k: np.ascontiguousarray(v) for k, v in arrays.items()}
    nc = bacc.Bacc("TRN2", target_bir_lowering=False, num_devices=1)
    args = [nc.dram_tensor(f"in_{n}", v.shape, mybir.dt.from_np(v.dtype), kind="ExternalInput").ap() for n, v in arrays.items()]
    out = nc.dram_tensor("out", (B, S, D), F32, kind="ExternalOutput").ap()
    program(nc, *args, out)
    r = run_bass_kernel_spmd(nc, [{f"in_{n}": v for n, v in arrays.items()}], core_ids=[0])
    return r.results[0]["out"]
```
